# Optimizing a Trainium2 kernel written in Bass

```python
import numpy as np
import jax
import jax.numpy as jnp

def _softmax(x, axis=-1):
    return jax.nn.softmax(x, axis=axis)

def _gelu(x):
    return jax.nn.gelu(x, approximate=True)

def _silu(x):
    return jax.nn.silu(x)

def _sigmoid(x):
    return jax.nn.sigmoid(x)

def _layernorm(x, axis=-1, eps=1e-05):
    m = jnp.mean(x, axis=axis, keepdims=True)
    v = jnp.var(x, axis=axis, keepdims=True)
    return (x - m) / jnp.sqrt(v + eps)

def _scatter_add(tgt, idx, src, axis=0):
    return tgt.at[idx].add(src)

def _segment_sum(src, seg, n):
    return jax.ops.segment_sum(src, seg, n)
kernel_name = 'mk_decoder_postln_d1_seqx_r8_066f24'

def setup_inputs(seed: int=0):
    np.random.seed(seed)
    _w = jnp.asarray

    def _rec_inputs():
        import jax
        import jax.numpy as jnp
        _rk = jax.random.key(seed)
        x = 0.01048 + 0.1018 * jax.random.normal(jax.random.fold_in(_rk, 1), (4, 256, 256), jnp.float32)
        _lenS = 256 - jax.random.randint(jax.random.fold_in(_rk, 7), (4,), 0, max(1, 256 // 4) + 1, jnp.int32)
        _lenS2 = 256 - jax.random.randint(jax.random.fold_in(_rk, 8), (4,), 0, max(1, 256 // 4) + 1, jnp.int32)
        _ctx_512P = jax.random.normal(jax.random.fold_in(_rk, 11), (4, 16, 64), jnp.float32)
        _ctx_512c = jax.random.dirichlet(jax.random.fold_in(_rk, 511), 0.3 * jnp.ones((16,), jnp.float32), (4, 256))
        _ctx_512t = jnp.einsum('bsk,bkd->bsd', _ctx_512c, _ctx_512P)
        _ctx_512t = _ctx_512t * jax.lax.rsqrt(jnp.mean(jnp.square(_ctx_512t)) + 1e-12) * 0.953939
        ctx_512 = -0.000292821 + 1.00034 * (_ctx_512t + 0.3 * jax.random.normal(jax.random.fold_in(_rk, 611), (4, 256, 64), jnp.float32))
        return (x, ctx_512)
    x, ctx_512 = _rec_inputs()

    def _L0_attn_setup():
        import jax, jax.numpy as jnp
        import numpy as np
        EMBED_DIM = 256
        N_HEADS = 16
        HEAD_DIM = EMBED_DIM // N_HEADS
        B, T = (2, 256)

        def rope(x, pos):
            half = HEAD_DIM // 2
            freqs = 10000.0 ** (-jnp.arange(half, dtype=jnp.float32) / half)
            theta = pos[:, None].astype(jnp.float32) * freqs[None, :]
            sin = jnp.sin(theta)[None, None, :, :]
            cos = jnp.cos(theta)[None, None, :, :]
            x1 = x[..., 0::2]
            x2 = x[..., 1::2]
            return jnp.concatenate([x1 * cos - x2 * sin, x1 * sin + x2 * cos], axis=-1)
        key = jax.random.key(seed)
        k1, k2, k3, k4, k5 = jax.random.split(key, 5)
        bound_qkv = 1.0 / np.sqrt(EMBED_DIM)
        return {'x': jax.random.normal(k1, (B, T, EMBED_DIM), dtype=jnp.float32), 'w_qkv': jax.random.uniform(k2, (3 * EMBED_DIM, EMBED_DIM), minval=-bound_qkv, maxval=bound_qkv), 'b_qkv': jax.random.uniform(k3, (3 * EMBED_DIM,), minval=-bound_qkv, maxval=bound_qkv), 'w_out': jax.random.uniform(k4, (EMBED_DIM, EMBED_DIM), minval=-bound_qkv, maxval=bound_qkv), 'b_out': jax.random.uniform(k5, (EMBED_DIM,), minval=-bound_qkv, maxval=bound_qkv)}
    _L0_attn_all = _L0_attn_setup()
    _L0_attn_in = {k: v for k, v in _L0_attn_all.items() if k in ('w_qkv', 'b_qkv', 'w_out', 'b_out')}
    del _L0_attn_all

    def _L0_xattn_setup():
        import jax, jax.numpy as jnp
        import numpy as np
        LRELU_ALPHA = 0.2
        MASK_VAL = -10000000000.0
        B, N, F_IN = (4, 256, 64)
        H, F_OUT = (8, 32)
        F_HID = H * F_OUT

        def gat_layer(x, adj, W, a_self, a_neigh, b):
            feat = jnp.einsum('nf,hfo->hno', x, W)
            attn_self = jnp.einsum('hno,ho->hn', feat, a_self)
            attn_neigh = jnp.einsum('hno,ho->hn', feat, a_neigh)
            e = attn_self[:, :, None] + attn_neigh[:, None, :]
            e = jax.nn.leaky_relu(e, LRELU_ALPHA)
            e = e + MASK_VAL * (1.0 - adj)[None, :, :]
            alpha = jax.nn.softmax(e, axis=-1)
            out = jnp.einsum('hnm,hmo->hno', alpha, feat) + b[:, None, :]
            out = jnp.transpose(out, (1, 0, 2)).reshape(out.shape[1], -1)
            return jax.nn.elu(out)
        key = jax.random.key(seed)
        ks = jax.random.split(key, 10)
        feats = jax.random.normal(ks[0], (B, N, F_IN), dtype=jnp.float32)
        a = (jax.random.uniform(ks[1], (B, N, N)) < 0.01).astype(jnp.float32)
        adj = jnp.maximum(a, jnp.eye(N, dtype=jnp.float32)[None])
        s0 = 1.0 / np.sqrt(F_IN)
        s1 = 1.0 / np.sqrt(F_HID)
        return {'feats': feats, 'adj': adj, 'W0': jax.random.normal(ks[2], (H, F_IN, F_OUT), dtype=jnp.float32) * s0, 'a_self0': jax.random.normal(ks[3], (H, F_OUT), dtype=jnp.float32) * 0.1, 'a_neigh0': jax.random.normal(ks[4], (H, F_OUT), dtype=jnp.float32) * 0.1, 'b0': jnp.zeros((H, F_OUT), dtype=jnp.float32), 'W1': jax.random.normal(ks[5], (H, F_HID, F_OUT), dtype=jnp.float32) * s1, 'a_self1': jax.random.normal(ks[6], (H, F_OUT), dtype=jnp.float32) * 0.1, 'a_neigh1': jax.random.normal(ks[7], (H, F_OUT), dtype=jnp.float32) * 0.1, 'b1': jnp.zeros((H, F_OUT), dtype=jnp.float32)}
    _L0_xattn_all = _L0_xattn_setup()
    _L0_xattn_in = {k: v for k, v in _L0_xattn_all.items() if k in ('W0', 'a_self0', 'a_neigh0', 'b0', 'W1', 'a_self1', 'a_neigh1', 'b1')}
    del _L0_xattn_all

    def _L0_ffn_setup():
        import jax, jax.numpy as jnp
        import numpy as np
        H = 256
        E = 16
        K = 4
        F_E = 176
        F_S = 704
        B, S = (2, 256)
        key = jax.random.key(seed)
        ks = jax.random.split(key, 9)
        sc = 0.02
        return {'hidden_states': jax.random.normal(ks[0], (B, S, H), dtype=jnp.float32), 'gate_w': jax.random.normal(ks[1], (E, H), dtype=jnp.float32) * sc, 'expert_gate_w': jax.random.normal(ks[2], (E, F_E, H), dtype=jnp.float32) * sc, 'expert_up_w': jax.random.normal(ks[3], (E, F_E, H), dtype=jnp.float32) * sc, 'expert_down_w': jax.random.normal(ks[4], (E, H, F_E), dtype=jnp.float32) * sc, 'shared_gate_w': jax.random.normal(ks[5], (F_S, H), dtype=jnp.float32) * sc, 'shared_up_w': jax.random.normal(ks[6], (F_S, H), dtype=jnp.float32) * sc, 'shared_down_w': jax.random.normal(ks[7], (H, F_S), dtype=jnp.float32) * sc, 'shared_expert_gate_w': jax.random.normal(ks[8], (1, H), dtype=jnp.float32) * sc}
    _L0_ffn_all = _L0_ffn_setup()
    _L0_ffn_in = {k: v for k, v in _L0_ffn_all.items() if k in ('gate_w', 'expert_gate_w', 'expert_up_w', 'expert_down_w', 'shared_gate_w', 'shared_up_w', 'shared_down_w', 'shared_expert_gate_w')}
    del _L0_ffn_all
    return {'x': x, 'ctx_512': ctx_512, 'L0_attn_w_qkv': _L0_attn_in['w_qkv'], 'L0_attn_b_qkv': _L0_attn_in['b_qkv'], 'L0_attn_w_out': _L0_attn_in['w_out'], 'L0_attn_b_out': _L0_attn_in['b_out'], 'L0_xattn_W0': _L0_xattn_in['W0'], 'L0_xattn_a_self0': _L0_xattn_in['a_self0'], 'L0_xattn_a_neigh0': _L0_xattn_in['a_neigh0'], 'L0_xattn_b0': _L0_xattn_in['b0'], 'L0_xattn_W1': _L0_xattn_in['W1'], 'L0_xattn_a_self1': _L0_xattn_in['a_self1'], 'L0_xattn_a_neigh1': _L0_xattn_in['a_neigh1'], 'L0_xattn_b1': _L0_xattn_in['b1'], 'L0_ffn_gate_w': _L0_ffn_in['gate_w'], 'L0_ffn_expert_gate_w': _L0_ffn_in['expert_gate_w'], 'L0_ffn_expert_up_w': _L0_ffn_in['expert_up_w'], 'L0_ffn_expert_down_w': _L0_ffn_in['expert_down_w'], 'L0_ffn_shared_gate_w': _L0_ffn_in['shared_gate_w'], 'L0_ffn_shared_up_w': _L0_ffn_in['shared_up_w'], 'L0_ffn_shared_down_w': _L0_ffn_in['shared_down_w'], 'L0_ffn_shared_expert_gate_w': _L0_ffn_in['shared_expert_gate_w']}

def reference(x, ctx_512, L0_attn_w_qkv, L0_attn_b_qkv, L0_attn_w_out, L0_attn_b_out, L0_xattn_W0, L0_xattn_a_self0, L0_xattn_a_neigh0, L0_xattn_b0, L0_xattn_W1, L0_xattn_a_self1, L0_xattn_a_neigh1, L0_xattn_b1, L0_ffn_gate_w, L0_ffn_expert_gate_w, L0_ffn_expert_up_w, L0_ffn_expert_down_w, L0_ffn_shared_gate_w, L0_ffn_shared_up_w, L0_ffn_shared_down_w, L0_ffn_shared_expert_gate_w):
    import jax
    import jax.numpy as jnp

    def _L0_attn_ref(x, w_qkv, b_qkv, w_out, b_out):
        import jax, jax.numpy as jnp
        import numpy as np
        EMBED_DIM = 256
        N_HEADS = 16
        HEAD_DIM = EMBED_DIM // N_HEADS
        B, T = (2, 256)

        def rope(x, pos):
            half = HEAD_DIM // 2
            freqs = 10000.0 ** (-jnp.arange(half, dtype=jnp.float32) / half)
            theta = pos[:, None].astype(jnp.float32) * freqs[None, :]
            sin = jnp.sin(theta)[None, None, :, :]
            cos = jnp.cos(theta)[None, None, :, :]
            x1 = x[..., 0::2]
            x2 = x[..., 1::2]
            return jnp.concatenate([x1 * cos - x2 * sin, x1 * sin + x2 * cos], axis=-1)
        Bn, Tn, D = x.shape
        qkv = x @ w_qkv.T + b_qkv
        q, k, v = jnp.split(qkv, 3, axis=-1)

        def reshape(t):
            return t.reshape(Bn, Tn, N_HEADS, HEAD_DIM).transpose(0, 2, 1, 3)
        q, k, v = map(reshape, (q, k, v))
        pos = jnp.arange(Tn)
        q = rope(q, pos)
        k = rope(k, pos)
        scale = HEAD_DIM ** (-0.5)
        attn = jnp.einsum('bhqd,bhkd->bhqk', q, k) * scale
        causal = jnp.triu(jnp.ones((Tn, Tn), dtype=bool), k=1)
        attn = jnp.where(causal[None, None], -jnp.inf, attn)
        attn = jax.nn.softmax(attn, axis=-1)
        out = jnp.einsum('bhqk,bhkd->bhqd', attn, v)
        out = out.transpose(0, 2, 1, 3).reshape(Bn, Tn, D)
        return out @ w_out.T + b_out

    def _L0_xattn_ref(feats, adj, W0, a_self0, a_neigh0, b0, W1, a_self1, a_neigh1, b1):
        import jax, jax.numpy as jnp
        import numpy as np
        LRELU_ALPHA = 0.2
        MASK_VAL = -10000000000.0
        B, N, F_IN = (4, 256, 64)
        H, F_OUT = (8, 32)
        F_HID = H * F_OUT

        def gat_layer(x, adj, W, a_self, a_neigh, b):
            feat = jnp.einsum('nf,hfo->hno', x, W)
            attn_self = jnp.einsum('hno,ho->hn', feat, a_self)
            attn_neigh = jnp.einsum('hno,ho->hn', feat, a_neigh)
            e = attn_self[:, :, None] + attn_neigh[:, None, :]
            e = jax.nn.leaky_relu(e, LRELU_ALPHA)
            e = e + MASK_VAL * (1.0 - adj)[None, :, :]
            alpha = jax.nn.softmax(e, axis=-1)
            out = jnp.einsum('hnm,hmo->hno', alpha, feat) + b[:, None, :]
            out = jnp.transpose(out, (1, 0, 2)).reshape(out.shape[1], -1)
            return jax.nn.elu(out)

        def per_graph(x, a):
            h = gat_layer(x, a, W0, a_self0, a_neigh0, b0)
            return gat_layer(h, a, W1, a_self1, a_neigh1, b1)
        return jax.vmap(per_graph)(feats, adj)

    def _L0_ffn_ref(hidden_states, gate_w, expert_gate_w, expert_up_w, expert_down_w, shared_gate_w, shared_up_w, shared_down_w, shared_expert_gate_w):
        import jax, jax.numpy as jnp
        import numpy as np
        H = 256
        E = 16
        K = 4
        F_E = 176
        F_S = 704
        B, S = (2, 256)
        b, s, h = hidden_states.shape
        x = hidden_states.reshape(-1, h)
        T = x.shape[0]
        router_logits = x @ gate_w.T
        routing = jax.nn.softmax(router_logits.astype(jnp.float32), axis=-1)
        rw, sel = jax.lax.top_k(routing, K)
        rw = rw / jnp.sum(rw, axis=-1, keepdims=True)
        rw = rw.astype(x.dtype)
        tok = jnp.arange(T)[:, None]
        comb = jnp.zeros((T, E), dtype=x.dtype).at[tok, sel].add(rw)

        def expert_step(acc, wts):
            gw, uw, dw, w = wts
            hdn = jax.nn.silu(x @ gw.T) * (x @ uw.T)
            return (acc + hdn @ dw.T * w[:, None], None)
        out, _ = jax.lax.scan(expert_step, jnp.zeros_like(x), (expert_gate_w, expert_up_w, expert_down_w, comb.T))
        shared = jax.nn.silu(x @ shared_gate_w.T) * (x @ shared_up_w.T) @ shared_down_w.T
        shared = jax.nn.sigmoid(x @ shared_expert_gate_w.T) * shared
        return (out + shared).reshape(b, s, h)
    x = _layernorm(x + _L0_attn_ref(x, L0_attn_w_qkv, L0_attn_b_qkv, L0_attn_w_out, L0_attn_b_out), axis=-1)
    x = _layernorm(x + _L0_xattn_ref(ctx_512, x, L0_xattn_W0, L0_xattn_a_self0, L0_xattn_a_neigh0, L0_xattn_b0, L0_xattn_W1, L0_xattn_a_self1, L0_xattn_a_neigh1, L0_xattn_b1), axis=-1)
    x = _layernorm(x + _L0_ffn_ref(x, L0_ffn_gate_w, L0_ffn_expert_gate_w, L0_ffn_expert_up_w, L0_ffn_expert_down_w, L0_ffn_shared_gate_w, L0_ffn_shared_up_w, L0_ffn_shared_down_w, L0_ffn_shared_expert_gate_w), axis=-1)
    return x

_drawn_inputs = setup_inputs


def setup_inputs(seed=0):
    import zlib

    import numpy as np

    out = dict(_drawn_inputs(seed))
    spreads = {'L0_xattn_b0': (0.0, 0.1), 'L0_xattn_b1': (0.0, 0.1)}
    factors = {'L0_ffn_gate_w': 8.0,
     'L0_ffn_expert_gate_w': 8.0,
     'L0_ffn_expert_up_w': 7.857,
     'L0_ffn_expert_down_w': 7.902,
     'L0_ffn_shared_gate_w': 3.858,
     'L0_ffn_shared_up_w': 3.867,
     'L0_ffn_shared_down_w': 3.877,
     'L0_ffn_shared_expert_gate_w': 8.0}
    for name, (base, spread) in spreads.items():
        noise = np.random.default_rng([zlib.crc32(name.encode()), seed]).standard_normal(out[name].shape)
        drawn = base * np.exp(spread * noise) if base else spread * noise
        out[name] = jnp.asarray(drawn.astype(out[name].dtype))
    for name, factor in factors.items():
        out[name] = (out[name] * factor).astype(out[name].dtype)
    return out
```

```python
import concourse.bass as bass
from concourse import mybir
from contextlib import ExitStack

B, T, D = 4, 256, 256
P = 128
NT = T // P
KD = D // P
NH, DH = 16, 16
SLOT = 64
CF, GH, GO = 64, 8, 32
GA = GO + 1
NE, FE, FS, TOPK = 16, 176, 704, 4
NG = NE + 1
NGP = NG + 1
NF = -(-(NE * FE + FS) // P)
NTT = B * NT
CHUNK = 512
NCH = B * T // CHUNK
EPS = 1e-5
NEG = -1e30
MASK_SCALE = 1e10
CAUSAL = P + T


class Steps:

    def __init__(self, eng, sem, base=0):
        self.eng, self.sem, self.base, self.n = eng, sem, base, 0

    def mark(self, ins):
        ins.then_inc(self.sem, 1)
        self.n += 1

    def wait(self):
        self.eng.wait_ge(self.sem, self.base + self.n)

    def link(self, ins):
        self.mark(ins)
        self.wait()


DVE_STEPS = 36


def decoder_layer(nc, xT, x, ctxT, wqkvT, bqkv, woT, bo, W0f, W0r, A0, b0, W1f, W1r, A1, b1,
                  gwT, ffnW, rope_cs, causal_q, causal_k, ident, head_sel, node_onehot, gate_sel,
                  scan_reset, out):
    f32, bf16, f32r = mybir.dt.float32, mybir.dt.bfloat16, mybir.dt.float32r
    ALU = mybir.AluOpType
    ACT = mybir.ActivationFunctionType
    AX = mybir.AxisListType

    ctx = ExitStack()
    with ctx:
        def sb(name, shape, dt=f32):
            return ctx.enter_context(nc.sbuf_tensor(name, shape, dt))

        def sem(name):
            return ctx.enter_context(nc.semaphore(name))

        PS = ctx.enter_context(nc.psum_tensor("PS", [P, 8, 512], f32))

        xT_sb = sb("xT_sb", [P, KD, T])
        xres = sb("xres", [P, NT, D])
        ctx_sb = sb("ctx_sb", [CF, T])
        ctx_hi = sb("ctx_hi", [CF, T], f32r)
        ctx_lo = sb("ctx_lo", [CF, T], f32r)
        wqkv_sb = sb("wqkv_sb", [P, KD, 3 * D])
        bqkv_sb = sb("bqkv_sb", [P, 3 * D])
        wo_sb = sb("wo_sb", [P, KD, D])
        bo_sb = sb("bo_sb", [P, D])
        rope_sb = sb("rope_sb", [P, NT, 2, DH])
        identf = sb("identf", [P, P])
        identb = sb("identb", [P, P], bf16)
        maskq = sb("maskq", [P, CAUSAL], bf16)
        maskk = sb("maskk", [P, CAUSAL], bf16)
        selh = sb("selh", [2 * NH, NH, P], f32r)
        onehot = sb("onehot", [2 * GH, GH, T], f32r)

        qk = sb("qk", [P, NT, 2 * D])
        t1 = sb("t1", [P, NT, 2 * D])
        t2 = sb("t2", [P, NT, 2 * D])
        q3 = sb("q3", [P, NT, NH * SLOT], f32r)
        k3 = sb("k3", [P, NT, NH * SLOT], f32r)
        q3T = sb("q3T", [P, NH // 2, T], f32r)
        k3T = sb("k3T", [P, NH // 2, T], f32r)
        vaug = sb("vaug", [P, NT, NH, DH + 1])
        negm = sb("negm", [P, NT, NH])
        negm2 = sb("negm2", [P, NT, 2 * NH], f32r)
        negmT = sb("negmT", [2 * NH, CAUSAL], f32r)
        pT = sb("pT", [P, 3, 2, CAUSAL])
        orec = sb("orec", [P, NT, NH])
        o_sb = sb("o_sb", [P, NT, D])
        oT = sb("oT", [P, KD, T])
        xb = sb("xb", [P, NT, D])

        resid = sb("resid", [P, NT, D])
        stats = sb("stats", [P, NT, 6])
        meanvar = sb("meanvar", [P, NT, 2])
        vareps = sb("vareps", [P, NT])
        rstd = sb("rstd", [P, NT])
        mhalf = sb("mhalf", [P, NTT])

        idle_v, idle_p = sb("idle_v", [P, 1]), sb("idle_p", [P, 1])

        w0r_sb = sb("w0r_sb", [P, KD, CF])
        a0_sb = sb("a0_sb", [P, KD, 2 * GH])
        a1_sb = sb("a1_sb", [P, KD, 2 * GH])
        WC = D + 2 * GH
        w0c = sb("w0c", [CF, WC])
        w0h = sb("w0h", [CF, WC], f32r)
        w0l = sb("w0l", [CF, WC], f32r)
        w1c = sb("w1c", [P, KD, WC])
        w1h = sb("w1h", [P, KD, WC], f32r)
        w1l = sb("w1l", [P, KD, WC], f32r)
        b01 = sb("b01", [P, 2, D])
        x1 = sb("x1", [P, NT, D])
        mk = sb("mk", [P, NT, T])
        feat = sb("feat", [P, NT, GH, GA])
        st2 = sb("st2", [P, NT, 2, 2 * GH], f32r)
        stT = sb("stT", [2 * GH, 2, T], f32r)
        al = sb("al", [P, 3, 4, T])
        gmax = sb("gmax", [P, 4 * 4])
        ngmax = sb("ngmax", [P, 4 * 4])
        grec = sb("grec", [P, NT, GH])
        gneg = sb("gneg", [P, NT, D])
        gpos = sb("gpos", [P, NT, D])
        gh = sb("gh", [P, NT, D])
        ghT_hi = sb("ghT_hi", [P, KD, T], f32r)
        ghT_lo = sb("ghT_lo", [P, KD, T], f32r)

        x2b = sb("x2b", [P, NT, D])
        x2 = sb("x2", [P, NTT, D])
        x2T_hi = sb("x2T_hi", [P, KD, B * T], f32r)
        x2T_lo = sb("x2T_lo", [P, KD, B * T], f32r)
        gw_sb = sb("gw_sb", [P, KD, NGP])
        gw_hi = sb("gw_hi", [P, KD, NGP], f32r)
        gw_lo = sb("gw_lo", [P, KD, NGP], f32r)
        reset_sb = sb("reset_sb", [P, NTT * NE])
        comb = sb("comb", [P, NTT, NG])
        r_a = sb("r_a", [P, NTT, NE])
        r_b = sb("r_b", [P, NTT, NE])
        r_c = sb("r_c", [P, NTT, NE])
        r_s = sb("r_s", [P, NTT])
        r_t = sb("r_t", [P, NTT])
        top8 = sb("top8", [P, NTT, 8])
        combp = sb("combp", [P, NTT, SLOT], bf16)
        combT = sb("combT", [3 * NG, B * T], bf16)
        WJ = 4 * P + D
        wraw = sb("wraw", [P, 2, WJ])
        whi = sb("whi", [P, 2, WJ], f32r)
        wlo = sb("wlo", [P, 2, WJ], f32r)
        gsel = sb("gsel", [3 * NG, 2, P], bf16)
        hid_hi = sb("hid_hi", [P, 2, CHUNK], f32r)
        hid_lo = sb("hid_lo", [P, 2, CHUNK], f32r)
        stats3 = sb("stats3", [P, NTT, 6])
        mv3 = sb("mv3", [P, NTT, 2])
        ve3 = sb("ve3", [P, NTT])
        rstd3 = sb("rstd3", [P, NTT])
        stage_h = al[0:2 * NH, :, :, :].rearrange("p a b c -> p (a b c)")[:, 0:NH * P].rearrange(
            "p (h c) -> p h c", c=P)
        stage_n = x2[0:2 * GH, :, :].rearrange("p a c -> p (a c)").rearrange("p (h c) -> p h c", c=T)
        w1r_sb = gneg
        gy = o_sb
        rot = al[:, 0:2, :, :].rearrange("p a b c -> p (a b c)")[:, 0:NT * 2 * D].rearrange(
            "p (t h d) -> p t h d", t=NT, d=DH)
        aT = pT[:, :, :, :].rearrange("p a b c -> p (a b c)")[:, 0:16 * P].rearrange("p (q a c) -> p q a c", q=4, c=P)
        sg, hu, hid = t1, t2, qk
        res3 = q3[:, :, :].bitcast(f32).rearrange("p a (b d) -> p (a b) d", d=D)
        y3 = k3[:, :, :].bitcast(f32).rearrange("p a (b d) -> p (a b) d", d=D)

        names = """consts_loaded att_w_loaded gat_w_loaded router_w_loaded xT_loaded xres_loaded ctx_loaded
            setup_zero gat_fold_ps gat_w_ready sel_ready ctx_split
            qkv_ready qk_biased v_ready t2_ready rot_ready q3_ready k3_hi k3_ready qkT_ps qkT_ready
            s_ready smax_done negm_ready negmT_ps negmT_ready st_ready exp_done pv_done on_ready oT_ps
            oT_ready xb_ready y_ready y_used var_ready rstd_ready
            feat_ps st2_ready feat_ready stT_ps stT_ready z_ready y_copied lr_done v_masked
            alpha_ready aT_ps aTA_done aTD_done gpv_done gneg_ready gexp_ready gh_ready ghT_ps ghT_ready
            x2_stored x2T_ready dve_step pool_step
            logit_ps gate_centered gate_exp comb_ready combT_ps combT_ready
            w_loaded0 w_loaded1 w_split g_ready u_ready c_ready silu_done u_used c_used hid_rounded hid_ready
            down_done acc_ready var3_ready rstd3_ready out_ready out_stored setup_step""".split()
        S = {n: sem(n) for n in names}

        block = ctx.enter_context(nc.Block())

        @block.sync
        def _(sp):
            for dst, src in ((rope_sb[:], rope_cs), (identf[:], ident), (maskq[:], causal_q), (maskk[:], causal_k),
                             (stage_h, head_sel), (stage_n, node_onehot), (reset_sb[:], scan_reset)):
                sp.dma_start(dst, src).then_inc(S["consts_loaded"], 16)
            for dst, src in ((w1r_sb[:], W1r), (a1_sb[:], A1), (w1c[:, :, 0:D], W1f)):
                sp.dma_start(dst, src).then_inc(S["gat_w_loaded"], 16)
            def load_batch(i, first=False):
                if not first:
                    sp.wait_ge(S["qkv_ready"], NT * i)
                sp.dma_start(xT_sb[:], xT[i]).then_inc(S["xT_loaded"], 16)
                if not first:
                    sp.wait_ge(S["ctx_split"], 2 * i)
                sp.dma_start(ctx_sb[:], ctxT[i]).then_inc(S["ctx_loaded"], 16)
                if not first:
                    sp.wait_ge(S["xb_ready"], i)
                sp.dma_start(xres[:], x[i]).then_inc(S["xres_loaded"], 16)

            load_batch(0, first=True)
            with sp.Fori(1, B) as i:
                load_batch(i)

            def load_hidden(j, slot):
                sp.dma_start(wraw[:, slot, :], ffnW[j]).then_inc(S[f"w_loaded{slot}"], 16)
                sp.dma_start(gsel[:, slot, :], gate_sel[j]).then_inc(S[f"w_loaded{slot}"], 16)

            load_hidden(0, 0)
            load_hidden(1, 1)
            with sp.Fori(1, NF // 2) as m:
                for slot in range(2):
                    sp.wait_ge(S["c_ready"], (2 * m + slot - 1) * NCH)
                    load_hidden(2 * m + slot, slot)
            for t in range(NTT):
                sp.wait_ge(S["out_ready"], t + 1)
                sp.dma_start(out[t], y3[:, t, :]).then_inc(S["out_stored"], 16)
            sp.wait_ge(S["out_stored"], 16 * NTT)

        @block.gpsimd
        def _(pool):
            pool.memset(mhalf[:], -0.5).then_inc(S["setup_zero"], 1)
            pool.memset(q3[:].bitcast(f32), 0.0).then_inc(S["setup_zero"], 1)
            pool.memset(k3[:].bitcast(f32), 0.0).then_inc(S["setup_zero"], 1)
            pool.memset(vaug[:, :, :, DH:DH + 1], 1.0).then_inc(S["setup_zero"], 1)
            pool.memset(feat[:, :, :, GO:GA], 1.0).then_inc(S["setup_zero"], 1)
            pool.memset(combp[:], 0.0).then_inc(S["setup_zero"], 1)
            pool.wait_ge(S["consts_loaded"], 16 * 7)
            pool.tensor_copy(identb[:], identf[:]).then_inc(S["sel_ready"], 1)
            pool.tensor_copy(selh[:], stage_h).then_inc(S["sel_ready"], 1)
            pool.tensor_copy(onehot[:], stage_n).then_inc(S["sel_ready"], 1)
            pool.wait_ge(S["setup_zero"], 6)

            with pool.Fori(0, B) as i:
                for t in range(NT):
                    pool.wait_ge(S["qk_biased"], NT * i + t + 1)
                    sines = rope_sb[:, t, 1, :].unsqueeze(1).broadcast_to([P, 2 * NH, DH])
                    pool.tensor_tensor(t2[:, t, :].rearrange("p (h d) -> p h d", d=DH),
                                       qk[:, t, :].rearrange("p (h d) -> p h d", d=DH),
                                       sines, ALU.mult).then_inc(S["t2_ready"], 1)
                    pool.wait_ge(S["rot_ready"], NT * i + t + 1)
                    kv = k3[:, t, :].rearrange("p (h s) -> p h s", s=SLOT)
                    src = rot[:, t, NH:2 * NH, :]
                    pool.tensor_tensor(idle_p[:], mhalf[:, 0:1], mhalf[:, 0:1], ALU.mult)
                    pool.tensor_copy(kv[:, :, 0:DH], src).then_inc(S["k3_hi"], 1)
                    pool.tensor_copy(kv[:, :, DH:2 * DH], src)
                    pool.wait_ge(S["k3_hi"], NT * i + t + 1)
                    pool.tensor_tensor(kv[:, :, 2 * DH:3 * DH], src, kv[:, :, 0:DH].bitcast(f32),
                                       ALU.subtract).then_inc(S["k3_ready"], 1)
                pool.wait_ge(S["xres_loaded"], 16 * (i + 1))
                pool.tensor_tensor(xb[:], xres[:], bo_sb[:].unsqueeze(1).broadcast_to([P, NT, D]),
                                   ALU.add).then_inc(S["xb_ready"], 1)
                pool.wait_ge(S["ctx_loaded"], 16 * (i + 1))
                pool.tensor_tensor(idle_p[:], mhalf[:, 0:1], mhalf[:, 0:1], ALU.mult)
                pool.tensor_copy(ctx_hi[:], ctx_sb[:]).then_inc(S["ctx_split"], 1)
                pool.wait_ge(S["ctx_split"], 2 * i + 1)
                pool.tensor_tensor(ctx_lo[:], ctx_sb[:], ctx_hi[:].bitcast(f32),
                                   ALU.subtract).then_inc(S["ctx_split"], 1)
                for n in range(2):
                    pool.wait_ge(S["var_ready"], 2 * i + n + 1)
                    pool.tensor_tensor(rstd[:], vareps[:], mhalf[:, 0:NT], ALU.pow).then_inc(S["rstd_ready"], 1)
                pool.wait_ge(S["gh_ready"], 2 * (i + 1))
                pool.tensor_tensor(idle_p[:], mhalf[:, 0:1], mhalf[:, 0:1], ALU.mult)
                pool.tensor_copy(x2[:, bass.ts(i, NT), :], x2b[:]).then_inc(S["x2_stored"], 1)

            pool.wait_ge(S["x2_stored"], B)

            def split_weights(j, slot, second):
                pool.wait_ge(S[f"w_loaded{slot}"], 32 * second)
                pool.tensor_tensor(idle_p[:], mhalf[:, 0:1], mhalf[:, 0:1], ALU.mult)
                pool.tensor_copy(whi[:, slot, :], wraw[:, slot, :]).then_inc(S["pool_step"], 1)
                pool.wait_ge(S["pool_step"], j + 1)
                pool.tensor_tensor(wlo[:, slot, :], wraw[:, slot, :], whi[:, slot, :].bitcast(f32),
                                   ALU.subtract).then_inc(S["w_split"], 1)

            split_weights(0, 0, 1)
            split_weights(1, 1, 1)
            with pool.Fori(1, NF // 2) as m:
                for slot in range(2):
                    j = 2 * m + slot
                    pool.wait_ge(S["down_done"], NCH * (j - 1))
                    split_weights(j, slot, m + 1)
            pool.wait_ge(S["var3_ready"], 1)
            pool.tensor_tensor(rstd3[:], ve3[:], mhalf[:], ALU.pow).then_inc(S["rstd3_ready"], 1)

        @block.scalar
        def _(act):
            for dst, src in ((wqkv_sb[:], wqkvT), (bqkv_sb[:], bqkv.partition_broadcast(P))):
                act.dma_start(dst, src).then_inc(S["att_w_loaded"], 16)
            for dst, src in ((wo_sb[:], woT), (bo_sb[:], bo.partition_broadcast(P))):
                act.dma_start(dst, src).then_inc(S["att_w_loaded"], 16)
            for dst, src in ((w0r_sb[:], W0r), (a0_sb[:], A0), (w0c[:, 0:D], W0f),
                             (b01[:, 0, :], b0.partition_broadcast(P)), (b01[:, 1, :], b1.partition_broadcast(P))):
                act.dma_start(dst, src).then_inc(S["gat_w_loaded"], 16)
            act.dma_start(gw_sb[:], gwT).then_inc(S["router_w_loaded"], 16)

            with act.Fori(0, B) as i:
                for n in range(4 * NT):
                    t, half, which = n // 4, n % 2, (n % 4) // 2
                    bank = (3 + n) % 8
                    act.wait_ge(S["qkT_ps"], 4 * NT * i + n + 1)
                    dst = (q3T, k3T)[which]
                    act.activation(dst[:, 4 * half:4 * half + 4, t * P:(t + 1) * P],
                                   PS[:, bank, :].rearrange("p (a c) -> p a c", c=P),
                                   ACT.Copy).then_inc(S["qkT_ready"], 1)
                for u in range(NH // 2):
                    act.wait_ge(S["st_ready"], 8 * i + u + 1)
                    if u >= 3:
                        act.wait_ge(S["pv_done"], 8 * i + u - 2)
                    b = 2 * (u % 3)
                    act.activation(pT[:, u % 3, :, :], PS[:, b:b + 2, 0:CAUSAL], ACT.Exp,
                                   scale=DH ** -0.5).then_inc(S["exp_done"], 1)
                for layer in range(2):
                    if layer == 1:
                        pass
                    def features(layer):
                        act.wait_ge(S["st2_ready"], 2 * i + layer + 1)
                        act.activation(feat[:, :, :, 0:GO],
                                       PS[:, 2:4, 0:D].rearrange("p t (h o) -> p t h o", o=GO),
                                       ACT.Copy).then_inc(S["feat_ready"], 1)
                    features(layer)
                    if layer == 0:
                        act.wait_ge(S["oT_ps"], i + 1)
                        act.activation(oT[:], PS[:, 0, :].rearrange("p (k t) -> p k t", k=KD),
                                       ACT.Copy).then_inc(S["oT_ready"], 1)

                    def leak(c):
                        act.wait_ge(S["z_ready"], 8 * i + 4 * layer + c + 1)
                        if 4 * layer + c >= 3:
                            act.wait_ge(S["aT_ps"], 16 * i + 2 * (4 * layer + c - 2))
                        b = 2 * (c % 2)
                        act.activation(al[:, (4 * layer + c) % 3, :, :],
                                       PS[:, b:b + 2, :].rearrange("p b (h m) -> p (b h) m", m=T),
                                       ACT.Copy, scale=0.2).then_inc(S["y_copied"], 1)

                    def exps(c):
                        act.wait_ge(S["v_masked"], 8 * i + 4 * layer + c + 1)
                        for h in range(4):
                            a = al[:, (4 * layer + c) % 3, h, :]
                            ins = act.activation(a, a, ACT.Exp, bias=ngmax[:, 4 * c + h:4 * c + h + 1])
                            if h % 2:
                                ins.then_inc(S["alpha_ready"], 1)

                    def evacuate(q):
                        n = 8 * layer + q
                        act.wait_ge(S["aT_ps"], 16 * i + n + 1)
                        if n >= 4:
                            act.wait_ge(S["gpv_done"], 16 * i + n - 3)
                        act.activation(aT[:, q % 4, :, :], PS[:, 4 + q % 2, :].rearrange("p (a c) -> p a c", c=P),
                                       ACT.Copy).then_inc(S["aTA_done"], 1)

                    leak(0)
                    leak(1)
                    for c in range(4):
                        exps(c)
                        if c + 2 < 4:
                            leak(c + 2)
                        evacuate(2 * c)
                    act.wait_ge(S["gneg_ready"], 2 * i + layer + 1)
                    act.activation(gneg[:], gneg[:], ACT.Exp).then_inc(S["gexp_ready"], 1)

            act.wait_ge(S["gate_centered"], 1)
            act.activation(r_b[:], r_a[:], ACT.Exp).then_inc(S["gate_exp"], 1)
            act.activation(r_t[:], PS[:, 7, 0:NTT * NGP].rearrange("p (t g) -> p t g", g=NGP)[:, :, NE],
                           ACT.Exp, scale=-1.0).then_inc(S["gate_exp"], 1)

            def silu(n, c):
                act.wait_ge(S["g_ready"], n + 1)
                if not isinstance(n, int) or n >= 2:
                    act.wait_ge(S["u_used"], n - 1)
                act.activation(sg[:, c, :], PS[:, 4, :], ACT.Silu).then_inc(S["silu_done"], 1)

            def round_hidden(n, c):
                act.wait_ge(S["c_used"], n + 1)
                if not isinstance(n, int) or n >= 2:
                    act.wait_ge(S["down_done"], n - 1)
                act.activation(hid_hi[:, c, :], hid[:, c, :], ACT.Copy).then_inc(S["hid_rounded"], 1)

            for c in range(NCH):
                silu(c, c)
                round_hidden(c, c)
            with act.Fori(1, NF) as j:
                for c in range(NCH):
                    silu(NCH * j + c, c)
                    round_hidden(NCH * j + c, c)

        @block.tensor
        def _(pe):
            pe.wait_ge(S["gat_w_loaded"], 16 * 8)
            for k in range(KD):
                pe.matmul(PS[0:CF, 0, 0:2 * GH], w0r_sb[:, k, :], a0_sb[:, k, :], start=(k == 0), stop=(k == KD - 1))
            for f in range(KD):
                for k in range(KD):
                    mm = pe.matmul(PS[:, 1 + f, 0:2 * GH], w1r_sb[:, k, f * P:(f + 1) * P], a1_sb[:, k, :],
                                   start=(k == 0), stop=(k == KD - 1))
            mm.then_inc(S["gat_fold_ps"], 1)
            pe.wait_ge(S["sel_ready"], 3)
            pe.wait_ge(S["gat_w_ready"], 1)
            pe.wait_ge(S["att_w_loaded"], 64)

            with pe.Fori(0, B) as i:
                pe.wait_ge(S["xT_loaded"], 16 * (i + 1))
                for t in range(NT):
                    for k in range(KD):
                        pe.matmul(PS[:, t, :], xT_sb[:, k, t * P:(t + 1) * P], wqkv_sb[:, k, 0:2 * D],
                                  start=(k == 0), stop=(k == KD - 1))
                    for k in range(KD):
                        mm = pe.matmul(PS[:, 2 + t, 0:D], xT_sb[:, k, t * P:(t + 1) * P],
                                       wqkv_sb[:, k, 2 * D:3 * D], start=(k == 0), stop=(k == KD - 1))
                    mm.then_inc(S["qkv_ready"], 1)
                for t in range(NT):
                    for which, ready, src in ((0, "q3_ready", q3), (1, "k3_ready", k3)):
                        pe.wait_ge(S[ready], NT * i + t + 1)
                        for half in range(2):
                            n = 4 * t + 2 * which + half
                            if n >= 8 - 3:
                                pe.wait_ge(S["v_ready"], NT * (i + 1))
                            for a in range(4):
                                c0 = (4 * half + a) * P
                                mm = pe.transpose(PS[:, (3 + n) % 8, a * P:(a + 1) * P],
                                                  src[:, t, c0:c0 + P].bitcast(f32), identf[:])
                            mm.then_inc(S["qkT_ps"], 1)
                pe.wait_ge(S["qkT_ready"], 8 * (i + 1))
                for g in range(4):
                    if g >= 2:
                        pe.wait_ge(S["smax_done"], 4 * i + g - 1)
                    for r in range(4):
                        bank = 4 * (g % 2) + r
                        pe.matmul(PS[:, bank, 0:CAUSAL], identb[:], maskq[:], start=True, stop=False,
                                  skip_group_check=True)
                    for r in range(4):
                        bank, h = 4 * (g % 2) + r, 4 * g + r
                        rows = slice(SLOT * (h % 2), SLOT * (h % 2) + 3 * DH)
                        pe.matmul(PS[:, bank, 0:P], q3T[rows, h // 2, 0:P], k3T[rows, h // 2, 0:P],
                                  start=False, stop=False, skip_group_check=True)
                        mm = pe.matmul(PS[:, bank, P:CAUSAL], q3T[rows, h // 2, P:T], k3T[rows, h // 2, :],
                                       start=False, stop=True, skip_group_check=True)
                    mm.then_inc(S["s_ready"], 1)
                pe.wait_ge(S["negm_ready"], i + 1)
                for t in range(NT):
                    mm = pe.transpose(PS[0:2 * NH, 0, t * P:(t + 1) * P], negm2[:, t, :].bitcast(f32), identf[:])
                mm.then_inc(S["negmT_ps"], 1)
                pe.wait_ge(S["negmT_ready"], i + 1)

                def scoresT(u):
                    if u >= 3:
                        pe.wait_ge(S["exp_done"], 8 * i + u - 2)
                    for r in range(2):
                        bank, h = 2 * (u % 3) + r, 2 * u + r
                        pe.matmul(PS[:, bank, 0:CAUSAL], selh[:, h, :], negmT[:], start=True, stop=False,
                                  skip_group_check=True)
                        pe.matmul(PS[:, bank, 0:CAUSAL], identb[:], maskk[:], start=False, stop=False,
                                  skip_group_check=True)
                    for r in range(2):
                        bank, h = 2 * (u % 3) + r, 2 * u + r
                        rows = slice(SLOT * (h % 2), SLOT * (h % 2) + 3 * DH)
                        pe.matmul(PS[:, bank, 0:T], k3T[rows, h // 2, 0:P], q3T[rows, h // 2, :],
                                  start=False, stop=False, skip_group_check=True)
                        mm = pe.matmul(PS[:, bank, T:CAUSAL], k3T[rows, h // 2, P:T], q3T[rows, h // 2, P:T],
                                       start=False, stop=True, skip_group_check=True)
                    mm.then_inc(S["st_ready"], 1)

                def weigh_values(u):
                    pe.wait_ge(S["exp_done"], 8 * i + u + 1)
                    for r in range(2):
                        h = 2 * u + r
                        cols = slice(h * (DH + 1), (h + 1) * (DH + 1))
                        pe.matmul(PS[:, 6, cols], pT[:, u % 3, r, 0:P], vaug[:, 0, h, :], start=True, stop=True)
                        pe.matmul(PS[:, 7, cols], pT[:, u % 3, r, P:T], vaug[:, 0, h, :], start=True, stop=False)
                        mm = pe.matmul(PS[:, 7, cols], pT[:, u % 3, r, T:CAUSAL], vaug[:, 1, h, :],
                                       start=False, stop=True)
                    mm.then_inc(S["pv_done"], 1)

                for u in range(NH // 2 + 1):
                    if u < NH // 2:
                        scoresT(u)
                    if u >= 1:
                        weigh_values(u - 1)

                pe.wait_ge(S["ctx_split"], 2 * (i + 1))
                for t in range(NT):
                    terms = ((ctx_hi, w0h), (ctx_lo, w0h), (ctx_hi, w0l))
                    for n, (a, w) in enumerate(terms):
                        mm = pe.matmul(PS[:, 2 + t, 0:WC], a[:, t * P:(t + 1) * P], w[:],
                                       start=(n == 0), stop=(n == 2))
                mm.then_inc(S["feat_ps"], 1)
                pe.wait_ge(S["on_ready"], i + 1)
                for t in range(NT):
                    for k in range(KD):
                        mm = pe.transpose(PS[:, 0, k * T + t * P:k * T + (t + 1) * P],
                                          o_sb[:, t, k * P:(k + 1) * P], identf[:])
                mm.then_inc(S["oT_ps"], 1)
                pe.wait_ge(S["oT_ready"], i + 1)
                for t in range(NT):
                    for k in range(KD):
                        mm = pe.matmul(PS[:, 1, t * D:(t + 1) * D], oT[:, k, t * P:(t + 1) * P], wo_sb[:, k, :],
                                       start=(k == 0), stop=(k == KD - 1))
                mm.then_inc(S["y_ready"], 1)

                for layer in range(2):
                    if layer == 1:
                        pe.wait_ge(S["ghT_ready"], 2 * i + 1)
                        pe.wait_ge(S["lr_done"], 8 * i + 4)
                        for t in range(NT):
                            n = 0
                            for k in range(KD):
                                for a, w in ((ghT_hi, w1h), (ghT_lo, w1h), (ghT_hi, w1l)):
                                    mm = pe.matmul(PS[:, 2 + t, 0:WC], a[:, k, t * P:(t + 1) * P], w[:, k, :],
                                                   start=(n == 0), stop=(n == 3 * KD - 1))
                                    n += 1
                        mm.then_inc(S["feat_ps"], 1)
                    pe.wait_ge(S["st2_ready"], 2 * i + layer + 1)
                    for which in range(2):
                        for t in range(NT):
                            c0 = which * T + t * P
                            mm = pe.transpose(PS[0:2 * GH, 4, c0:c0 + P], st2[:, t, which, :].bitcast(f32), identf[:])
                    mm.then_inc(S["stT_ps"], 1)
                    pe.wait_ge(S["stT_ready"], 2 * i + layer + 1)

                    def pair_scores(c):
                        t, z = c // 2, 4 * layer + c
                        if z >= 2:
                            pe.wait_ge(S["lr_done"], 8 * i + z - 1)
                        elif c == 0:
                            pe.wait_ge(S["y_used"], i + 1)
                        else:
                            pe.wait_ge(S["feat_ready"], 2 * i + 1)
                        if z == 5:
                            pe.wait_ge(S["feat_ready"], 2 * i + 2)
                        for b in range(2):
                            bank, h0 = 2 * (c % 2) + b, 4 * (c % 2) + 2 * b
                            pe.matmul(PS[:, bank, :], stT[:, 0, t * P:(t + 1) * P], onehot[:, h0:h0 + 2, :],
                                      start=True, stop=False, skip_group_check=True)
                            for r in range(2):
                                mm = pe.matmul(PS[:, bank, r * T:(r + 1) * T], onehot[:, h0 + r, 0:P], stT[:, 1, :],
                                               start=False, stop=(r == 1), skip_group_check=True)
                        mm.then_inc(S["z_ready"], 1)

                    def turn_alpha(q):
                        n, c = 8 * layer + q, q // 2
                        pe.wait_ge(S["alpha_ready"], 16 * i + n + 1)
                        if n >= 2:
                            pe.wait_ge(S[("aTA_done", "aTD_done")[q % 2]], 8 * i + n // 2)
                        for r in range(2):
                            for m in range(2):
                                a = 2 * r + m
                                mm = pe.transpose(PS[:, 4 + q % 2, a * P:(a + 1) * P],
                                                  al[:, (4 * layer + c) % 3, 2 * (q % 2) + r, m * P:(m + 1) * P],
                                                  identf[:])
                        mm.then_inc(S["aT_ps"], 1)

                    def weigh_features(q):
                        t, n = q // 4, 8 * layer + q
                        pe.wait_ge(S[("aTA_done", "aTD_done")[q % 2]], 8 * i + n // 2 + 1)
                        if q == 0:
                            pe.wait_ge(S["feat_ready"], 2 * i + layer + 1)
                        for r in range(2):
                            h = 4 * ((q // 2) % 2) + 2 * (q % 2) + r
                            for m in range(2):
                                mm = pe.matmul(PS[:, 6 + t, h * GA:(h + 1) * GA], aT[:, q % 4, 2 * r + m, :],
                                               feat[:, m, h, :], start=(m == 0), stop=(m == 1))
                        mm.then_inc(S["gpv_done"], 1)

                    pair_scores(0)
                    pair_scores(1)
                    for q in range(9):
                        if q < 8:
                            turn_alpha(q)
                        if q in (1, 3):
                            pair_scores(2 + q // 2)
                        if q >= 1:
                            weigh_features(q - 1)
                    pe.wait_ge(S["gh_ready"], 2 * i + layer + 1)
                    src = (gh, x2b)[layer]
                    for t in range(NT):
                        for k in range(KD):
                            mm = pe.transpose(PS[:, 4, k * T + t * P:k * T + (t + 1) * P],
                                              src[:, t, k * P:(k + 1) * P], identf[:])
                    mm.then_inc(S["ghT_ps"], 1)

            pe.wait_ge(S["ghT_ready"], 2 * B)
            for t in range(NTT):
                n = 0
                for k in range(KD):
                    for a, w in ((x2T_hi, gw_hi), (x2T_lo, gw_hi), (x2T_hi, gw_lo)):
                        mm = pe.matmul(PS[:, 7, t * NGP:(t + 1) * NGP], a[:, k, t * P:(t + 1) * P], w[:, k, :],
                                       start=(n == 0), stop=(n == 3 * KD - 1))
                        n += 1
            mm.then_inc(S["logit_ps"], 1)
            pe.wait_ge(S["comb_ready"], 1)
            for t in range(NTT):
                mm = pe.transpose(PS[0:3 * NG, 7, t * SLOT:(t + 1) * SLOT].bitcast(bf16),
                                  combp[:, t, 0:3 * NG], identb[:])
            mm.then_inc(S["combT_ps"], 1)

            def gate_up(n, slot, c, fresh=False):
                for which, bank, used, ready in ((0, 4, "silu_done", "g_ready"), (1, 5, "u_used", "u_ready")):
                    if not fresh:
                        pe.wait_ge(S[used], n)
                    s = 0
                    for k in range(KD):
                        w0 = (2 * which + k) * P
                        for w, a in ((whi, x2T_hi), (whi, x2T_lo), (wlo, x2T_hi)):
                            mm = pe.matmul(PS[:, bank, :], w[:, slot, w0:w0 + P],
                                           a[:, k, c * CHUNK:(c + 1) * CHUNK], start=(s == 0), stop=(s == 3 * KD - 1))
                            s += 1
                    mm.then_inc(S[ready], 1)
                if fresh:
                    pe.wait_ge(S["combT_ready"], 1)
                else:
                    pe.wait_ge(S["c_used"], n)
                pe.matmul(PS[:, 6, :], gsel[:, slot, :], combT[:, c * CHUNK:(c + 1) * CHUNK],
                          start=True, stop=True).then_inc(S["c_ready"], 1)

            def down(n, slot, c, first=False, last=False):
                pe.wait_ge(S["hid_ready"], n + 1)
                for t in range(CHUNK // P):
                    bank, cols = 2 * c + t // 2, slice((t % 2) * D, (t % 2 + 1) * D)
                    for s, (a, w) in enumerate(((hid_hi, whi), (hid_lo, whi), (hid_hi, wlo))):
                        mm = pe.matmul(PS[:, bank, cols], a[:, c, t * P:(t + 1) * P], w[:, slot, 4 * P:WJ],
                                       start=(first and s == 0 and t % 2 == 0), stop=(last and s == 2),
                                       skip_group_check=True)
                mm.then_inc(S["down_done"], 1)

            pe.wait_ge(S["w_split"], 1)
            gate_up(0, 0, 0, fresh=True)
            gate_up(1, 0, 1)
            down(0, 0, 0, first=True)
            pe.wait_ge(S["w_split"], 2)
            gate_up(2, 1, 0)
            down(1, 0, 1, first=True)
            with pe.Fori(0, NF // 2 - 1) as m:
                for o in range(2):
                    j = 2 * m + 1 + o
                    slot, after = (1 + o) % 2, o % 2
                    gate_up(NCH * j + 1, slot, 1)
                    down(NCH * j, slot, 0)
                    pe.wait_ge(S["w_split"], j + 2)
                    gate_up(NCH * j + 2, after, 0)
                    down(NCH * j + 1, slot, 1)
            n = NCH * (NF - 1)
            gate_up(n + 1, 1, 1)
            down(n, 1, 0, last=True)
            down(n + 1, 1, 1, last=True)

        @block.vector
        def _(dve):
            dve.wait_ge(S["gat_fold_ps"], 1)
            setup = Steps(dve, S["setup_step"])
            setup.mark(dve.tensor_copy(w0c[:, D:WC], PS[0:CF, 0, 0:2 * GH]))
            setup.mark(dve.tensor_copy(w1c[:, :, D:WC], PS[:, 1:1 + KD, 0:2 * GH]))
            setup.wait()
            setup.mark(dve.tensor_copy(w0h[:], w0c[:]))
            setup.mark(dve.tensor_copy(w1h[:], w1c[:]))
            dve.wait_ge(S["router_w_loaded"], 16)
            setup.mark(dve.tensor_copy(gw_hi[:], gw_sb[:]))
            setup.wait()
            dve.tensor_tensor(w0l[:], w0c[:], w0h[:].bitcast(f32), ALU.subtract)
            dve.tensor_tensor(gw_lo[:], gw_sb[:], gw_hi[:].bitcast(f32), ALU.subtract)
            dve.tensor_tensor(w1l[:], w1c[:], w1h[:].bitcast(f32), ALU.subtract).then_inc(S["gat_w_ready"], 1)
            dve.wait_ge(S["setup_zero"], 6)
            dve.wait_ge(S["att_w_loaded"], 64)
            dve.wait_ge(S["consts_loaded"], 16 * 7)

            with dve.Fori(0, B) as i:
                chain = Steps(dve, S["dve_step"], DVE_STEPS * i)

                def norm(source, add, target, n):
                    ins = dve.tensor_tensor(resid[:], source, add, ALU.add)
                    if n == 0:
                        ins.then_inc(S["y_used"], 1)
                        dve.wait_ge(S["y_used"], i + 1)
                    else:
                        chain.link(ins)
                    for t in range(NT):
                        chain.mark(dve.bn_stats(stats[:, t, :], resid[:, t, :]))
                    chain.wait()
                    dve.tensor_tensor(idle_v[:], mhalf[:, 0:1], mhalf[:, 0:1], ALU.mult)
                    for t in range(NT):
                        chain.mark(dve.bn_aggr(meanvar[:, t, :], stats[:, t, :]))
                    chain.wait()
                    dve.tensor_scalar(vareps[:], meanvar[:, :, 1], EPS, None, ALU.add).then_inc(S["var_ready"], 1)
                    dve.wait_ge(S["rstd_ready"], 2 * i + n + 1)
                    for t in range(NT):
                        ins = dve.tensor_scalar(target[:, t, :], resid[:, t, :], meanvar[:, t, 0:1], rstd[:, t:t + 1],
                                                ALU.subtract, ALU.mult)
                    return ins

                for t in range(NT):
                    dve.wait_ge(S["qkv_ready"], NT * i + t + 1)
                    dve.tensor_tensor(qk[:, t, :], PS[:, t, :], bqkv_sb[:, 0:2 * D], ALU.add).then_inc(S["qk_biased"], 1)
                    dve.tensor_tensor(vaug[:, t, :, 0:DH],
                                      PS[:, 2 + t, 0:D].rearrange("p (h d) -> p h d", d=DH),
                                      bqkv_sb[:, 2 * D:3 * D].rearrange("p (h d) -> p h d", d=DH),
                                      ALU.add).then_inc(S["v_ready"], 1)
                for t in range(NT):
                    dve.wait_ge(S["qk_biased"], NT * i + t + 1)
                    cosines = rope_sb[:, t, 0, :].unsqueeze(1).broadcast_to([P, 2 * NH, DH])
                    chain.link(dve.tensor_tensor(t1[:, t, :].rearrange("p (h d) -> p h d", d=DH),
                                                 qk[:, t, :].rearrange("p (h d) -> p h d", d=DH),
                                                 cosines, ALU.mult))
                    dve.wait_ge(S["t2_ready"], NT * i + t + 1)
                    c = t1[:, t, :].rearrange("p (h f e) -> p h f e", e=2, f=DH // 2)
                    s = t2[:, t, :].rearrange("p (h f e) -> p h f e", e=2, f=DH // 2)
                    dve.tensor_tensor(rot[:, t, :, 0:DH // 2], c[:, :, :, 0], s[:, :, :, 1], ALU.add)
                    dve.tensor_tensor(rot[:, t, :, DH // 2:DH], c[:, :, :, 1], s[:, :, :, 0],
                                      ALU.add).then_inc(S["rot_ready"], 1)
                    dve.wait_ge(S["rot_ready"], NT * i + t + 1)
                    qv = q3[:, t, :].rearrange("p (h s) -> p h s", s=SLOT)
                    src = rot[:, t, 0:NH, :]
                    dve.tensor_copy(qv[:, :, 2 * DH:3 * DH], src)
                    chain.link(dve.tensor_copy(qv[:, :, 0:DH], src))
                    dve.tensor_tensor(qv[:, :, DH:2 * DH], src, qv[:, :, 0:DH].bitcast(f32),
                                      ALU.subtract).then_inc(S["q3_ready"], 1)
                for g in range(4):
                    dve.wait_ge(S["s_ready"], 4 * i + g + 1)
                    b = 4 * (g % 2)
                    dve.tensor_reduce(negm[:, 0, 4 * g:4 * g + 4], PS[:, b:b + 4, 0:P], AX.X, ALU.max, negate=True)
                    dve.tensor_reduce(negm[:, 1, 4 * g:4 * g + 4], PS[:, b:b + 4, P:CAUSAL], AX.X, ALU.max,
                                      negate=True).then_inc(S["smax_done"], 1)
                dve.wait_ge(S["smax_done"], 4 * (i + 1))
                chain.link(dve.tensor_copy(negm2[:, :, 0:NH], negm[:]))
                dve.tensor_tensor(negm2[:, :, NH:2 * NH], negm[:], negm2[:, :, 0:NH].bitcast(f32),
                                  ALU.subtract).then_inc(S["negm_ready"], 1)
                dve.wait_ge(S["negmT_ps"], i + 1)
                dve.tensor_copy(negmT[:, 0:T], PS[0:2 * NH, 0, 0:T])
                dve.tensor_copy(negmT[:, T:CAUSAL], PS[0:2 * NH, 0, P:T]).then_inc(S["negmT_ready"], 1)

                dve.wait_ge(S["pv_done"], 8 * (i + 1))
                o_ps = PS[:, 6:8, 0:NH * (DH + 1)].rearrange("p t (h d) -> p t h d", d=DH + 1)
                chain.link(dve.reciprocal(orec[:], o_ps[:, :, :, DH]))
                dve.tensor_tensor(o_sb[:].rearrange("p t (h d) -> p t h d", d=DH), o_ps[:, :, :, 0:DH],
                                  orec[:].unsqueeze(3).broadcast_to([P, NT, NH, DH]), ALU.mult).then_inc(S["on_ready"], 1)

                def split_scores(layer):
                    dve.wait_ge(S["feat_ps"], 2 * i + layer + 1)
                    src = PS[:, 2:4, D:WC].rearrange("p t (w h) -> p t w h", h=GH)
                    chain.link(dve.tensor_copy(st2[:, :, :, 0:GH], src))
                    dve.tensor_tensor(st2[:, :, :, GH:2 * GH], src, st2[:, :, :, 0:GH].bitcast(f32),
                                      ALU.subtract).then_inc(S["st2_ready"], 1)

                split_scores(0)
                dve.wait_ge(S["y_ready"], i + 1)
                dve.wait_ge(S["xb_ready"], i + 1)
                chain.link(norm(PS[:, 1, :].rearrange("p (t d) -> p t d", t=NT), xb[:], x1, 0))
                chain.mark(dve.tensor_scalar(mk[:], x1[:], 1.0, MASK_SCALE, ALU.subtract, ALU.mult))

                for layer in range(2):
                    if layer == 1:
                        split_scores(1)
                    dve.wait_ge(S["stT_ps"], 2 * i + layer + 1)
                    dve.tensor_copy(stT[:], PS[0:2 * GH, 4, :].rearrange("p (w n) -> p w n", w=2)).then_inc(
                        S["stT_ready"], 1)

                    def mask_and_max(c):
                        t, z, b = c // 2, 4 * layer + c, 2 * (c % 2)
                        a = al[:, z % 3, :, :]
                        dve.wait_ge(S["y_copied"], 8 * i + z + 1)
                        dve.tensor_tensor(a, PS[:, b:b + 2, :].rearrange("p b (h m) -> p (b h) m", m=T), a,
                                          ALU.max).then_inc(S["lr_done"], 1)
                        dve.wait_ge(S["lr_done"], 8 * i + z + 1)
                        if c == 0:
                            chain.wait()
                        dve.tensor_tensor(idle_v[:], mhalf[:, 0:1], mhalf[:, 0:1], ALU.mult)
                        for h in range(4):
                            ins = dve.tensor_tensor_reduce(out=a[:, h, :], in0=a[:, h, :], in1=mk[:, t, :], scale=1.0,
                                                           scalar=-3.4e38, op0=ALU.add, op1=ALU.max,
                                                           accum_out=gmax[:, 4 * c + h:4 * c + h + 1])
                        chain.link(ins)
                        dve.tensor_scalar(ngmax[:, 4 * c:4 * c + 4], gmax[:, 4 * c:4 * c + 4], -1.0, None,
                                          ALU.mult).then_inc(S["v_masked"], 1)

                    def evacuate(q):
                        n = 8 * layer + q
                        dve.wait_ge(S["aT_ps"], 16 * i + n + 1)
                        if n >= 4:
                            dve.wait_ge(S["gpv_done"], 16 * i + n - 3)
                        dve.tensor_copy(aT[:, q % 4, :, :],
                                        PS[:, 4 + q % 2, :].rearrange("p (a c) -> p a c", c=P)).then_inc(
                                            S["aTD_done"], 1)

                    mask_and_max(0)
                    for c in range(4):
                        if c + 1 < 4:
                            mask_and_max(c + 1)
                        evacuate(2 * c + 1)
                    dve.wait_ge(S["gpv_done"], 16 * i + 8 * (layer + 1))
                    g_ps = PS[:, 6:8, 0:GH * GA].rearrange("p t (h o) -> p t h o", o=GA)
                    chain.link(dve.reciprocal(grec[:], g_ps[:, :, :, GO]))
                    chain.link(dve.tensor_tensor(gy[:].rearrange("p t (h o) -> p t h o", o=GO), g_ps[:, :, :, 0:GO],
                                                 grec[:].unsqueeze(3).broadcast_to([P, NT, GH, GO]), ALU.mult))
                    chain.link(dve.tensor_tensor(gy[:], gy[:], b01[:, layer, :].unsqueeze(1).broadcast_to([P, NT, D]),
                                                 ALU.add))
                    dve.tensor_scalar(gpos[:], gy[:], 0.0, None, ALU.max)
                    dve.tensor_scalar(gneg[:], gy[:], 0.0, None, ALU.min).then_inc(S["gneg_ready"], 1)
                    dve.wait_ge(S["gexp_ready"], 2 * i + layer + 1)
                    ins = dve.scalar_tensor_tensor(gh[:], gneg[:], -1.0, gpos[:], ALU.add, ALU.add)
                    if layer == 0:
                        ins.then_inc(S["gh_ready"], 1)
                    else:
                        chain.link(ins)
                        norm(gh[:], x1[:], x2b, 1).then_inc(S["gh_ready"], 1)
                    dve.wait_ge(S["ghT_ps"], 2 * i + layer + 1)
                    src = PS[:, 4, :].rearrange("p (k n) -> p k n", k=KD)
                    if layer == 0:
                        hi, lo = ghT_hi[:], ghT_lo[:]
                    else:
                        hi, lo = x2T_hi[:, :, bass.ts(i, T)], x2T_lo[:, :, bass.ts(i, T)]
                    chain.link(dve.tensor_copy(hi, src))
                    dve.tensor_tensor(lo, src, hi.bitcast(f32), ALU.subtract).then_inc(S["ghT_ready"], 1)
                assert chain.n == DVE_STEPS, chain.n

            r = Steps(dve, S["setup_step"], 0)
            r.n = setup.n
            dve.wait_ge(S["logit_ps"], 1)
            logits = PS[:, 7, 0:NTT * NGP].rearrange("p (t g) -> p t g", g=NGP)[:, :, 0:NE]
            r.link(dve.tensor_reduce(r_s[:], logits, AX.X, ALU.max))
            wide = lambda a: a.unsqueeze(2).broadcast_to([P, NTT, NE])
            dve.tensor_tensor(r_a[:], logits, wide(r_s[:]), ALU.subtract).then_inc(S["gate_centered"], 1)
            dve.wait_ge(S["gate_exp"], 2)
            r.link(dve.tensor_reduce(r_s[:], r_b[:], AX.X, ALU.add))
            r.link(dve.reciprocal(r_s[:], r_s[:]))
            r.link(dve.tensor_tensor(r_a[:], r_b[:], wide(r_s[:]), ALU.mult))
            for t in range(NTT):
                ins = dve.max(top8[:, t, :], r_a[:, t, :])
            r.link(ins)
            fourth = top8[:, :, TOPK - 1]
            r.mark(dve.tensor_tensor(r_b[:], r_a[:], wide(fourth), ALU.is_gt))
            r.mark(dve.tensor_tensor(r_c[:], r_a[:], wide(fourth), ALU.is_equal))
            r.wait()
            r.link(dve.tensor_reduce(r_s[:], r_b[:], AX.X, ALU.add))
            r.link(dve.tensor_scalar(r_s[:], r_s[:], -1.0, float(TOPK), ALU.mult, ALU.add))
            rank = comb[:].rearrange("p t g -> p (t g)")[:, 0:NTT * NE]
            r.link(dve.tensor_tensor_scan(rank, reset_sb[:], r_c[:].rearrange("p t g -> p (t g)"), 0.0,
                                          ALU.mult, ALU.add))
            rank3 = rank.rearrange("p (t g) -> p t g", g=NE)
            r.link(dve.tensor_tensor(rank3, rank3, wide(r_s[:]), ALU.is_le))
            r.link(dve.tensor_tensor(r_c[:], r_c[:], rank3, ALU.mult))
            r.link(dve.tensor_tensor(r_b[:], r_b[:], r_c[:], ALU.add))
            r.link(dve.tensor_tensor(r_b[:], r_b[:], r_a[:], ALU.mult))
            r.link(dve.tensor_reduce(r_s[:], r_b[:], AX.X, ALU.add))
            r.link(dve.reciprocal(r_s[:], r_s[:]))
            r.mark(dve.tensor_tensor(comb[:, :, 0:NE], r_b[:], wide(r_s[:]), ALU.mult))
            r.link(dve.tensor_scalar(r_t[:], r_t[:], 1.0, None, ALU.add))
            r.link(dve.reciprocal(comb[:, :, NE], r_t[:]))
            for part in range(3):
                dst = combp[:, :, part * NG:(part + 1) * NG]
                ins = dve.tensor_copy(dst, comb[:])
                if part < 2:
                    r.link(ins)
                    r.link(dve.tensor_tensor(comb[:], comb[:], dst, ALU.subtract))
            ins.then_inc(S["comb_ready"], 1)
            dve.wait_ge(S["combT_ps"], 1)
            dve.tensor_copy(combT[:], PS[0:3 * NG, 7, :].bitcast(bf16)).then_inc(S["combT_ready"], 1)

            def hidden(n, c, fresh=False):
                dve.wait_ge(S["silu_done"], n + 1)
                dve.wait_ge(S["u_ready"], n + 1)
                dve.tensor_tensor(hu[:, c, :], PS[:, 5, :], sg[:, c, :], ALU.mult).then_inc(S["u_used"], 1)
                dve.wait_ge(S["u_used"], n + 1)
                dve.wait_ge(S["c_ready"], n + 1)
                dve.tensor_tensor(hid[:, c, :], PS[:, 6, :], hu[:, c, :], ALU.mult).then_inc(S["c_used"], 1)
                if not fresh:
                    dve.wait_ge(S["down_done"], n - 1)
                dve.wait_ge(S["hid_rounded"], n + 1)
                dve.tensor_tensor(hid_lo[:, c, :], hid[:, c, :], hid_hi[:, c, :].bitcast(f32),
                                  ALU.subtract).then_inc(S["hid_ready"], 1)

            for c in range(NCH):
                hidden(c, c, fresh=True)
            with dve.Fori(1, NF) as j:
                for c in range(NCH):
                    hidden(NCH * j + c, c)

            dve.wait_ge(S["down_done"], NCH * NF)
            dve.wait_ge(S["x2_stored"], B)
            f = r
            for b in range(4):
                f.mark(dve.tensor_tensor(res3[:, 2 * b:2 * b + 2, :], PS[:, b, :].rearrange("p (t d) -> p t d", d=D),
                                         x2[:, 2 * b:2 * b + 2, :], ALU.add))
            f.wait()
            for t in range(NTT):
                f.mark(dve.bn_stats(stats3[:, t, :], res3[:, t, :]))
            f.wait()
            for t in range(NTT):
                f.mark(dve.bn_aggr(mv3[:, t, :], stats3[:, t, :]))
            f.wait()
            dve.tensor_scalar(ve3[:], mv3[:, :, 1], EPS, None, ALU.add).then_inc(S["var3_ready"], 1)
            dve.wait_ge(S["rstd3_ready"], 1)
            for t in range(NTT):
                dve.tensor_scalar(y3[:, t, :], res3[:, t, :], mv3[:, t, 0:1], rstd3[:, t:t + 1],
                                  ALU.subtract, ALU.mult).then_inc(S["out_ready"], 1)


def layouts(np, a):
    c = np.ascontiguousarray

    def rows(w):
        return c(w.reshape(-1, P, w.shape[-1]).transpose(1, 0, 2))

    x, con = a["x"], a["ctx_512"]
    out = {
        "xT": c(x.transpose(0, 2, 1).reshape(B, KD, P, T).transpose(0, 2, 1, 3)),
        "x": c(x.reshape(B, NT, P, D).transpose(0, 2, 1, 3)),
        "ctxT": c(con.transpose(0, 2, 1)),
        "wqkvT": rows(a["L0_attn_w_qkv"].T),
        "bqkv": a["L0_attn_b_qkv"],
        "woT": rows(a["L0_attn_w_out"].T),
        "bo": a["L0_attn_b_out"],
    }
    for n in range(2):
        w = a[f"L0_xattn_W{n}"]
        fold = np.zeros((GH, GO, 2 * GH), np.float32)
        for h in range(GH):
            fold[h, :, h] = a[f"L0_xattn_a_self{n}"][h]
            fold[h, :, GH + h] = a[f"L0_xattn_a_neigh{n}"][h]
        flat = w.transpose(1, 0, 2).reshape(w.shape[1], D)
        out[f"W{n}f"] = c(flat) if n == 0 else rows(flat)
        out[f"W{n}r"] = rows(flat.T)
        out[f"A{n}"] = rows(fold.reshape(D, 2 * GH))
        out[f"b{n}"] = c(a[f"L0_xattn_b{n}"].reshape(D))
    router = np.zeros((D, NGP), np.float32)
    router[:, 0:NE] = a["L0_ffn_gate_w"].T
    router[:, NE] = a["L0_ffn_shared_expert_gate_w"][0]
    out["gwT"] = rows(router)
    hidden = NF * P
    wide = []
    for kind in ("gate", "up"):
        w = np.zeros((hidden, D), np.float32)
        w[0:NE * FE] = a[f"L0_ffn_expert_{kind}_w"].reshape(NE * FE, D)
        w[NE * FE:NE * FE + FS] = a[f"L0_ffn_shared_{kind}_w"]
        wide.append(w.reshape(NF, P, KD, P).transpose(0, 3, 2, 1).reshape(NF, P, KD * P))
    w = np.zeros((hidden, D), np.float32)
    w[0:NE * FE] = a["L0_ffn_expert_down_w"].transpose(0, 2, 1).reshape(NE * FE, D)
    w[NE * FE:NE * FE + FS] = a["L0_ffn_shared_down_w"].T
    wide.append(w.reshape(NF, P, D))
    out["ffnW"] = c(np.concatenate(wide, axis=2))
    return out


def constants(np, bf16):
    half = DH // 2
    freqs = np.float32(10000.0) ** (-np.arange(half, dtype=np.float32) / np.float32(half))
    theta = np.arange(T, dtype=np.float32)[:, None] * freqs[None, :]
    cos, sin = np.cos(theta), np.sin(theta)
    table = np.zeros((T, 2, half, 2), np.float32)
    table[:, 0, :, 0], table[:, 0, :, 1] = cos, cos
    table[:, 1, :, 0], table[:, 1, :, 1] = sin, -sin
    above = np.where(np.arange(P)[None, :] > np.arange(P)[:, None], NEG, 0.0)
    none = np.zeros((P, P))
    head = np.zeros((2, NH, NH, P), np.float32)
    node = np.zeros((2, GH, GH, T), np.float32)
    for h in range(NH):
        head[:, h, h] = 1.0
    for h in range(GH):
        node[:, h, h] = 1.0
    expert = np.minimum(np.arange(NF * P) // FE, NE)
    gates = np.zeros((3, NG, NF * P), np.float32)
    gates[:, expert, np.arange(NF * P)] = 1.0
    reset = np.ones((P, NTT, NE), np.float32)
    reset[:, :, 0] = 0.0
    return {
        "rope_cs": np.ascontiguousarray(table.reshape(NT, P, 2, DH).transpose(1, 0, 2, 3)),
        "causal_q": np.concatenate([above, none, above], axis=1).astype(bf16),
        "causal_k": np.concatenate([above.T, none, above.T], axis=1).astype(bf16),
        "ident": np.eye(P, dtype=np.float32),
        "head_sel": head.reshape(2 * NH, NH, P),
        "node_onehot": node.reshape(2 * GH, GH, T),
        "gate_sel": np.ascontiguousarray(gates.reshape(3 * NG, NF, P).transpose(1, 0, 2)).astype(bf16),
        "scan_reset": reset.reshape(P, NTT * NE),
    }


_ORDER = ["xT", "x", "ctxT", "wqkvT", "bqkv", "woT", "bo", "W0f", "W0r", "A0", "b0", "W1f", "W1r", "A1", "b1",
          "gwT", "ffnW", "rope_cs", "causal_q", "causal_k", "ident", "head_sel", "node_onehot", "gate_sel",
          "scan_reset"]


def kernel(**inputs):
    import numpy as np
    import ml_dtypes
    import concourse.bacc as bacc
    from concourse.bass_utils import run_bass_kernel_spmd

    given = {name: np.asarray(value) for name, value in inputs.items()}
    arrays = {**layouts(np, given), **constants(np, ml_dtypes.bfloat16)}
    nc = bacc.Bacc("TRN2", target_bir_lowering=False, num_devices=1)
    args, sent = [], {}
    for name in _ORDER:
        a = np.ascontiguousarray(arrays[name])
        sent[f"in_{name}"] = a
        args.append(nc.dram_tensor(f"in_{name}", a.shape, mybir.dt.from_np(a.dtype), kind="ExternalInput").ap())
    out = nc.dram_tensor("out_0", (NTT, P, D), mybir.dt.float32, kind="ExternalOutput").ap()
    decoder_layer(nc, *args, out)
    result = run_bass_kernel_spmd(nc, [sent], core_ids=[0])
    return result.results[0]["out_0"].reshape(B, T, D)
```

```python
import concourse.bass as bass
from concourse import mybir
from contextlib import ExitStack

B, T, D = 4, 256, 256
P = 128
NT = T // P
KD = D // P
NH, DH = 16, 16
SLOT = 64
VS = 32
CF, GH, GO = 64, 8, 32
NU = NT * GH // 2
PTS, ALS, ATS = 4, 4, 3
NE, FE, FS, TOPK = 16, 176, 704, 4
NG = NE + 1
NGP = NG + 1
NF = -(-(NE * FE + FS) // P)
NTT = B * NT
CHUNK = 512
NCH = B * T // CHUNK
EPS = 1e-5
NEG = -1e30
MASK_SCALE = 1e10
CAUSAL = P + T


class Steps:

    def __init__(self, eng, sem, base=0):
        self.eng, self.sem, self.base, self.n = eng, sem, base, 0

    def mark(self, ins):
        ins.then_inc(self.sem, 1)
        self.n += 1

    def wait(self):
        self.eng.wait_ge(self.sem, self.base + self.n)

    def link(self, ins):
        self.mark(ins)
        self.wait()


ATT_STEPS, GAT_STEPS = 6, 22


def decoder_layer(nc, xT, x, ctxT, wqkvT, bqkv, woT, bo, W0f, W0r, A0, b0, W1f, W1r, A1, b1,
                  gwT, ffnW, rope_cs, causal_q, causal_k, ident, head_sel, node_onehot, gate_sel,
                  scan_reset, out):
    f32, bf16, f32r = mybir.dt.float32, mybir.dt.bfloat16, mybir.dt.float32r
    ALU = mybir.AluOpType
    ACT = mybir.ActivationFunctionType
    AX = mybir.AxisListType

    ctx = ExitStack()
    with ctx:
        def sb(name, shape, dt=f32):
            return ctx.enter_context(nc.sbuf_tensor(name, shape, dt))

        def sem(name):
            return ctx.enter_context(nc.semaphore(name))

        PS = ctx.enter_context(nc.psum_tensor("PS", [P, 8, 512], f32))

        xT_sb = sb("xT_sb", [P, KD, T])
        xres = sb("xres", [P, NT, D])
        ctx_sb = sb("ctx_sb", [CF, T])
        ctx_hi = sb("ctx_hi", [CF, T], f32r)
        ctx_lo = sb("ctx_lo", [CF, T], f32r)
        wqkv_sb = sb("wqkv_sb", [P, KD, 3 * D])
        bqkv_sb = sb("bqkv_sb", [P, 3 * D])
        wo_sb = sb("wo_sb", [P, KD, D])
        bo_sb = sb("bo_sb", [P, D])
        rope_sb = sb("rope_sb", [P, NT, 2, DH])
        identf = sb("identf", [P, P])
        identb = sb("identb", [P, P], bf16)
        maskq = sb("maskq", [P, CAUSAL], bf16)
        maskk = sb("maskk", [P, CAUSAL], bf16)
        selh = sb("selh", [2 * NH, NH, P], f32r)
        onehot = sb("onehot", [2 * GH, GH, T], f32r)

        qk = sb("qk", [P, NT, 2 * D])
        t1 = sb("t1", [P, NT, 2 * D])
        t2 = sb("t2", [P, NT, 2 * D])
        rot = sb("rot", [P, NT, 2 * NH, DH])
        q3 = sb("q3", [P, NT, NH * SLOT], f32r)
        k3 = sb("k3", [P, NT, NH * SLOT], f32r)
        q3T = sb("q3T", [P, NH // 2, T], f32r)
        k3T = sb("k3T", [P, NH // 2, T], f32r)
        vaug = sb("vaug", [P, NT, NH, VS])
        negm = sb("negm", [P, NT, NH])
        negm2 = sb("negm2", [P, NT, 2 * NH], f32r)
        negmT = sb("negmT", [2 * NH, CAUSAL], f32r)
        pT = sb("pT", [P, PTS, CAUSAL])
        orec = sb("orec", [P, NT, NH])
        o_sb = sb("o_sb", [P, NT, D])
        oT = sb("oT", [P, KD, T])
        xb = sb("xb", [P, NT, D])

        resid1 = sb("resid1", [P, NT, D])
        resid2 = sb("resid2", [P, NT, D])
        stats = sb("stats", [P, NT, 6])
        meanvar = sb("meanvar", [P, NT, 2])
        vareps = sb("vareps", [P, NT])
        rstd = sb("rstd", [P, NT])
        mhalf = sb("mhalf", [P, NTT])

        idle_v, idle_p = sb("idle_v", [P, 1]), sb("idle_p", [P, 1])

        w0r_sb = sb("w0r_sb", [P, KD, CF])
        a0_sb = sb("a0_sb", [P, KD, 2 * GH])
        a1_sb = sb("a1_sb", [P, KD, 2 * GH])
        WC = D + 2 * GH
        w0c = sb("w0c", [CF, WC])
        w0h = sb("w0h", [CF, WC], f32r)
        w0l = sb("w0l", [CF, WC], f32r)
        w1c = sb("w1c", [P, KD, WC])
        w1h = sb("w1h", [P, KD, WC], f32r)
        w1l = sb("w1l", [P, KD, WC], f32r)
        b01 = sb("b01", [P, 2, D])
        x1 = sb("x1", [P, NT, D])
        mk = sb("mk", [P, NT, T])
        feat = sb("feat", [P, NT, GH, GO])
        st2 = sb("st2", [P, NT, 2, 2 * GH], f32r)
        stT = sb("stT", [2 * GH, 2, T], f32r)
        al = sb("al", [P, ALS, 2, T])
        aT = sb("aT", [P, ATS, 4, P])
        gmin = sb("gmin", [P, NT * GH])
        gsum = sb("gsum", [P, NT, GH])
        gy = sb("gy", [P, NT, D])
        grec = sb("grec", [P, NT, GH])
        gneg = sb("gneg", [P, NT, D])
        gpos = sb("gpos", [P, NT, D])
        gh = sb("gh", [P, NT, D])
        ghT_hi = sb("ghT_hi", [P, KD, T], f32r)
        ghT_lo = sb("ghT_lo", [P, KD, T], f32r)

        x2b = sb("x2b", [P, NT, D])
        x2 = sb("x2", [P, NTT, D])
        x2T_hi = sb("x2T_hi", [P, KD, B * T], f32r)
        x2T_lo = sb("x2T_lo", [P, KD, B * T], f32r)
        gw_sb = sb("gw_sb", [P, KD, NGP])
        gw_hi = sb("gw_hi", [P, KD, NGP], f32r)
        gw_lo = sb("gw_lo", [P, KD, NGP], f32r)
        reset_sb = sb("reset_sb", [P, NTT * NE])
        comb = sb("comb", [P, NTT, NG])
        logitsT = sb("logitsT", [NGP, B * T])
        r_a = sb("r_a", [P, NTT, NE])
        r_b = sb("r_b", [P, NTT, NE])
        r_c = sb("r_c", [P, NTT, NE])
        r_s = sb("r_s", [P, NTT])
        r_t = sb("r_t", [P, NTT])
        top8 = sb("top8", [P, NTT, 8])
        combp = sb("combp", [P, NTT, SLOT], bf16)
        combT = sb("combT", [3 * NG, B * T], bf16)
        WJ = 4 * P + D
        wraw = sb("wraw", [P, 2, WJ])
        gsel = sb("gsel", [3 * NG, 2, P], bf16)
        hid_hi = sb("hid_hi", [P, 2, CHUNK], f32r)
        hid_lo = sb("hid_lo", [P, 2, CHUNK], f32r)
        stats3 = sb("stats3", [P, NTT, 6])
        mv3 = sb("mv3", [P, NTT, 2])
        ve3 = sb("ve3", [P, NTT])
        rstd3 = sb("rstd3", [P, NTT])
        stage_h = al[0:2 * NH, :, :, :].rearrange("p a b c -> p (a b c)").rearrange("p (h c) -> p h c", c=P)
        stage_n = x2[0:2 * GH, :, :].rearrange("p a c -> p (a c)").rearrange("p (h c) -> p h c", c=T)
        w1r_sb = gneg
        whi = q3T[:, :, :].rearrange("p a b -> p (a b)")[:, 0:2 * WJ].rearrange("p (s w) -> p s w", s=2)
        wlo = k3T[:, :, :].rearrange("p a b -> p (a b)")[:, 0:2 * WJ].rearrange("p (s w) -> p s w", s=2)
        sg, hu, hid, sums = t1, t2, qk, t1
        res3 = q3[:, :, :].bitcast(f32).rearrange("p a (b d) -> p (a b) d", d=D)
        y3 = k3[:, :, :].bitcast(f32).rearrange("p a (b d) -> p (a b) d", d=D)

        names = """consts_loaded att_w_loaded gat_w_loaded router_w_loaded xT_loaded xres_loaded ctx_loaded
            setup_zero gat_fold_ps gat_w_ready sel_ready ctx_split
            qkv_ready qk_biased v_ready t2_ready rot_ready q3_ready k3_hi k3_ready qkT_ps qkT_ready
            s_ready smax_done negm_ready negmT_ps negmT_ready st_ready exp_done pv_done sums_copied sums_ps on_ready oT_ps
            oT_ready xb_ready y_ready y_used var_ready rstd_ready
            feat_ps st2_ready feat_ready stT_ps stT_ready z_ready y_copied lr_done v_masked
            alpha_ready aT_ps aT_done gpv_done gsums_copied gsums_ps gneg_ready gexp_ready gh_ready ghT_ps ghT_ready
            x2_stored x2T_ready att_step gat_step pool_step
            logit_ps logit_copied logits_turned gate_centered gate_exp comb_ready combT_ps combT_ready
            w_loaded0 w_loaded1 w_split wd_split g_ready u_ready c_ready silu_done u_used c_used hid_rounded hid_ready
            down_done acc_ready var3_ready rstd3_ready out_ready out_stored setup_step""".split()
        S = {n: sem(n) for n in names}

        block = ctx.enter_context(nc.Block())

        @block.sync
        def _(sp):
            for dst, src in ((rope_sb[:], rope_cs), (identf[:], ident), (maskq[:], causal_q), (maskk[:], causal_k),
                             (stage_h, head_sel), (stage_n, node_onehot), (reset_sb[:], scan_reset)):
                sp.dma_start(dst, src).then_inc(S["consts_loaded"], 16)
            for dst, src in ((w1r_sb[:], W1r), (a1_sb[:], A1), (w1c[:, :, 0:D], W1f)):
                sp.dma_start(dst, src).then_inc(S["gat_w_loaded"], 16)
            def load_batch(i, first=False):
                if not first:
                    sp.wait_ge(S["qkv_ready"], NT * i)
                sp.dma_start(xT_sb[:], xT[i]).then_inc(S["xT_loaded"], 16)
                if not first:
                    sp.wait_ge(S["ctx_split"], 2 * i)
                sp.dma_start(ctx_sb[:], ctxT[i]).then_inc(S["ctx_loaded"], 16)
                if not first:
                    sp.wait_ge(S["xb_ready"], i)
                sp.dma_start(xres[:], x[i]).then_inc(S["xres_loaded"], 16)

            load_batch(0, first=True)
            with sp.Fori(1, B) as i:
                load_batch(i)

            def load_hidden(j, slot):
                sp.dma_start(wraw[:, slot, :], ffnW[j]).then_inc(S[f"w_loaded{slot}"], 16)
                sp.dma_start(gsel[:, slot, :], gate_sel[j]).then_inc(S[f"w_loaded{slot}"], 16)

            load_hidden(0, 0)
            load_hidden(1, 1)
            with sp.Fori(1, NF // 2) as m:
                for slot in range(2):
                    sp.wait_ge(S["c_ready"], (2 * m + slot - 1) * NCH)
                    sp.wait_ge(S["wd_split"], 2 * m + slot - 1)
                    load_hidden(2 * m + slot, slot)
            for t in range(NTT):
                sp.wait_ge(S["out_ready"], t + 1)
                sp.dma_start(out[t], y3[:, t, :]).then_inc(S["out_stored"], 16)
            sp.wait_ge(S["out_stored"], 16 * NTT)

        @block.gpsimd
        def _(pool):
            pool.memset(mhalf[:], -0.5).then_inc(S["setup_zero"], 1)
            pool.memset(q3[:].bitcast(f32), 0.0).then_inc(S["setup_zero"], 1)
            pool.memset(k3[:].bitcast(f32), 0.0).then_inc(S["setup_zero"], 1)
            pool.memset(vaug[:, :, :, DH:DH + 1], 1.0).then_inc(S["setup_zero"], 1)
            pool.memset(vaug[:, :, :, DH + 1:VS], 0.0).then_inc(S["setup_zero"], 1)
            pool.memset(combp[:], 0.0).then_inc(S["setup_zero"], 1)
            pool.wait_ge(S["consts_loaded"], 16 * 7)
            pool.tensor_copy(identb[:], identf[:]).then_inc(S["sel_ready"], 1)
            pool.tensor_copy(selh[:], stage_h).then_inc(S["sel_ready"], 1)
            pool.tensor_copy(onehot[:], stage_n).then_inc(S["sel_ready"], 1)
            pool.wait_ge(S["setup_zero"], 6)

            def rotate_keys(i):
                for t in range(NT):
                    pool.wait_ge(S["qk_biased"], NT * i + t + 1)
                    sines = rope_sb[:, t, 1, :].unsqueeze(1).broadcast_to([P, 2 * NH, DH])
                    pool.tensor_tensor(t2[:, t, :].rearrange("p (h d) -> p h d", d=DH),
                                       qk[:, t, :].rearrange("p (h d) -> p h d", d=DH),
                                       sines, ALU.mult).then_inc(S["t2_ready"], 1)
                for t in range(NT):
                    pool.wait_ge(S["rot_ready"], NT * i + t + 1)
                    kv = k3[:, t, :].rearrange("p (h s) -> p h s", s=SLOT)
                    src = rot[:, t, NH:2 * NH, :]
                    pool.tensor_tensor(idle_p[:], mhalf[:, 0:1], mhalf[:, 0:1], ALU.mult)
                    pool.tensor_copy(kv[:, :, 0:DH], src).then_inc(S["k3_hi"], 1)
                    pool.tensor_copy(kv[:, :, DH:2 * DH], src)
                    pool.wait_ge(S["k3_hi"], NT * i + t + 1)
                    pool.tensor_tensor(kv[:, :, 2 * DH:3 * DH], src, kv[:, :, 0:DH].bitcast(f32),
                                       ALU.subtract).then_inc(S["k3_ready"], 1)

            def side_inputs(i, first=False):
                pool.wait_ge(S["xres_loaded"], 16 * (i + 1))
                if not first:
                    pool.wait_ge(S["y_used"], i)
                pool.tensor_tensor(xb[:], xres[:], bo_sb[:].unsqueeze(1).broadcast_to([P, NT, D]),
                                   ALU.add).then_inc(S["xb_ready"], 1)
                pool.wait_ge(S["ctx_loaded"], 16 * (i + 1))
                if not first:
                    pool.wait_ge(S["feat_ps"], 2 * i - 1)
                pool.tensor_tensor(idle_p[:], mhalf[:, 0:1], mhalf[:, 0:1], ALU.mult)
                pool.tensor_copy(ctx_hi[:], ctx_sb[:]).then_inc(S["ctx_split"], 1)
                pool.wait_ge(S["ctx_split"], 2 * i + 1)
                pool.tensor_tensor(ctx_lo[:], ctx_sb[:], ctx_hi[:].bitcast(f32),
                                   ALU.subtract).then_inc(S["ctx_split"], 1)

            def inverse_deviation(g, n):
                pool.wait_ge(S["var_ready"], 2 * g + n + 1)
                pool.tensor_tensor(rstd[:], vareps[:], mhalf[:, 0:NT], ALU.pow).then_inc(S["rstd_ready"], 1)

            def store_normed(g):
                pool.wait_ge(S["gh_ready"], 2 * (g + 1))
                pool.tensor_tensor(idle_p[:], mhalf[:, 0:1], mhalf[:, 0:1], ALU.mult)
                pool.tensor_copy(x2[:, bass.ts(g, NT), :], x2b[:]).then_inc(S["x2_stored"], 1)

            rotate_keys(0)
            side_inputs(0, first=True)
            with pool.Fori(0, B - 1) as g:
                inverse_deviation(g, 0)
                rotate_keys(g + 1)
                side_inputs(g + 1)
                inverse_deviation(g, 1)
                store_normed(g)
            inverse_deviation(B - 1, 0)

            def split_part(cols, j, slot, step, done, fresh):
                if not fresh:
                    pool.tensor_tensor(idle_p[:], mhalf[:, 0:1], mhalf[:, 0:1], ALU.mult)
                pool.tensor_copy(whi[:, slot, cols], wraw[:, slot, cols]).then_inc(S["pool_step"], 1)
                pool.wait_ge(S["pool_step"], 2 * j + step)
                pool.tensor_tensor(wlo[:, slot, cols], wraw[:, slot, cols], whi[:, slot, cols].bitcast(f32),
                                   ALU.subtract).then_inc(S[done], 1)

            def split_weights(j, slot, nth, fresh=False):
                pool.wait_ge(S[f"w_loaded{slot}"], 32 * nth)
                if not fresh:
                    pool.wait_ge(S["u_ready"], NCH * (j - 1))
                split_part(slice(0, 4 * P), j, slot, 1, "w_split", fresh)
                if not fresh:
                    pool.wait_ge(S["down_done"], NCH * (j - 1))
                split_part(slice(4 * P, WJ), j, slot, 2, "wd_split", fresh)

            pool.wait_ge(S["st_ready"], NH * B)
            split_weights(0, 0, 1, fresh=True)
            split_weights(1, 1, 1, fresh=True)
            inverse_deviation(B - 1, 1)
            store_normed(B - 1)
            pool.wait_ge(S["x2_stored"], B)
            with pool.Fori(1, NF // 2) as m:
                for slot in range(2):
                    split_weights(2 * m + slot, slot, m + 1)
            pool.wait_ge(S["var3_ready"], 1)
            pool.tensor_tensor(rstd3[:], ve3[:], mhalf[:], ALU.pow).then_inc(S["rstd3_ready"], 1)

        @block.scalar
        def _(act):
            for dst, src in ((wqkv_sb[:], wqkvT), (bqkv_sb[:], bqkv.partition_broadcast(P))):
                act.dma_start(dst, src).then_inc(S["att_w_loaded"], 16)
            for dst, src in ((wo_sb[:], woT), (bo_sb[:], bo.partition_broadcast(P))):
                act.dma_start(dst, src).then_inc(S["att_w_loaded"], 16)
            for dst, src in ((w0r_sb[:], W0r), (a0_sb[:], A0), (w0c[:, 0:D], W0f),
                             (b01[:, 0, :], b0.partition_broadcast(P)), (b01[:, 1, :], b1.partition_broadcast(P))):
                act.dma_start(dst, src).then_inc(S["gat_w_loaded"], 16)
            act.dma_start(gw_sb[:], gwT).then_inc(S["router_w_loaded"], 16)

            def turned_qk(i, n):
                t, half, which = n // 4, n % 2, (n % 4) // 2
                act.wait_ge(S["qkT_ps"], 8 * i + n + 1)
                act.activation((q3T, k3T)[which][:, 4 * half:4 * half + 4, t * P:(t + 1) * P],
                               PS[:, n % 4, :].rearrange("p (a c) -> p a c", c=P), ACT.Copy).then_inc(S["qkT_ready"], 1)

            def numerators(i, h):
                act.wait_ge(S["st_ready"], NH * i + h + 1)
                if h >= PTS:
                    act.wait_ge(S["pv_done"], NH // 2 * i + (h - PTS) // 2 + 1)
                act.activation(pT[:, h % PTS, :], PS[:, h % 2, 0:CAUSAL], ACT.Exp,
                               scale=DH ** -0.5).then_inc(S["exp_done"], 1)

            def attention_sums(i, b):
                act.wait_ge(S["pv_done"], NH // 2 * i + 4 * b + 4)
                act.activation(sums[:, b, :], PS[:, 2 + b, :], ACT.Copy).then_inc(S["sums_copied"], 1)

            def attention_out(i):
                act.wait_ge(S["oT_ps"], i + 1)
                act.activation(oT[:], PS[:, 2, :].rearrange("p (k t) -> p k t", k=KD), ACT.Copy).then_inc(S["oT_ready"], 1)

            def features(g, layer):
                act.wait_ge(S["st2_ready"], 2 * g + layer + 1)
                act.activation(feat[:], PS[:, 4:6, 0:D].rearrange("p t (h o) -> p t h o", o=GO),
                               ACT.Copy).then_inc(S["feat_ready"], 1)

            def leak(g, layer, u):
                n = NU * layer + u
                act.wait_ge(S["z_ready"], 2 * NU * g + n + 1)
                if n >= ALS:
                    act.wait_ge(S["aT_ps"], 2 * NU * g + n - ALS + 1)
                act.activation(al[:, n % ALS, :, :], PS[:, 4 + u % 2, :].rearrange("p (h m) -> p h m", m=T),
                               ACT.Copy, scale=0.2).then_inc(S["y_copied"], 1)

            def exps(g, layer, u):
                n = NU * layer + u
                act.wait_ge(S["v_masked"], 2 * NU * g + n + 1)
                for r in range(2):
                    a, c = al[:, n % ALS, r, :], 2 * u + r
                    ins = act.activation(a, a, ACT.Exp, scale=-1.0, bias=gmin[:, c:c + 1],
                                         accum_out=gsum[:, c // GH, c % GH:c % GH + 1])
                ins.then_inc(S["alpha_ready"], 1)

            def turned_alpha(g, layer, u):
                n = NU * layer + u
                act.wait_ge(S["aT_ps"], 2 * NU * g + n + 1)
                if n >= ATS:
                    act.wait_ge(S["gpv_done"], 2 * NU * g + n - ATS + 1)
                act.activation(aT[:, n % ATS, :, :], PS[:, 6, :].rearrange("p (a c) -> p a c", c=P),
                               ACT.Copy).then_inc(S["aT_done"], 1)

            def feature_sums(g, layer):
                act.wait_ge(S["gpv_done"], NU * (2 * g + layer + 1))
                act.activation(gy[:].rearrange("p t d -> p (t d)"), PS[:, 7, :], ACT.Copy).then_inc(S["gsums_copied"], 1)

            def copy_logits(g):
                act.wait_ge(S["logit_ps"], g + 1)
                act.activation(logitsT[:, bass.ts(g, T)], PS[0:NGP, 6, 0:T], ACT.Copy).then_inc(S["logit_copied"], 1)

            def elu_exp(g, layer):
                act.wait_ge(S["gneg_ready"], 2 * g + layer + 1)
                act.activation(gneg[:], gneg[:], ACT.Exp).then_inc(S["gexp_ready"], 1)

            def both(g, i):
                gat, att = g is not None, i is not None
                for layer in range(2):
                    if gat:
                        features(g, layer)
                        leak(g, layer, 0)
                        leak(g, layer, 1)
                    for s in range(NU):
                        if gat:
                            exps(g, layer, s)
                            if s + 2 < NU:
                                leak(g, layer, s + 2)
                        if att and layer == 0 and s in (1, 2):
                            for n in range(4 * (s - 1), 4 * s):
                                turned_qk(i, n)
                        if gat:
                            turned_alpha(g, layer, s)
                        if att and layer == 1:
                            numerators(i, 2 * s)
                            numerators(i, 2 * s + 1)
                            if s == 5:
                                attention_sums(i, 0)
                    if att and layer == 1:
                        attention_sums(i, 1)
                    if gat:
                        feature_sums(g, layer)
                    if att and layer == 1:
                        attention_out(i)
                    if gat:
                        elu_exp(g, layer)
                if gat:
                    copy_logits(g)

            both(None, 0)
            with act.Fori(0, B - 1) as g:
                both(g, g + 1)
            both(B - 1, None)

            act.wait_ge(S["gate_centered"], 1)
            act.activation(r_b[:], r_a[:], ACT.Exp).then_inc(S["gate_exp"], 1)
            act.activation(r_t[:], PS[:, 7, 0:NTT * NGP].rearrange("p (t g) -> p t g", g=NGP)[:, :, NE],
                           ACT.Exp, scale=-1.0).then_inc(S["gate_exp"], 1)

            def silu(n, c):
                act.wait_ge(S["g_ready"], n + 1)
                if not isinstance(n, int) or n >= 2:
                    act.wait_ge(S["u_used"], n - 1)
                act.activation(sg[:, c, :], PS[:, 4, :], ACT.Silu).then_inc(S["silu_done"], 1)

            def round_hidden(n, c):
                act.wait_ge(S["c_used"], n + 1)
                if not isinstance(n, int) or n >= 2:
                    act.wait_ge(S["down_done"], n - 1)
                act.activation(hid_hi[:, c, :], hid[:, c, :], ACT.Copy).then_inc(S["hid_rounded"], 1)

            for c in range(NCH):
                silu(c, c)
                round_hidden(c, c)
            with act.Fori(1, NF) as j:
                for c in range(NCH):
                    silu(NCH * j + c, c)
                    round_hidden(NCH * j + c, c)

        @block.tensor
        def _(pe):
            pe.wait_ge(S["gat_w_loaded"], 16 * 8)
            for k in range(KD):
                pe.matmul(PS[0:CF, 0, 0:2 * GH], w0r_sb[:, k, :], a0_sb[:, k, :], start=(k == 0), stop=(k == KD - 1))
            for f in range(KD):
                for k in range(KD):
                    mm = pe.matmul(PS[:, 1 + f, 0:2 * GH], w1r_sb[:, k, f * P:(f + 1) * P], a1_sb[:, k, :],
                                   start=(k == 0), stop=(k == KD - 1))
            mm.then_inc(S["gat_fold_ps"], 1)
            pe.wait_ge(S["sel_ready"], 3)
            pe.wait_ge(S["gat_w_ready"], 1)
            pe.wait_ge(S["att_w_loaded"], 64)

            def project(i, first):
                pe.wait_ge(S["xT_loaded"], 16 * (i + 1))
                if not first:
                    pe.wait_ge(S["y_used"], i)
                for t in range(NT):
                    for k in range(KD):
                        pe.matmul(PS[:, 2 * t, :], xT_sb[:, k, t * P:(t + 1) * P], wqkv_sb[:, k, 0:2 * D],
                                  start=(k == 0), stop=(k == KD - 1))
                    for k in range(KD):
                        mm = pe.matmul(PS[:, 2 * t + 1, 0:D], xT_sb[:, k, t * P:(t + 1) * P],
                                       wqkv_sb[:, k, 2 * D:3 * D], start=(k == 0), stop=(k == KD - 1))
                    mm.then_inc(S["qkv_ready"], 1)

            def turn_qk(i, t):
                if t == 0:
                    pe.wait_ge(S["v_ready"], NT * (i + 1))
                for which, ready, src in ((0, "q3_ready", q3), (1, "k3_ready", k3)):
                    pe.wait_ge(S[ready], NT * i + t + 1)
                    for half in range(2):
                        n = 4 * t + 2 * which + half
                        if n >= 4:
                            pe.wait_ge(S["qkT_ready"], 8 * i + n - 3)
                        for a in range(4):
                            c0 = (4 * half + a) * P
                            mm = pe.transpose(PS[:, n % 4, a * P:(a + 1) * P], src[:, t, c0:c0 + P].bitcast(f32), identf[:])
                        mm.then_inc(S["qkT_ps"], 1)

            def scores(i, u):
                if u == 0:
                    pe.wait_ge(S["qkT_ready"], 8 * (i + 1))
                if u >= 2:
                    pe.wait_ge(S["smax_done"], 8 * i + u - 1)
                for r in range(2):
                    pe.matmul(PS[:, 2 * (u % 2) + r, 0:CAUSAL], identb[:], maskq[:], start=True, stop=False,
                              skip_group_check=True)
                for r in range(2):
                    bank = 2 * (u % 2) + r
                    rows = slice(SLOT * r, SLOT * r + 3 * DH)
                    pe.matmul(PS[:, bank, 0:P], q3T[rows, u, 0:P], k3T[rows, u, 0:P],
                              start=False, stop=False, skip_group_check=True)
                    mm = pe.matmul(PS[:, bank, P:CAUSAL], q3T[rows, u, P:T], k3T[rows, u, :],
                                   start=False, stop=True, skip_group_check=True)
                mm.then_inc(S["s_ready"], 1)

            def turn_maxima(i):
                pe.wait_ge(S["negm_ready"], i + 1)
                for t in range(NT):
                    mm = pe.transpose(PS[0:2 * NH, 0, t * P:(t + 1) * P], negm2[:, t, :].bitcast(f32), identf[:])
                mm.then_inc(S["negmT_ps"], 1)

            def scoresT(i, a):
                if a == 0:
                    pe.wait_ge(S["negmT_ready"], i + 1)
                else:
                    pe.wait_ge(S["exp_done"], NH * i + 2 * a)
                for r in range(2):
                    pe.matmul(PS[:, r, 0:CAUSAL], identb[:], maskk[:], start=True, stop=False, skip_group_check=True)
                    pe.matmul(PS[:, r, 0:CAUSAL], selh[:, 2 * a + r, :], negmT[:], start=False, stop=False,
                              skip_group_check=True)
                for r in range(2):
                    rows = slice(SLOT * r, SLOT * r + 3 * DH)
                    pe.matmul(PS[:, r, 0:T], k3T[rows, a, 0:P], q3T[rows, a, :], start=False, stop=False,
                              skip_group_check=True)
                    pe.matmul(PS[:, r, T:CAUSAL], k3T[rows, a, P:T], q3T[rows, a, P:T], start=False, stop=True,
                              skip_group_check=True).then_inc(S["st_ready"], 1)

            def weigh_values(i, a):
                pe.wait_ge(S["exp_done"], NH * i + 2 * a + 2)
                for keys in range(NT):
                    for r in range(2):
                        h = 2 * a + r
                        rows, bank, c0 = slice(VS * (h % 4), VS * (h % 4 + 1)), 2 + h // 8, (h // 4) % 2 * T
                        queries = slice(0, T) if keys == 0 else slice(T, CAUSAL)
                        mm = pe.matmul(PS[rows, bank, c0 + keys * P:c0 + T], vaug[:, keys, h, :],
                                       pT[:, h % PTS, queries], start=(keys == 0), stop=(keys == NT - 1),
                                       skip_group_check=True)
                mm.then_inc(S["pv_done"], 1)

            def turn_sums(i):
                pe.wait_ge(S["sums_copied"], 2 * (i + 1))
                pe.wait_ge(S["exp_done"], NH * (i + 1))
                for t in range(NT):
                    for f in range(NH // 4):
                        c0 = (f % 2) * T + t * P
                        mm = pe.transpose(PS[:, t, f * P:(f + 1) * P], sums[:, f // 2, c0:c0 + P], identf[:])
                mm.then_inc(S["sums_ps"], 1)

            def output_projection(i):
                pe.wait_ge(S["on_ready"], i + 1)
                for t in range(NT):
                    for k in range(KD):
                        mm = pe.transpose(PS[:, 2, k * T + t * P:k * T + (t + 1) * P],
                                          o_sb[:, t, k * P:(k + 1) * P], identf[:])
                mm.then_inc(S["oT_ps"], 1)
                pe.wait_ge(S["oT_ready"], i + 1)
                for t in range(NT):
                    for k in range(KD):
                        mm = pe.matmul(PS[:, 3, t * D:(t + 1) * D], oT[:, k, t * P:(t + 1) * P], wo_sb[:, k, :],
                                       start=(k == 0), stop=(k == KD - 1))
                mm.then_inc(S["y_ready"], 1)

            def node_features(g, layer):
                if layer == 0:
                    pe.wait_ge(S["ctx_split"], 2 * (g + 1))
                    terms = [(ctx_hi, w0h, None), (ctx_lo, w0h, None), (ctx_hi, w0l, None)]
                else:
                    pe.wait_ge(S["ghT_ready"], 2 * g + 1)
                    terms = [(a, w, k) for k in range(KD) for a, w in ((ghT_hi, w1h), (ghT_lo, w1h), (ghT_hi, w1l))]
                for t in range(NT):
                    for n, (a, w, k) in enumerate(terms):
                        cols = slice(t * P, (t + 1) * P)
                        mm = pe.matmul(PS[:, 4 + t, 0:WC], a[:, cols] if k is None else a[:, k, cols],
                                       w[:] if k is None else w[:, k, :], start=(n == 0), stop=(n == len(terms) - 1))
                mm.then_inc(S["feat_ps"], 1)

            def turn_node_scores(g, layer):
                if layer == 0 and not (isinstance(g, int) and g == 0):
                    pe.wait_ge(S["logit_copied"], g)
                pe.wait_ge(S["st2_ready"], 2 * g + layer + 1)
                for which in range(2):
                    for t in range(NT):
                        c0 = which * T + t * P
                        mm = pe.transpose(PS[0:2 * GH, 6, c0:c0 + P], st2[:, t, which, :].bitcast(f32), identf[:])
                mm.then_inc(S["stT_ps"], 1)

            def pair_scores(g, layer, u):
                t, n, bank, h0 = u // (GH // 2), NU * layer + u, 4 + u % 2, 2 * (u % (GH // 2))
                if u == 0:
                    pe.wait_ge(S["stT_ready"], 2 * g + layer + 1)
                    pe.wait_ge(S["feat_ready"], 2 * g + layer + 1)
                if u >= 2:
                    pe.wait_ge(S["lr_done"], 2 * NU * g + n - 1)
                pe.matmul(PS[:, bank, :], stT[:, 0, t * P:(t + 1) * P], onehot[:, h0:h0 + 2, :],
                          start=True, stop=False, skip_group_check=True)
                for r in range(2):
                    mm = pe.matmul(PS[:, bank, r * T:(r + 1) * T], onehot[:, h0 + r, 0:P], stT[:, 1, :],
                                   start=False, stop=(r == 1), skip_group_check=True)
                mm.then_inc(S["z_ready"], 1)

            def turn_alpha(g, layer, u):
                n = NU * layer + u
                pe.wait_ge(S["alpha_ready"], 2 * NU * g + n + 1)
                if n:
                    pe.wait_ge(S["aT_done"], 2 * NU * g + n)
                for a in range(4):
                    m = a % 2
                    mm = pe.transpose(PS[:, 6, a * P:(a + 1) * P], al[:, n % ALS, a // 2, m * P:(m + 1) * P], identf[:])
                mm.then_inc(S["aT_ps"], 1)

            def weigh_features(g, layer, u):
                t, n = u // (GH // 2), NU * layer + u
                pe.wait_ge(S["aT_done"], 2 * NU * g + n + 1)
                for m in range(2):
                    for r in range(2):
                        h = 2 * (u % (GH // 2)) + r
                        rows, c0 = slice(GO * (h % 4), GO * (h % 4 + 1)), (t * 2 + h // 4) * P
                        mm = pe.matmul(PS[rows, 7, c0:c0 + P], feat[:, m, h, :], aT[:, n % ATS, 2 * r + m, :],
                                       start=(m == 0), stop=(m == 1), skip_group_check=True)
                mm.then_inc(S["gpv_done"], 1)

            def turn_features(g, layer):
                pe.wait_ge(S["gsums_copied"], 2 * g + layer + 1)
                for a in range(4):
                    mm = pe.transpose(PS[:, 6, a * P:(a + 1) * P], gy[:, a // 2, (a % 2) * P:(a % 2 + 1) * P], identf[:])
                mm.then_inc(S["gsums_ps"], 1)

            def router_logits(g):
                pe.wait_ge(S["ghT_ready"], 2 * g + 2)
                n = 0
                for k in range(KD):
                    for a, w in ((x2T_hi, gw_hi), (x2T_lo, gw_hi), (x2T_hi, gw_lo)):
                        mm = pe.matmul(PS[0:NGP, 6, 0:T], w[:, k, :], a[:, k, bass.ts(g, T)],
                                       start=(n == 0), stop=(n == 3 * KD - 1))
                        n += 1
                mm.then_inc(S["logit_ps"], 1)

            def turn_layer_out(g, layer):
                pe.wait_ge(S["gh_ready"], 2 * g + layer + 1)
                for t in range(NT):
                    for k in range(KD):
                        mm = pe.transpose(PS[:, 6, k * T + t * P:k * T + (t + 1) * P],
                                          (gh, x2b)[layer][:, t, k * P:(k + 1) * P], identf[:])
                mm.then_inc(S["ghT_ps"], 1)

            def both(g, i, first=False):
                gat, att = g is not None, i is not None
                if gat:
                    node_features(g, 0)
                if att:
                    project(i, first)
                for layer in range(2):
                    if gat:
                        turn_node_scores(g, layer)
                        pair_scores(g, layer, 0)
                        pair_scores(g, layer, 1)
                    if att and layer == 1:
                        turn_maxima(i)
                    for s in range(NU + 1):
                        if gat and s < NU:
                            if s + 2 < NU:
                                pair_scores(g, layer, s + 2)
                            turn_alpha(g, layer, s)
                        if att and layer == 0:
                            if s in (0, 1):
                                turn_qk(i, s)
                            elif s in (3, 4, 5, 6, 7):
                                scores(i, s - 3)
                        if att and layer == 1:
                            if s < NU:
                                scoresT(i, s)
                            if s:
                                weigh_values(i, s - 1)
                        if gat and s:
                            weigh_features(g, layer, s - 1)
                    if att and layer == 0:
                        for u in range(5, 8):
                            scores(i, u)
                    if att and layer == 1:
                        turn_sums(i)
                    if gat:
                        turn_features(g, layer)
                    if att and layer == 1:
                        output_projection(i)
                    if gat:
                        turn_layer_out(g, layer)
                        if layer == 0:
                            node_features(g, 1)
                        else:
                            router_logits(g)

            both(None, 0, first=True)
            with pe.Fori(0, B - 1) as g:
                both(g, g + 1)
            both(B - 1, None)

            pe.wait_ge(S["logit_copied"], B)
            for t in range(NTT):
                mm = pe.transpose(PS[:, 7, t * NGP:(t + 1) * NGP], logitsT[:, t * P:(t + 1) * P],
                                  identf[0:NGP, 0:NGP])
            mm.then_inc(S["logits_turned"], 1)
            pe.wait_ge(S["comb_ready"], 1)
            for t in range(NTT):
                mm = pe.transpose(PS[0:3 * NG, 7, t * SLOT:(t + 1) * SLOT].bitcast(bf16),
                                  combp[:, t, 0:3 * NG], identb[:])
            mm.then_inc(S["combT_ps"], 1)

            def gate_up(n, slot, c, fresh=False):
                for which, bank, used, ready in ((0, 4, "silu_done", "g_ready"), (1, 5, "u_used", "u_ready")):
                    if not fresh:
                        pe.wait_ge(S[used], n)
                    s = 0
                    for k in range(KD):
                        w0 = (2 * which + k) * P
                        for w, a in ((whi, x2T_hi), (whi, x2T_lo), (wlo, x2T_hi)):
                            mm = pe.matmul(PS[:, bank, :], w[:, slot, w0:w0 + P],
                                           a[:, k, c * CHUNK:(c + 1) * CHUNK], start=(s == 0), stop=(s == 3 * KD - 1))
                            s += 1
                    mm.then_inc(S[ready], 1)
                if fresh:
                    pe.wait_ge(S["combT_ready"], 1)
                else:
                    pe.wait_ge(S["c_used"], n)
                pe.matmul(PS[:, 6, :], gsel[:, slot, :], combT[:, c * CHUNK:(c + 1) * CHUNK],
                          start=True, stop=True).then_inc(S["c_ready"], 1)

            def down(n, tile, slot, c, first=False, last=False):
                pe.wait_ge(S["hid_ready"], n + 1)
                if c == 0:
                    pe.wait_ge(S["wd_split"], tile + 1)
                for t in range(CHUNK // P):
                    bank, cols = 2 * c + t // 2, slice((t % 2) * D, (t % 2 + 1) * D)
                    for s, (a, w) in enumerate(((hid_hi, whi), (hid_lo, whi), (hid_hi, wlo))):
                        mm = pe.matmul(PS[:, bank, cols], a[:, c, t * P:(t + 1) * P], w[:, slot, 4 * P:WJ],
                                       start=(first and s == 0 and t % 2 == 0), stop=(last and s == 2),
                                       skip_group_check=True)
                mm.then_inc(S["down_done"], 1)

            pe.wait_ge(S["w_split"], 1)
            gate_up(0, 0, 0, fresh=True)
            gate_up(1, 0, 1)
            down(0, 0, 0, 0, first=True)
            pe.wait_ge(S["w_split"], 2)
            gate_up(2, 1, 0)
            down(1, 0, 0, 1, first=True)
            with pe.Fori(0, NF // 2 - 1) as m:
                for o in range(2):
                    j = 2 * m + 1 + o
                    slot, after = (1 + o) % 2, o % 2
                    gate_up(NCH * j + 1, slot, 1)
                    down(NCH * j, j, slot, 0)
                    pe.wait_ge(S["w_split"], j + 2)
                    gate_up(NCH * j + 2, after, 0)
                    down(NCH * j + 1, j, slot, 1)
            n = NCH * (NF - 1)
            gate_up(n + 1, 1, 1)
            down(n, NF - 1, 1, 0, last=True)
            down(n + 1, NF - 1, 1, 1, last=True)

        @block.vector
        def _(dve):
            dve.wait_ge(S["gat_fold_ps"], 1)
            setup = Steps(dve, S["setup_step"])
            setup.mark(dve.tensor_copy(w0c[:, D:WC], PS[0:CF, 0, 0:2 * GH]))
            setup.mark(dve.tensor_copy(w1c[:, :, D:WC], PS[:, 1:1 + KD, 0:2 * GH]))
            setup.wait()
            setup.mark(dve.tensor_copy(w0h[:], w0c[:]))
            setup.mark(dve.tensor_copy(w1h[:], w1c[:]))
            dve.wait_ge(S["router_w_loaded"], 16)
            setup.mark(dve.tensor_copy(gw_hi[:], gw_sb[:]))
            setup.wait()
            dve.tensor_tensor(w0l[:], w0c[:], w0h[:].bitcast(f32), ALU.subtract)
            dve.tensor_tensor(gw_lo[:], gw_sb[:], gw_hi[:].bitcast(f32), ALU.subtract)
            dve.tensor_tensor(w1l[:], w1c[:], w1h[:].bitcast(f32), ALU.subtract).then_inc(S["gat_w_ready"], 1)
            dve.wait_ge(S["setup_zero"], 6)
            dve.wait_ge(S["att_w_loaded"], 64)
            dve.wait_ge(S["consts_loaded"], 16 * 7)

            def add_biases(i):
                for t in range(NT):
                    dve.wait_ge(S["qkv_ready"], NT * i + t + 1)
                    dve.tensor_tensor(qk[:, t, :], PS[:, 2 * t, :], bqkv_sb[:, 0:2 * D],
                                      ALU.add).then_inc(S["qk_biased"], 1)
                    dve.tensor_tensor(vaug[:, t, :, 0:DH],
                                      PS[:, 2 * t + 1, 0:D].rearrange("p (h d) -> p h d", d=DH),
                                      bqkv_sb[:, 2 * D:3 * D].rearrange("p (h d) -> p h d", d=DH),
                                      ALU.add).then_inc(S["v_ready"], 1)

            def rotate(i, t, chain):
                dve.wait_ge(S["qk_biased"], NT * i + t + 1)
                cosines = rope_sb[:, t, 0, :].unsqueeze(1).broadcast_to([P, 2 * NH, DH])
                chain.link(dve.tensor_tensor(t1[:, t, :].rearrange("p (h d) -> p h d", d=DH),
                                             qk[:, t, :].rearrange("p (h d) -> p h d", d=DH),
                                             cosines, ALU.mult))
                dve.wait_ge(S["t2_ready"], NT * i + t + 1)
                c = t1[:, t, :].rearrange("p (h f e) -> p h f e", e=2, f=DH // 2)
                s = t2[:, t, :].rearrange("p (h f e) -> p h f e", e=2, f=DH // 2)
                dve.tensor_tensor(rot[:, t, :, 0:DH // 2], c[:, :, :, 0], s[:, :, :, 1], ALU.add)
                dve.tensor_tensor(rot[:, t, :, DH // 2:DH], c[:, :, :, 1], s[:, :, :, 0],
                                  ALU.add).then_inc(S["rot_ready"], 1)
                dve.wait_ge(S["rot_ready"], NT * i + t + 1)
                qv = q3[:, t, :].rearrange("p (h s) -> p h s", s=SLOT)
                src = rot[:, t, 0:NH, :]
                dve.tensor_copy(qv[:, :, 2 * DH:3 * DH], src)
                chain.link(dve.tensor_copy(qv[:, :, 0:DH], src))
                dve.tensor_tensor(qv[:, :, DH:2 * DH], src, qv[:, :, 0:DH].bitcast(f32),
                                  ALU.subtract).then_inc(S["q3_ready"], 1)

            def row_maxima(i, u):
                dve.wait_ge(S["s_ready"], 8 * i + u + 1)
                b = 2 * (u % 2)
                dve.tensor_reduce(negm[:, 0, 2 * u:2 * u + 2], PS[:, b:b + 2, 0:P], AX.X, ALU.max, negate=True)
                dve.tensor_reduce(negm[:, 1, 2 * u:2 * u + 2], PS[:, b:b + 2, P:CAUSAL], AX.X, ALU.max,
                                  negate=True).then_inc(S["smax_done"], 1)

            def split_maxima(i, chain):
                dve.wait_ge(S["smax_done"], 8 * (i + 1))
                chain.link(dve.tensor_copy(negm2[:, :, 0:NH], negm[:]))
                dve.tensor_tensor(negm2[:, :, NH:2 * NH], negm[:], negm2[:, :, 0:NH].bitcast(f32),
                                  ALU.subtract).then_inc(S["negm_ready"], 1)

            def turned_maxima(i):
                dve.wait_ge(S["negmT_ps"], i + 1)
                dve.tensor_copy(negmT[:, 0:T], PS[0:2 * NH, 0, 0:T])
                dve.tensor_copy(negmT[:, T:CAUSAL], PS[0:2 * NH, 0, P:T]).then_inc(S["negmT_ready"], 1)

            def attention_over_sums(i, chain):
                dve.wait_ge(S["sums_ps"], i + 1)
                o_ps = PS[:, 0:2, :].rearrange("p t (h d) -> p t h d", d=VS)
                chain.link(dve.reciprocal(orec[:], o_ps[:, :, :, DH]))
                dve.tensor_tensor(o_sb[:].rearrange("p t (h d) -> p t h d", d=DH), o_ps[:, :, :, 0:DH],
                                  orec[:].unsqueeze(3).broadcast_to([P, NT, NH, DH]), ALU.mult).then_inc(S["on_ready"], 1)

            def first_residual(i):
                dve.wait_ge(S["y_ready"], i + 1)
                dve.wait_ge(S["xb_ready"], i + 1)
                dve.tensor_tensor(resid1[:], PS[:, 3, :].rearrange("p (t d) -> p t d", t=NT), xb[:],
                                  ALU.add).then_inc(S["y_used"], 1)

            def moments(resid, chain):
                for t in range(NT):
                    chain.mark(dve.bn_stats(stats[:, t, :], resid[:, t, :]))
                chain.wait()
                dve.tensor_tensor(idle_v[:], mhalf[:, 0:1], mhalf[:, 0:1], ALU.mult)
                for t in range(NT):
                    chain.mark(dve.bn_aggr(meanvar[:, t, :], stats[:, t, :]))
                chain.wait()
                dve.tensor_scalar(vareps[:], meanvar[:, :, 1], EPS, None, ALU.add).then_inc(S["var_ready"], 1)

            def normed(g, n, resid, target):
                dve.wait_ge(S["rstd_ready"], 2 * g + n + 1)
                for t in range(NT):
                    ins = dve.tensor_scalar(target[:, t, :], resid[:, t, :], meanvar[:, t, 0:1], rstd[:, t:t + 1],
                                            ALU.subtract, ALU.mult)
                return ins

            def split_scores(g, layer, chain):
                dve.wait_ge(S["feat_ps"], 2 * g + layer + 1)
                src = PS[:, 4:6, D:WC].rearrange("p t (w h) -> p t w h", h=GH)
                chain.link(dve.tensor_scalar(st2[:, :, :, 0:GH], src, -1.0, None, ALU.mult))
                dve.scalar_tensor_tensor(st2[:, :, :, GH:2 * GH], src, -1.0, st2[:, :, :, 0:GH].bitcast(f32),
                                         ALU.mult, ALU.subtract).then_inc(S["st2_ready"], 1)

            def turned_node_scores(g, layer):
                dve.wait_ge(S["stT_ps"], 2 * g + layer + 1)
                dve.tensor_copy(stT[:], PS[0:2 * GH, 6, :].rearrange("p (w n) -> p w n", w=2)).then_inc(
                    S["stT_ready"], 1)

            def mask_and_min(g, layer, u):
                t, n = u // (GH // 2), NU * layer + u
                a = al[:, n % ALS, :, :]
                dve.wait_ge(S["y_copied"], 2 * NU * g + n + 1)
                dve.tensor_tensor(a, PS[:, 4 + u % 2, :].rearrange("p (h m) -> p h m", m=T), a,
                                  ALU.min).then_inc(S["lr_done"], 1)
                dve.wait_ge(S["lr_done"], 2 * NU * g + n + 1)
                dve.tensor_tensor(idle_v[:], mhalf[:, 0:1], mhalf[:, 0:1], ALU.mult)
                for r in range(2):
                    ins = dve.tensor_tensor_reduce(out=a[:, r, :], in0=a[:, r, :], in1=mk[:, t, :], scale=1.0,
                                                   scalar=3.4e38, op0=ALU.add, op1=ALU.min,
                                                   accum_out=gmin[:, 2 * u + r:2 * u + r + 1])
                ins.then_inc(S["v_masked"], 1)

            def bias_and_elu(g, layer, chain):
                dve.wait_ge(S["gsums_ps"], 2 * g + layer + 1)
                chain.link(dve.reciprocal(grec[:], gsum[:]))
                chain.link(dve.tensor_tensor(gy[:].rearrange("p t (h o) -> p t h o", o=GO),
                                             PS[:, 6, :].rearrange("p (t h o) -> p t h o", t=NT, o=GO),
                                             grec[:].unsqueeze(3).broadcast_to([P, NT, GH, GO]), ALU.mult))
                chain.link(dve.tensor_tensor(gy[:], gy[:], b01[:, layer, :].unsqueeze(1).broadcast_to([P, NT, D]),
                                             ALU.add))
                dve.tensor_scalar(gpos[:], gy[:], 0.0, None, ALU.max)
                dve.tensor_scalar(gneg[:], gy[:], 0.0, None, ALU.min).then_inc(S["gneg_ready"], 1)

            def layer_out(g, layer, chain):
                dve.wait_ge(S["gexp_ready"], 2 * g + layer + 1)
                ins = dve.scalar_tensor_tensor(gh[:], gneg[:], -1.0, gpos[:], ALU.add, ALU.add)
                if layer == 0:
                    ins.then_inc(S["gh_ready"], 1)
                else:
                    chain.link(ins)
                    chain.link(dve.tensor_tensor(resid2[:], gh[:], x1[:], ALU.add))
                    moments(resid2, chain)
                    normed(g, 1, resid2, x2b).then_inc(S["gh_ready"], 1)

            def turned_layer_out(g, layer, chain):
                dve.wait_ge(S["ghT_ps"], 2 * g + layer + 1)
                src = PS[:, 6, :].rearrange("p (k n) -> p k n", k=KD)
                if layer == 0:
                    hi, lo = ghT_hi[:], ghT_lo[:]
                else:
                    hi, lo = x2T_hi[:, :, bass.ts(g, T)], x2T_lo[:, :, bass.ts(g, T)]
                chain.link(dve.tensor_copy(hi, src))
                dve.tensor_tensor(lo, src, hi.bitcast(f32), ALU.subtract).then_inc(S["ghT_ready"], 1)

            def both(g, i):
                gat, att = g is not None, i is not None
                ac = Steps(dve, S["att_step"], ATT_STEPS * i) if att else None
                gc = Steps(dve, S["gat_step"], GAT_STEPS * g) if gat else None
                if gat:
                    dve.wait_ge(S["y_used"], g + 1)
                    moments(resid1, gc)
                    split_scores(g, 0, gc)
                if att:
                    add_biases(i)
                if gat:
                    gc.link(normed(g, 0, resid1, x1))
                    gc.link(dve.tensor_scalar(mk[:], x1[:], 1.0, -MASK_SCALE, ALU.subtract, ALU.mult))
                for layer in range(2):
                    if gat:
                        if layer == 1:
                            split_scores(g, 1, gc)
                        turned_node_scores(g, layer)
                    if att and layer == 1:
                        turned_maxima(i)
                    for s in range(NU):
                        if gat:
                            mask_and_min(g, layer, s)
                        if att and layer == 0:
                            if s in (0, 1):
                                rotate(i, s, ac)
                            elif s >= 4:
                                row_maxima(i, s - 4)
                    if att and layer == 0:
                        for u in range(4, 8):
                            row_maxima(i, u)
                        split_maxima(i, ac)
                    if gat and layer == 0:
                        bias_and_elu(g, 0, gc)
                        layer_out(g, 0, gc)
                        turned_layer_out(g, 0, gc)
                if att:
                    attention_over_sums(i, ac)
                if gat:
                    bias_and_elu(g, 1, gc)
                if att:
                    first_residual(i)
                if gat:
                    layer_out(g, 1, gc)
                    turned_layer_out(g, 1, gc)
                assert not att or ac.n == ATT_STEPS, ac.n
                assert not gat or gc.n == GAT_STEPS, gc.n

            both(None, 0)
            with dve.Fori(0, B - 1) as g:
                both(g, g + 1)
            both(B - 1, None)

            r = Steps(dve, S["setup_step"], 0)
            r.n = setup.n
            dve.wait_ge(S["logits_turned"], 1)
            routed = PS[:, 7, 0:NTT * NGP].rearrange("p (t g) -> p t g", g=NGP)[:, :, 0:NE]
            r.link(dve.tensor_reduce(r_s[:], routed, AX.X, ALU.max))
            wide = lambda a: a.unsqueeze(2).broadcast_to([P, NTT, NE])
            dve.tensor_tensor(r_a[:], routed, wide(r_s[:]), ALU.subtract).then_inc(S["gate_centered"], 1)
            dve.wait_ge(S["gate_exp"], 2)
            r.link(dve.tensor_reduce(r_s[:], r_b[:], AX.X, ALU.add))
            r.link(dve.reciprocal(r_s[:], r_s[:]))
            r.link(dve.tensor_tensor(r_a[:], r_b[:], wide(r_s[:]), ALU.mult))
            for t in range(NTT):
                ins = dve.max(top8[:, t, :], r_a[:, t, :])
            r.link(ins)
            fourth = top8[:, :, TOPK - 1]
            r.mark(dve.tensor_tensor(r_b[:], r_a[:], wide(fourth), ALU.is_gt))
            r.mark(dve.tensor_tensor(r_c[:], r_a[:], wide(fourth), ALU.is_equal))
            r.wait()
            r.link(dve.tensor_reduce(r_s[:], r_b[:], AX.X, ALU.add))
            r.link(dve.tensor_scalar(r_s[:], r_s[:], -1.0, float(TOPK), ALU.mult, ALU.add))
            rank = comb[:].rearrange("p t g -> p (t g)")[:, 0:NTT * NE]
            r.link(dve.tensor_tensor_scan(rank, reset_sb[:], r_c[:].rearrange("p t g -> p (t g)"), 0.0,
                                          ALU.mult, ALU.add))
            rank3 = rank.rearrange("p (t g) -> p t g", g=NE)
            r.link(dve.tensor_tensor(rank3, rank3, wide(r_s[:]), ALU.is_le))
            r.link(dve.tensor_tensor(r_c[:], r_c[:], rank3, ALU.mult))
            r.link(dve.tensor_tensor(r_b[:], r_b[:], r_c[:], ALU.add))
            r.link(dve.tensor_tensor(r_b[:], r_b[:], r_a[:], ALU.mult))
            r.link(dve.tensor_reduce(r_s[:], r_b[:], AX.X, ALU.add))
            r.link(dve.reciprocal(r_s[:], r_s[:]))
            r.mark(dve.tensor_tensor(comb[:, :, 0:NE], r_b[:], wide(r_s[:]), ALU.mult))
            r.link(dve.tensor_scalar(r_t[:], r_t[:], 1.0, None, ALU.add))
            r.link(dve.reciprocal(comb[:, :, NE], r_t[:]))
            for part in range(3):
                dst = combp[:, :, part * NG:(part + 1) * NG]
                ins = dve.tensor_copy(dst, comb[:])
                if part < 2:
                    r.link(ins)
                    r.link(dve.tensor_tensor(comb[:], comb[:], dst, ALU.subtract))
            ins.then_inc(S["comb_ready"], 1)
            dve.wait_ge(S["combT_ps"], 1)
            dve.tensor_copy(combT[:], PS[0:3 * NG, 7, :].bitcast(bf16)).then_inc(S["combT_ready"], 1)

            def hidden(n, c, fresh=False):
                dve.wait_ge(S["silu_done"], n + 1)
                dve.wait_ge(S["u_ready"], n + 1)
                dve.tensor_tensor(hu[:, c, :], PS[:, 5, :], sg[:, c, :], ALU.mult).then_inc(S["u_used"], 1)
                dve.wait_ge(S["u_used"], n + 1)
                dve.wait_ge(S["c_ready"], n + 1)
                dve.tensor_tensor(hid[:, c, :], PS[:, 6, :], hu[:, c, :], ALU.mult).then_inc(S["c_used"], 1)
                if not fresh:
                    dve.wait_ge(S["down_done"], n - 1)
                dve.wait_ge(S["hid_rounded"], n + 1)
                dve.tensor_tensor(hid_lo[:, c, :], hid[:, c, :], hid_hi[:, c, :].bitcast(f32),
                                  ALU.subtract).then_inc(S["hid_ready"], 1)

            for c in range(NCH):
                hidden(c, c, fresh=True)
            with dve.Fori(1, NF) as j:
                for c in range(NCH):
                    hidden(NCH * j + c, c)

            dve.wait_ge(S["down_done"], NCH * NF)
            dve.wait_ge(S["x2_stored"], B)
            f = r
            for b in range(4):
                f.mark(dve.tensor_tensor(res3[:, 2 * b:2 * b + 2, :], PS[:, b, :].rearrange("p (t d) -> p t d", d=D),
                                         x2[:, 2 * b:2 * b + 2, :], ALU.add))
            f.wait()
            for t in range(NTT):
                f.mark(dve.bn_stats(stats3[:, t, :], res3[:, t, :]))
            f.wait()
            for t in range(NTT):
                f.mark(dve.bn_aggr(mv3[:, t, :], stats3[:, t, :]))
            f.wait()
            dve.tensor_scalar(ve3[:], mv3[:, :, 1], EPS, None, ALU.add).then_inc(S["var3_ready"], 1)
            dve.wait_ge(S["rstd3_ready"], 1)
            for t in range(NTT):
                dve.tensor_scalar(y3[:, t, :], res3[:, t, :], mv3[:, t, 0:1], rstd3[:, t:t + 1],
                                  ALU.subtract, ALU.mult).then_inc(S["out_ready"], 1)


def layouts(np, a):
    c = np.ascontiguousarray

    def rows(w):
        return c(w.reshape(-1, P, w.shape[-1]).transpose(1, 0, 2))

    x, con = a["x"], a["ctx_512"]
    out = {
        "xT": c(x.transpose(0, 2, 1).reshape(B, KD, P, T).transpose(0, 2, 1, 3)),
        "x": c(x.reshape(B, NT, P, D).transpose(0, 2, 1, 3)),
        "ctxT": c(con.transpose(0, 2, 1)),
        "wqkvT": rows(a["L0_attn_w_qkv"].T),
        "bqkv": a["L0_attn_b_qkv"],
        "woT": rows(a["L0_attn_w_out"].T),
        "bo": a["L0_attn_b_out"],
    }
    for n in range(2):
        w = a[f"L0_xattn_W{n}"]
        fold = np.zeros((GH, GO, 2 * GH), np.float32)
        for h in range(GH):
            fold[h, :, h] = a[f"L0_xattn_a_self{n}"][h]
            fold[h, :, GH + h] = a[f"L0_xattn_a_neigh{n}"][h]
        flat = w.transpose(1, 0, 2).reshape(w.shape[1], D)
        out[f"W{n}f"] = c(flat) if n == 0 else rows(flat)
        out[f"W{n}r"] = rows(flat.T)
        out[f"A{n}"] = rows(fold.reshape(D, 2 * GH))
        out[f"b{n}"] = c(a[f"L0_xattn_b{n}"].reshape(D))
    router = np.zeros((D, NGP), np.float32)
    router[:, 0:NE] = a["L0_ffn_gate_w"].T
    router[:, NE] = a["L0_ffn_shared_expert_gate_w"][0]
    out["gwT"] = rows(router)
    hidden = NF * P
    wide = []
    for kind in ("gate", "up"):
        w = np.zeros((hidden, D), np.float32)
        w[0:NE * FE] = a[f"L0_ffn_expert_{kind}_w"].reshape(NE * FE, D)
        w[NE * FE:NE * FE + FS] = a[f"L0_ffn_shared_{kind}_w"]
        wide.append(w.reshape(NF, P, KD, P).transpose(0, 3, 2, 1).reshape(NF, P, KD * P))
    w = np.zeros((hidden, D), np.float32)
    w[0:NE * FE] = a["L0_ffn_expert_down_w"].transpose(0, 2, 1).reshape(NE * FE, D)
    w[NE * FE:NE * FE + FS] = a["L0_ffn_shared_down_w"].T
    wide.append(w.reshape(NF, P, D))
    out["ffnW"] = c(np.concatenate(wide, axis=2))
    return out


def constants(np, bf16):
    half = DH // 2
    freqs = np.float32(10000.0) ** (-np.arange(half, dtype=np.float32) / np.float32(half))
    theta = np.arange(T, dtype=np.float32)[:, None] * freqs[None, :]
    cos, sin = np.cos(theta), np.sin(theta)
    table = np.zeros((T, 2, half, 2), np.float32)
    table[:, 0, :, 0], table[:, 0, :, 1] = cos, cos
    table[:, 1, :, 0], table[:, 1, :, 1] = sin, -sin
    above = np.where(np.arange(P)[None, :] > np.arange(P)[:, None], NEG, 0.0)
    none = np.zeros((P, P))
    head = np.zeros((2, NH, NH, P), np.float32)
    node = np.zeros((2, GH, GH, T), np.float32)
    for h in range(NH):
        head[:, h, h] = 1.0
    for h in range(GH):
        node[:, h, h] = 1.0
    expert = np.minimum(np.arange(NF * P) // FE, NE)
    gates = np.zeros((3, NG, NF * P), np.float32)
    gates[:, expert, np.arange(NF * P)] = 1.0
    reset = np.ones((P, NTT, NE), np.float32)
    reset[:, :, 0] = 0.0
    return {
        "rope_cs": np.ascontiguousarray(table.reshape(NT, P, 2, DH).transpose(1, 0, 2, 3)),
        "causal_q": np.concatenate([above, none, above], axis=1).astype(bf16),
        "causal_k": np.concatenate([above.T, none, above.T], axis=1).astype(bf16),
        "ident": np.eye(P, dtype=np.float32),
        "head_sel": head.reshape(2 * NH, NH, P),
        "node_onehot": node.reshape(2 * GH, GH, T),
        "gate_sel": np.ascontiguousarray(gates.reshape(3 * NG, NF, P).transpose(1, 0, 2)).astype(bf16),
        "scan_reset": reset.reshape(P, NTT * NE),
    }


_ORDER = ["xT", "x", "ctxT", "wqkvT", "bqkv", "woT", "bo", "W0f", "W0r", "A0", "b0", "W1f", "W1r", "A1", "b1",
          "gwT", "ffnW", "rope_cs", "causal_q", "causal_k", "ident", "head_sel", "node_onehot", "gate_sel",
          "scan_reset"]


def kernel(**inputs):
    import numpy as np
    import ml_dtypes
    import concourse.bacc as bacc
    from concourse.bass_utils import run_bass_kernel_spmd

    given = {name: np.asarray(value) for name, value in inputs.items()}
    arrays = {**layouts(np, given), **constants(np, ml_dtypes.bfloat16)}
    nc = bacc.Bacc("TRN2", target_bir_lowering=False, num_devices=1)
    args, sent = [], {}
    for name in _ORDER:
        a = np.ascontiguousarray(arrays[name])
        sent[f"in_{name}"] = a
        args.append(nc.dram_tensor(f"in_{name}", a.shape, mybir.dt.from_np(a.dtype), kind="ExternalInput").ap())
    out = nc.dram_tensor("out_0", (NTT, P, D), mybir.dt.float32, kind="ExternalOutput").ap()
    decoder_layer(nc, *args, out)
    result = run_bass_kernel_spmd(nc, [sent], core_ids=[0])
    return result.results[0]["out_0"].reshape(B, T, D)
```

```python
import concourse.bass as bass
from concourse import mybir
from contextlib import ExitStack

B, T, D = 4, 256, 256
P = 128
NT = T // P
KD = D // P
NH, DH = 16, 16
SLOT = 64
VS = 32
CF, GH, GO = 64, 8, 32
NU = NT * GH // 2
PTS, ALS, ATS = 4, 4, 3
NE, FE, FS, TOPK = 16, 176, 704, 4
NG = NE + 1
NGP = NG + 1
NF = -(-(NE * FE + FS) // P)
NTT = B * NT
CHUNK = 512
NCH = B * T // CHUNK
EPS = 1e-5
NEG = -1e30
MASK_SCALE = 1e10
CAUSAL = P + T


class Steps:

    def __init__(self, eng, sem, base=0):
        self.eng, self.sem, self.base, self.n = eng, sem, base, 0

    def mark(self, ins):
        ins.then_inc(self.sem, 1)
        self.n += 1

    def wait(self):
        self.eng.wait_ge(self.sem, self.base + self.n)

    def link(self, ins):
        self.mark(ins)
        self.wait()


ATT_STEPS, GAT_STEPS = 6, 21


def decoder_layer(nc, xT, x, ctxT, wqkvT, bqkv, woT, bo, W0f, W0r, A0, b0, W1f, W1r, A1, b1,
                  gwT, ffnW, rope_cs, causal_q, causal_k, ident, head_sel, node_onehot, gate_sel,
                  scan_reset, out):
    f32, bf16, f32r = mybir.dt.float32, mybir.dt.bfloat16, mybir.dt.float32r
    ALU = mybir.AluOpType
    ACT = mybir.ActivationFunctionType
    AX = mybir.AxisListType

    ctx = ExitStack()
    with ctx:
        def sb(name, shape, dt=f32):
            return ctx.enter_context(nc.sbuf_tensor(name, shape, dt))

        def sem(name):
            return ctx.enter_context(nc.semaphore(name))

        PS = ctx.enter_context(nc.psum_tensor("PS", [P, 8, 512], f32))

        xT_sb = sb("xT_sb", [P, KD, T])
        xres = sb("xres", [P, NT, D])
        ctx_sb = sb("ctx_sb", [CF, T])
        ctx_hi = sb("ctx_hi", [CF, T], f32r)
        ctx_lo = sb("ctx_lo", [CF, T], f32r)
        wqkv_sb = sb("wqkv_sb", [P, KD, 3 * D])
        bqkv_sb = sb("bqkv_sb", [P, 3 * D])
        wo_sb = sb("wo_sb", [P, KD, D])
        bo_sb = sb("bo_sb", [P, D])
        rope_sb = sb("rope_sb", [P, NT, 2, DH])
        identf = sb("identf", [P, P])
        identb = sb("identb", [P, P], bf16)
        maskq = sb("maskq", [P, P], bf16)
        maskk = sb("maskk", [P, P], bf16)
        selh = sb("selh", [2 * NH, NH, P], f32r)
        onehot = sb("onehot", [2 * GH, GH, P], f32r)

        qk = sb("qk", [P, NT, 2 * D])
        t1 = sb("t1", [P, NT, 2 * D])
        t2 = sb("t2", [P, NT, 2 * D])
        rot = sb("rot", [P, NT, 2 * NH, DH])
        q3 = sb("q3", [P, NT, NH * SLOT], f32r)
        k3 = sb("k3", [P, NT, NH * SLOT], f32r)
        q3T = sb("q3T", [P, NH // 2, T], f32r)
        k3T = sb("k3T", [P, NH // 2, T], f32r)
        vaug = sb("vaug", [P, NT, NH, VS])
        negm = sb("negm", [P, NT, NH])
        negm2 = sb("negm2", [P, NT, 2 * NH], f32r)
        negmT = sb("negmT", [2 * NH, CAUSAL], f32r)
        pT = sb("pT", [P, PTS, CAUSAL])
        orec = sb("orec", [P, NT, NH])
        o_sb = sb("o_sb", [P, NT, D])
        oT = sb("oT", [P, KD, T])
        xb = sb("xb", [P, NT, D])

        resid1 = sb("resid1", [P, NT, D])
        resid2 = sb("resid2", [P, NT, D])
        stats = sb("stats", [P, NT, 6])
        meanvar = sb("meanvar", [P, NT, 2])
        vareps = sb("vareps", [P, NT])
        rstd = sb("rstd", [P, NT])
        mhalf = sb("mhalf", [P, NTT])

        idle_v, idle_p = sb("idle_v", [P, 1]), sb("idle_p", [P, 1])

        w0r_sb = sb("w0r_sb", [P, KD, CF])
        a0_sb = sb("a0_sb", [P, KD, 2 * GH])
        a1_sb = sb("a1_sb", [P, KD, 2 * GH])
        WC = D + 2 * GH
        w0c = sb("w0c", [CF, WC])
        w0h = sb("w0h", [CF, WC], f32r)
        w0l = sb("w0l", [CF, WC], f32r)
        w1c = sb("w1c", [P, KD, WC])
        w1h = sb("w1h", [P, KD, WC], f32r)
        w1l = sb("w1l", [P, KD, WC], f32r)
        b01 = sb("b01", [1, 2, D])
        bh = sb("bh", [1, 2, D], f32r)
        bl = sb("bl", [1, 2, D], f32r)
        x1 = sb("x1", [P, NT, D])
        mk = sb("mk", [P, NT, T])
        feat = sb("feat", [P, NT, GH, GO])
        nself = sb("nself", [P, NT, GH])
        nself02 = sb("nself02", [P, NT, GH])
        st2 = sb("st2", [P, NT, 2 * GH], f32r)
        stT = sb("stT", [2 * GH, T], f32r)
        al = sb("al", [P, ALS, 2, T])
        aT = sb("aT", [P, ATS, 4, P])
        gmin = sb("gmin", [P, NT * GH])
        gsum = sb("gsum", [P, NT, GH])
        gy = sb("gy", [P, NT, D])
        grec = sb("grec", [P, NT, GH])
        gneg = sb("gneg", [P, NT, D])
        gh = sb("gh", [P, NT, D])
        ghT_hi = sb("ghT_hi", [P, KD, T], f32r)
        ghT_lo = sb("ghT_lo", [P, KD, T], f32r)

        x2b = sb("x2b", [P, NT, D])
        x2 = sb("x2", [P, NTT, D])
        x2T_hi = sb("x2T_hi", [P, KD, B * T], f32r)
        x2T_lo = sb("x2T_lo", [P, KD, B * T], f32r)
        gw_sb = sb("gw_sb", [P, KD, NGP])
        gw_hi = sb("gw_hi", [P, KD, NGP], f32r)
        gw_lo = sb("gw_lo", [P, KD, NGP], f32r)
        reset_sb = sb("reset_sb", [P, NTT * NE])
        comb = sb("comb", [P, NTT, NG])
        logitsT = sb("logitsT", [NGP, B * T])
        r_a = sb("r_a", [P, NTT, NE])
        r_b = sb("r_b", [P, NTT, NE])
        r_c = sb("r_c", [P, NTT, NE])
        r_s = sb("r_s", [P, NTT])
        r_t = sb("r_t", [P, NTT])
        top8 = sb("top8", [P, NTT, 8])
        combp = sb("combp", [P, NTT, SLOT], bf16)
        combT = sb("combT", [3 * NG, B * T], bf16)
        WJ = 4 * P + D
        wraw = sb("wraw", [P, 2, WJ])
        gsel = sb("gsel", [3 * NG, 2, P], bf16)
        hid_hi = sb("hid_hi", [P, 2, CHUNK], f32r)
        hid_lo = sb("hid_lo", [P, 2, CHUNK], f32r)
        stats3 = sb("stats3", [P, NTT, 6])
        mv3 = sb("mv3", [P, NTT, 2])
        ve3 = sb("ve3", [P, NTT])
        rstd3 = sb("rstd3", [P, NTT])
        stage_h = al[0:2 * NH, :, :, :].rearrange("p a b c -> p (a b c)").rearrange("p (h c) -> p h c", c=P)
        stage_n = x2[0:2 * GH, 0:GH * P // D, :].rearrange("p a c -> p (a c)").rearrange("p (h c) -> p h c", c=P)
        w1r_sb = gneg
        whi = q3T[:, :, :].rearrange("p a b -> p (a b)")[:, 0:2 * WJ].rearrange("p (s w) -> p s w", s=2)
        wlo = k3T[:, :, :].rearrange("p a b -> p (a b)")[:, 0:2 * WJ].rearrange("p (s w) -> p s w", s=2)
        sg, hu, hid, sums = t1, t2, qk, t1
        res3 = q3[:, :, :].bitcast(f32).rearrange("p a (b d) -> p (a b) d", d=D)
        y3 = k3[:, :, :].bitcast(f32).rearrange("p a (b d) -> p (a b) d", d=D)

        names = """tables_loaded consts_loaded wqkv_loaded att_w_loaded gat_w_loaded router_w_loaded xT_loaded xres_loaded ctx_loaded
            setup_zero gat_fold_ps gat_w_ready identb_ready sel_ready ctx_split
            qkv_ready qk_biased v_ready t2_ready rot_ready q3_ready k3_hi k3_ready qkT_ps qkT_ready
            s_ready smax_done negm_ready negmT_ps negmT_ready st_ready exp_done pv_done sums_copied sums_ps on_ready oT_ps
            oT_ready xb_ready y_ready y_used var_ready rstd_ready
            feat_ps st2_ready feat_ready stT_ps stT_ready z_ready y_copied lr_done v_masked
            alpha_ready aT_ps aT_done gpv_done gsums_copied gsums_ps gneg_ready gexp_ready gh_ready ghT_ps ghT_ready
            x2_stored att_step gat_step head_step pool_step
            logit_ps logit_copied logits_turned gate_centered gate_exp comb_ready combT_ps combT_ready
            w_loaded0 w_loaded1 w_split wd_split g_ready u_ready c_ready silu_done u_used c_used hid_rounded hid_ready
            down_done var3_ready rstd3_ready out_ready out_stored setup_step""".split()
        S = {n: sem(n) for n in names}

        block = ctx.enter_context(nc.Block())

        @block.sync
        def _(sp):
            def load_batch(i):
                sp.wait_ge(S["qkv_ready"], NT * i)
                sp.dma_start(xT_sb[:], xT[i]).then_inc(S["xT_loaded"], 16)
                sp.wait_ge(S["ctx_split"], 2 * i)
                sp.dma_start(ctx_sb[:], ctxT[i]).then_inc(S["ctx_loaded"], 16)
                sp.wait_ge(S["xb_ready"], i)
                sp.dma_start(xres[:], x[i]).then_inc(S["xres_loaded"], 16)

            sp.dma_start(xT_sb[:], xT[0]).then_inc(S["xT_loaded"], 16)
            for dst, src in ((rope_sb[:], rope_cs), (identf[:], ident), (maskq[:], causal_q), (maskk[:], causal_k)):
                sp.dma_start(dst, src).then_inc(S["tables_loaded"], 16)
            for dst, src in ((stage_h, head_sel), (stage_n, node_onehot), (reset_sb[:], scan_reset)):
                sp.dma_start(dst, src).then_inc(S["consts_loaded"], 16)
            sp.dma_start(ctx_sb[:], ctxT[0]).then_inc(S["ctx_loaded"], 16)
            sp.dma_start(xres[:], x[0]).then_inc(S["xres_loaded"], 16)
            for dst, src in ((w1r_sb[:], W1r), (a1_sb[:], A1), (w1c[:, :, 0:D], W1f)):
                sp.dma_start(dst, src).then_inc(S["gat_w_loaded"], 16)
            with sp.Fori(1, B) as i:
                load_batch(i)

            def load_hidden(j, slot):
                sp.dma_start(wraw[:, slot, :], ffnW[j]).then_inc(S[f"w_loaded{slot}"], 16)
                sp.dma_start(gsel[:, slot, :], gate_sel[j]).then_inc(S[f"w_loaded{slot}"], 16)

            load_hidden(0, 0)
            load_hidden(1, 1)
            with sp.Fori(1, NF // 2) as m:
                for slot in range(2):
                    sp.wait_ge(S["c_ready"], (2 * m + slot - 1) * NCH)
                    sp.wait_ge(S["wd_split"], 2 * m + slot - 1)
                    load_hidden(2 * m + slot, slot)
            for t in range(NTT):
                sp.wait_ge(S["out_ready"], t + 1)
                sp.dma_start(out[t], y3[:, t, :]).then_inc(S["out_stored"], 16)
            sp.wait_ge(S["out_stored"], 16 * NTT)

        @block.gpsimd
        def _(pool):
            pool.memset(mhalf[:], -0.5).then_inc(S["setup_zero"], 1)
            pool.memset(q3[:].bitcast(f32), 0.0).then_inc(S["setup_zero"], 1)
            pool.memset(k3[:].bitcast(f32), 0.0).then_inc(S["setup_zero"], 1)
            pool.memset(vaug[:, :, :, DH:DH + 1], 1.0).then_inc(S["setup_zero"], 1)
            pool.memset(vaug[:, :, :, DH + 1:VS], 0.0).then_inc(S["setup_zero"], 1)
            pool.memset(combp[:], 0.0).then_inc(S["setup_zero"], 1)
            pool.wait_ge(S["tables_loaded"], 16 * 4)
            pool.tensor_copy(identb[:], identf[:]).then_inc(S["identb_ready"], 1)
            pool.wait_ge(S["setup_zero"], 6)

            def rotate_keys(i):
                for t in range(NT):
                    pool.wait_ge(S["qk_biased"], NT * i + t + 1)
                    sines = rope_sb[:, t, 1, :].unsqueeze(1).broadcast_to([P, 2 * NH, DH])
                    pool.tensor_tensor(t2[:, t, :].rearrange("p (h d) -> p h d", d=DH),
                                       qk[:, t, :].rearrange("p (h d) -> p h d", d=DH),
                                       sines, ALU.mult).then_inc(S["t2_ready"], 1)
                for t in range(NT):
                    pool.wait_ge(S["rot_ready"], NT * i + t + 1)
                    kv = k3[:, t, :].rearrange("p (h s) -> p h s", s=SLOT)
                    src = rot[:, t, NH:2 * NH, :]
                    pool.tensor_tensor(idle_p[:], mhalf[:, 0:1], mhalf[:, 0:1], ALU.mult)
                    pool.tensor_copy(kv[:, :, 0:DH], src).then_inc(S["k3_hi"], 1)
                    pool.tensor_copy(kv[:, :, DH:2 * DH], src)
                    pool.wait_ge(S["k3_hi"], NT * i + t + 1)
                    pool.tensor_tensor(kv[:, :, 2 * DH:3 * DH], src, kv[:, :, 0:DH].bitcast(f32),
                                       ALU.subtract).then_inc(S["k3_ready"], 1)

            def side_inputs(i, first=False):
                pool.wait_ge(S["xres_loaded"], 16 * (i + 1))
                if not first:
                    pool.wait_ge(S["y_used"], i)
                pool.tensor_tensor(xb[:], xres[:], bo_sb[:].unsqueeze(1).broadcast_to([P, NT, D]),
                                   ALU.add).then_inc(S["xb_ready"], 1)
                pool.wait_ge(S["ctx_loaded"], 16 * (i + 1))
                if not first:
                    pool.wait_ge(S["feat_ps"], 2 * i - 1)
                pool.tensor_tensor(idle_p[:], mhalf[:, 0:1], mhalf[:, 0:1], ALU.mult)
                pool.tensor_copy(ctx_hi[:], ctx_sb[:]).then_inc(S["ctx_split"], 1)
                pool.wait_ge(S["ctx_split"], 2 * i + 1)
                pool.tensor_tensor(ctx_lo[:], ctx_sb[:], ctx_hi[:].bitcast(f32),
                                   ALU.subtract).then_inc(S["ctx_split"], 1)

            def inverse_deviation(g, n):
                pool.wait_ge(S["var_ready"], 2 * g + n + 1)
                pool.tensor_tensor(rstd[:], vareps[:], mhalf[:, 0:NT], ALU.pow).then_inc(S["rstd_ready"], 1)

            def store_normed(g):
                pool.wait_ge(S["gh_ready"], 2 * (g + 1))
                pool.tensor_tensor(idle_p[:], mhalf[:, 0:1], mhalf[:, 0:1], ALU.mult)
                pool.tensor_copy(x2[:, bass.ts(g, NT), :], x2b[:]).then_inc(S["x2_stored"], 1)

            rotate_keys(0)
            side_inputs(0, first=True)
            with pool.Fori(0, B - 1) as g:
                inverse_deviation(g, 0)
                rotate_keys(g + 1)
                side_inputs(g + 1)
                inverse_deviation(g, 1)
                store_normed(g)
            inverse_deviation(B - 1, 0)

            def split_part(cols, j, slot, step, done, fresh):
                if not fresh:
                    pool.tensor_tensor(idle_p[:], mhalf[:, 0:1], mhalf[:, 0:1], ALU.mult)
                pool.tensor_copy(whi[:, slot, cols], wraw[:, slot, cols]).then_inc(S["pool_step"], 1)
                pool.wait_ge(S["pool_step"], 2 * j + step)
                pool.tensor_tensor(wlo[:, slot, cols], wraw[:, slot, cols], whi[:, slot, cols].bitcast(f32),
                                   ALU.subtract).then_inc(S[done], 1)

            def split_weights(j, slot, nth, fresh=False):
                pool.wait_ge(S[f"w_loaded{slot}"], 32 * nth)
                if not fresh:
                    pool.wait_ge(S["u_ready"], NCH * (j - 1))
                split_part(slice(0, 4 * P), j, slot, 1, "w_split", fresh)
                if not fresh:
                    pool.wait_ge(S["down_done"], NCH * (j - 1))
                split_part(slice(4 * P, WJ), j, slot, 2, "wd_split", fresh)

            pool.wait_ge(S["st_ready"], NH * B)
            split_weights(0, 0, 1, fresh=True)
            split_weights(1, 1, 1, fresh=True)
            inverse_deviation(B - 1, 1)
            store_normed(B - 1)
            pool.wait_ge(S["x2_stored"], B)
            with pool.Fori(1, NF // 2) as m:
                for slot in range(2):
                    split_weights(2 * m + slot, slot, m + 1)
            for c in range(NCH):
                tiles = slice(4 * c, 4 * c + 4)
                pool.wait_ge(S["var3_ready"], c + 1)
                pool.tensor_tensor(rstd3[:, tiles], ve3[:, tiles], mhalf[:, tiles],
                                   ALU.pow).then_inc(S["rstd3_ready"], 1)

        @block.scalar
        def _(act):
            act.dma_start(wqkv_sb[:], wqkvT).then_inc(S["wqkv_loaded"], 16)
            for dst, src in ((bqkv_sb[:], bqkv.partition_broadcast(P)), (wo_sb[:], woT),
                             (bo_sb[:], bo.partition_broadcast(P))):
                act.dma_start(dst, src).then_inc(S["att_w_loaded"], 16)
            for dst, src in ((w0r_sb[:], W0r), (a0_sb[:], A0), (w0c[:, 0:D], W0f),
                             (b01[:, 0, :], b0), (b01[:, 1, :], b1)):
                act.dma_start(dst, src).then_inc(S["gat_w_loaded"], 16)
            act.dma_start(gw_sb[:], gwT).then_inc(S["router_w_loaded"], 16)
            act.wait_ge(S["consts_loaded"], 16 * 3)
            act.activation(selh[:], stage_h, ACT.Copy).then_inc(S["sel_ready"], 1)
            act.activation(onehot[:], stage_n, ACT.Copy).then_inc(S["sel_ready"], 1)

            def turned_qk(i, n):
                t, half, which = n // 4, n % 2, (n % 4) // 2
                act.wait_ge(S["qkT_ps"], 8 * i + n + 1)
                act.activation((q3T, k3T)[which][:, 4 * half:4 * half + 4, t * P:(t + 1) * P],
                               PS[:, n % 4, :].rearrange("p (a c) -> p a c", c=P), ACT.Copy).then_inc(S["qkT_ready"], 1)

            def numerators(i, h, alone):
                act.wait_ge(S["st_ready"], NH * i + h + 1)
                if h >= PTS:
                    act.wait_ge(S["pv_done"], NH // 2 * i + (h - PTS) // 2 + 1)
                act.activation(pT[:, h % PTS, :], PS[:, (h // 2 % 2 * 4 if alone else 0) + h % 2, 0:CAUSAL], ACT.Exp,
                               scale=DH ** -0.5).then_inc(S["exp_done"], 1)

            def attention_sums(i, b):
                act.wait_ge(S["pv_done"], NH // 2 * i + 4 * b + 4)
                act.activation(sums[:, b, :], PS[:, 2 + b, :], ACT.Copy).then_inc(S["sums_copied"], 1)

            def attention_out(i):
                act.wait_ge(S["oT_ps"], i + 1)
                act.activation(oT[:], PS[:, 2, :].rearrange("p (k t) -> p k t", k=KD), ACT.Copy).then_inc(S["oT_ready"], 1)

            def features(g, layer):
                act.wait_ge(S["st2_ready"], 2 * g + layer + 1)
                act.activation(feat[:], PS[:, 4:6, 0:D].rearrange("p t (h o) -> p t h o", o=GO),
                               ACT.Copy).then_inc(S["feat_ready"], 1)

            def leak(g, layer, a):
                act.wait_ge(S["z_ready"], NU * g + NU // 2 * layer + a + 1)
                if NU * layer + 2 * a >= ALS:
                    act.wait_ge(S["aT_ps"], 2 * NU * g + NU * layer + 2 * a + 2 - ALS)
                for t in range(NT):
                    for r in range(2):
                        ins = act.activation(al[:, (2 * a + t) % ALS, r, :], PS[:, 4 + a % 2, r * T:(r + 1) * T],
                                             ACT.Identity, scale=0.2, bias=nself02[:, t, 2 * a + r:2 * a + r + 1])
                ins.then_inc(S["y_copied"], 1)

            def exps(g, layer, u):
                n = NU * layer + u
                act.wait_ge(S["v_masked"], 2 * NU * g + n + 1)
                for r in range(2):
                    a, c = al[:, n % ALS, r, :], u % 2 * GH + u // 2 * 2 + r
                    ins = act.activation(a, a, ACT.Exp, scale=-1.0, bias=gmin[:, c:c + 1],
                                         accum_out=gsum[:, c // GH, c % GH:c % GH + 1])
                ins.then_inc(S["alpha_ready"], 1)

            def turned_alpha(g, layer, u, alone):
                n = NU * layer + u
                act.wait_ge(S["aT_ps"], 2 * NU * g + n + 1)
                if n >= ATS:
                    act.wait_ge(S["gpv_done"], 2 * NU * g + n - ATS + 1)
                act.activation(aT[:, n % ATS, :, :], PS[:, 6 * (n % 2) if alone else 6, :].rearrange("p (a c) -> p a c", c=P),
                               ACT.Copy).then_inc(S["aT_done"], 1)

            def feature_sums(g, layer):
                act.wait_ge(S["gpv_done"], NU * (2 * g + layer + 1))
                act.activation(gy[:].rearrange("p t d -> p (t d)"), PS[:, 7, :], ACT.Copy).then_inc(S["gsums_copied"], 1)

            def copy_logits(g):
                act.wait_ge(S["logit_ps"], g + 1)
                act.activation(logitsT[:, bass.ts(g, T)], PS[0:NGP, 6, 0:T], ACT.Copy).then_inc(S["logit_copied"], 1)

            def elu_exp(g, layer):
                for t in range(NT):
                    act.wait_ge(S["gneg_ready"], NT * (2 * g + layer) + t + 1)
                    act.activation(gneg[:, t, :], gneg[:, t, :], ACT.Exp).then_inc(S["gexp_ready"], 1)

            def both(g, i):
                gat, att = g is not None, i is not None
                for layer in range(2):
                    if gat and layer == 1:
                        features(g, 1)
                        leak(g, 1, 0)
                        leak(g, 1, 1)
                    ahead = 0 if att and layer == 0 else 1
                    if gat and ahead:
                        exps(g, layer, 0)
                    for s in range(NU):
                        if att and layer == 1:
                            numerators(i, 2 * s, not gat)
                            numerators(i, 2 * s + 1, not gat)
                        if gat and s + ahead < NU:
                            exps(g, layer, s + ahead)
                        if att and layer == 0 and s in (1, 2):
                            for n in range(4 * (s - 1), 4 * s):
                                turned_qk(i, n)
                        if gat:
                            if not (att and layer == 1):
                                turned_alpha(g, layer, s, not att)
                            if s in (1, 3):
                                leak(g, layer, s // 2 + 2)
                        if att and layer == 1:
                            if s == 5:
                                attention_sums(i, 0)
                    if att and layer == 1:
                        attention_sums(i, 1)
                    if gat:
                        feature_sums(g, layer)
                    if att and layer == 1:
                        attention_out(i)
                    if gat:
                        elu_exp(g, layer)
                    if att and layer == 1:
                        features(i, 0)
                        leak(i, 0, 0)
                        leak(i, 0, 1)
                if gat:
                    copy_logits(g)

            both(None, 0)
            with act.Fori(0, B - 1) as g:
                both(g, g + 1)
            both(B - 1, None)

            act.wait_ge(S["gate_centered"], 1)
            act.activation(r_b[:], r_a[:], ACT.Exp).then_inc(S["gate_exp"], 1)
            act.activation(r_t[:], PS[:, 7, 0:NTT * NGP].rearrange("p (t g) -> p t g", g=NGP)[:, :, NE],
                           ACT.Exp, scale=-1.0).then_inc(S["gate_exp"], 1)

            def silu(n, c):
                act.wait_ge(S["g_ready"], n + 1)
                if not isinstance(n, int) or n >= 2:
                    act.wait_ge(S["u_used"], n - 1)
                act.activation(sg[:, c, :], PS[:, 4, :], ACT.Silu).then_inc(S["silu_done"], 1)

            def round_hidden(n, c):
                act.wait_ge(S["c_used"], n + 1)
                if not isinstance(n, int) or n >= 2:
                    act.wait_ge(S["down_done"], n - 1)
                act.activation(hid_hi[:, c, :], hid[:, c, :], ACT.Copy).then_inc(S["hid_rounded"], 1)

            for c in range(NCH):
                silu(c, c)
                round_hidden(c, c)
            with act.Fori(1, NF) as j:
                for c in range(NCH):
                    silu(NCH * j + c, c)
                    round_hidden(NCH * j + c, c)

        @block.tensor
        def _(pe):
            def fold_scores():
                pe.wait_ge(S["gat_w_loaded"], 16 * 8)
                for k in range(KD):
                    pe.matmul(PS[0:CF, 6, 0:2 * GH], w0r_sb[:, k, :], a0_sb[:, k, :], start=(k == 0), stop=(k == KD - 1))
                for f in range(KD):
                    for k in range(KD):
                        mm = pe.matmul(PS[:, 7, f * 2 * GH:(f + 1) * 2 * GH], w1r_sb[:, k, f * P:(f + 1) * P], a1_sb[:, k, :],
                                       start=(k == 0), stop=(k == KD - 1))
                mm.then_inc(S["gat_fold_ps"], 1)

            def project(i, t):
                if t == 0:
                    pe.wait_ge(S["xT_loaded"], 16 * (i + 1))
                for k in range(KD):
                    pe.matmul(PS[:, 2 * t, :], xT_sb[:, k, t * P:(t + 1) * P], wqkv_sb[:, k, 0:2 * D],
                              start=(k == 0), stop=(k == KD - 1))
                for k in range(KD):
                    mm = pe.matmul(PS[:, 2 * t + 1, 0:D], xT_sb[:, k, t * P:(t + 1) * P],
                                   wqkv_sb[:, k, 2 * D:3 * D], start=(k == 0), stop=(k == KD - 1))
                mm.then_inc(S["qkv_ready"], 1)

            def turn_qk(i, t):
                if t == 0:
                    pe.wait_ge(S["v_ready"], NT * (i + 1))
                for which, ready, src in ((0, "q3_ready", q3), (1, "k3_ready", k3)):
                    pe.wait_ge(S[ready], NT * i + t + 1)
                    for half in range(2):
                        n = 4 * t + 2 * which + half
                        if n >= 4:
                            pe.wait_ge(S["qkT_ready"], 8 * i + n - 3)
                        for a in range(4):
                            c0 = (4 * half + a) * P
                            mm = pe.transpose(PS[:, n % 4, a * P:(a + 1) * P], src[:, t, c0:c0 + P].bitcast(f32), identf[:])
                        mm.then_inc(S["qkT_ps"], 1)

            def scores(i, u):
                if u == 0:
                    pe.wait_ge(S["qkT_ready"], 8 * (i + 1))
                if u >= 2:
                    pe.wait_ge(S["smax_done"], 8 * i + u - 1)
                for r in range(2):
                    bank = 2 * (u % 2) + r
                    rows = slice(SLOT * r, SLOT * r + 3 * DH)
                    pe.matmul(PS[:, bank, 0:P], q3T[rows, u, 0:P], k3T[rows, u, 0:P],
                              start=True, stop=False, skip_group_check=True)
                    pe.matmul(PS[:, bank, P:CAUSAL], q3T[rows, u, P:T], k3T[rows, u, :],
                              start=False, stop=False, skip_group_check=True)
                for r in range(2):
                    for c0 in (0, T):
                        mm = pe.matmul(PS[:, 2 * (u % 2) + r, c0:c0 + P], identb[:], maskq[:],
                                       start=False, stop=True, skip_group_check=True)
                mm.then_inc(S["s_ready"], 1)

            def turn_maxima(i):
                pe.wait_ge(S["negm_ready"], i + 1)
                for t in range(NT):
                    mm = pe.transpose(PS[0:2 * NH, 0, t * P:(t + 1) * P], negm2[:, t, :].bitcast(f32), identf[:])
                mm.then_inc(S["negmT_ps"], 1)

            def scoresT(i, a, alone):
                base, deep = (a % 2 * 4, 2) if alone else (0, 1)
                if a == 0:
                    pe.wait_ge(S["negmT_ready"], i + 1)
                if a >= deep:
                    pe.wait_ge(S["exp_done"], NH * i + 2 * (a - deep + 1))
                for r in range(2):
                    pe.matmul(PS[:, base + r, 0:CAUSAL], selh[:, 2 * a + r, :], negmT[:], start=True, stop=False,
                              skip_group_check=True)
                    for c0 in (0, T):
                        pe.matmul(PS[:, base + r, c0:c0 + P], identb[:], maskk[:], start=False, stop=False,
                                  skip_group_check=True)
                for r in range(2):
                    rows = slice(SLOT * r, SLOT * r + 3 * DH)
                    pe.matmul(PS[:, base + r, 0:T], k3T[rows, a, 0:P], q3T[rows, a, :], start=False, stop=False,
                              skip_group_check=True)
                    pe.matmul(PS[:, base + r, T:CAUSAL], k3T[rows, a, P:T], q3T[rows, a, P:T], start=False, stop=True,
                              skip_group_check=True).then_inc(S["st_ready"], 1)

            def weigh_values(i, a):
                pe.wait_ge(S["exp_done"], NH * i + 2 * a + 2)
                for keys in range(NT):
                    for r in range(2):
                        h = 2 * a + r
                        rows, bank, c0 = slice(VS * (h % 4), VS * (h % 4 + 1)), 2 + h // 8, (h // 4) % 2 * T
                        queries = slice(0, T) if keys == 0 else slice(T, CAUSAL)
                        mm = pe.matmul(PS[rows, bank, c0 + keys * P:c0 + T], vaug[:, keys, h, :],
                                       pT[:, h % PTS, queries], start=(keys == 0), stop=(keys == NT - 1),
                                       skip_group_check=True)
                mm.then_inc(S["pv_done"], 1)

            def turn_sums(i):
                pe.wait_ge(S["sums_copied"], 2 * (i + 1))
                pe.wait_ge(S["exp_done"], NH * (i + 1))
                for t in range(NT):
                    for f in range(NH // 4):
                        c0 = (f % 2) * T + t * P
                        mm = pe.transpose(PS[:, t, f * P:(f + 1) * P], sums[:, f // 2, c0:c0 + P], identf[:])
                mm.then_inc(S["sums_ps"], 1)

            def output_projection(i):
                pe.wait_ge(S["on_ready"], i + 1)
                for t in range(NT):
                    for k in range(KD):
                        mm = pe.transpose(PS[:, 2, k * T + t * P:k * T + (t + 1) * P],
                                          o_sb[:, t, k * P:(k + 1) * P], identf[:])
                mm.then_inc(S["oT_ps"], 1)
                pe.wait_ge(S["oT_ready"], i + 1)
                for t in range(NT):
                    for k in range(KD):
                        mm = pe.matmul(PS[:, 3, t * D:(t + 1) * D], oT[:, k, t * P:(t + 1) * P], wo_sb[:, k, :],
                                       start=(k == 0), stop=(k == KD - 1))
                mm.then_inc(S["y_ready"], 1)

            def node_features(g, layer):
                if layer == 0:
                    pe.wait_ge(S["ctx_split"], 2 * (g + 1))
                    terms = [(ctx_hi, w0h, None), (ctx_lo, w0h, None), (ctx_hi, w0l, None)]
                else:
                    pe.wait_ge(S["ghT_ready"], 2 * g + 1)
                    terms = [(a, w, k) for k in range(KD) for a, w in ((ghT_hi, w1h), (ghT_lo, w1h), (ghT_hi, w1l))]
                for t in range(NT):
                    for n, (a, w, k) in enumerate(terms):
                        cols = slice(t * P, (t + 1) * P)
                        mm = pe.matmul(PS[:, 4 + t, 0:WC], a[:, cols] if k is None else a[:, k, cols],
                                       w[:] if k is None else w[:, k, :], start=(n == 0), stop=(n == len(terms) - 1),
                                       skip_group_check=True)
                        if n == 0:
                            for part in (bh, bl):
                                pe.matmul(PS[:, 4 + t, 0:D], onehot[0:1, 0, :], part[:, layer, :],
                                          start=False, stop=False, skip_group_check=True)
                mm.then_inc(S["feat_ps"], 1)

            def turn_node_scores(g, layer):
                pe.wait_ge(S["st2_ready"], 2 * g + layer + 1)
                for t in range(NT):
                    mm = pe.transpose(PS[0:2 * GH, 7, t * P:(t + 1) * P], st2[:, t, :].bitcast(f32), identf[:])
                mm.then_inc(S["stT_ps"], 1)

            def spread_neighbours(g, layer, a):
                if a == 0:
                    pe.wait_ge(S["stT_ready"], 2 * g + layer + 1)
                    pe.wait_ge(S["feat_ready"], 2 * g + layer + 1)
                else:
                    if a >= 2:
                        pe.wait_ge(S["lr_done"], 2 * NU * g + NU * layer + 2 * a - 2)
                for r in range(2):
                    mm = pe.matmul(PS[:, 4 + a % 2, r * T:(r + 1) * T], onehot[:, 2 * a + r, :], stT[:],
                                   start=(r == 0), stop=(r == 1), skip_group_check=True)
                mm.then_inc(S["z_ready"], 1)

            def turn_alpha(g, layer, u, alone):
                n = NU * layer + u
                pe.wait_ge(S["alpha_ready"], 2 * NU * g + n + 1)
                bank, deep = (6 * (n % 2), 2) if alone else (6, 1)
                if n >= deep:
                    pe.wait_ge(S["aT_done"], 2 * NU * g + n - deep + 1)
                for a in range(4):
                    m = a % 2
                    mm = pe.transpose(PS[:, bank, a * P:(a + 1) * P], al[:, n % ALS, a // 2, m * P:(m + 1) * P], identf[:])
                mm.then_inc(S["aT_ps"], 1)

            def weigh_features(g, layer, u):
                t, n = u % 2, NU * layer + u
                pe.wait_ge(S["aT_done"], 2 * NU * g + n + 1)
                for m in range(2):
                    for r in range(2):
                        h = u // 2 * 2 + r
                        rows, c0 = slice(GO * (h % 4), GO * (h % 4 + 1)), (t * 2 + h // 4) * P
                        mm = pe.matmul(PS[rows, 7, c0:c0 + P], feat[:, m, h, :], aT[:, n % ATS, 2 * r + m, :],
                                       start=(m == 0), stop=(m == 1), skip_group_check=True)
                mm.then_inc(S["gpv_done"], 1)

            def turn_features(g, layer):
                pe.wait_ge(S["gsums_copied"], 2 * g + layer + 1)
                for a in range(4):
                    mm = pe.transpose(PS[:, 6, a * P:(a + 1) * P], gy[:, a // 2, (a % 2) * P:(a % 2 + 1) * P], identf[:])
                mm.then_inc(S["gsums_ps"], 1)

            def router_logits(g):
                pe.wait_ge(S["ghT_ready"], 2 * g + 2)
                n = 0
                for k in range(KD):
                    for a, w in ((x2T_hi, gw_hi), (x2T_lo, gw_hi), (x2T_hi, gw_lo)):
                        mm = pe.matmul(PS[0:NGP, 6, 0:T], w[:, k, :], a[:, k, bass.ts(g, T)],
                                       start=(n == 0), stop=(n == 3 * KD - 1))
                        n += 1
                mm.then_inc(S["logit_ps"], 1)

            def turn_layer_out(g, layer):
                pe.wait_ge(S["gh_ready"], 2 * g + layer + 1)
                for t in range(NT):
                    for k in range(KD):
                        mm = pe.transpose(PS[:, 6, k * T + t * P:k * T + (t + 1) * P],
                                          (gh, x2b)[layer][:, t, k * P:(k + 1) * P], identf[:])
                mm.then_inc(S["ghT_ps"], 1)

            def both(g, i, ahead=False):
                gat, att = g is not None, i is not None
                for layer in range(2):
                    if gat and layer == 1:
                        turn_node_scores(g, 1)
                        spread_neighbours(g, 1, 0)
                        spread_neighbours(g, 1, 1)
                    if att and layer == 1:
                        turn_maxima(i)
                        if not gat:
                            fold_scores()
                            pe.wait_ge(S["sel_ready"], 2)
                        scoresT(i, 0, not gat)
                    for s in range(NU + 1):
                        if gat and s < NU:
                            if s in (1, 3):
                                spread_neighbours(g, layer, s // 2 + 2)
                            turn_alpha(g, layer, s, not att)
                        if gat and s and not (att and layer == 0):
                            weigh_features(g, layer, s - 1)
                        if att and layer == 0:
                            if s in (0, 1):
                                turn_qk(i, s)
                            elif s >= 4:
                                scores(i, s - 4)
                            if gat and s:
                                weigh_features(g, layer, s - 1)
                        if att and layer == 1:
                            if s + 1 < NU:
                                scoresT(i, s + 1, not gat)
                            if s < NU:
                                weigh_values(i, s)
                    if att and layer == 0:
                        scores(i, 5)
                    if att and layer == 1:
                        turn_sums(i)
                    if gat:
                        turn_features(g, layer)
                    if att and layer == 0:
                        scores(i, 6)
                    if att and layer == 1:
                        if gat:
                            pe.wait_ge(S["lr_done"], 2 * NU * (g + 1))
                        else:
                            pe.wait_ge(S["gat_w_ready"], 1)
                        node_features(i, 0)
                        output_projection(i)
                        turn_node_scores(i, 0)
                        if ahead:
                            project(i + 1, 0)
                    if gat:
                        turn_layer_out(g, layer)
                    if att and layer == 0:
                        scores(i, 7)
                    if att and layer == 1:
                        spread_neighbours(i, 0, 0)
                        spread_neighbours(i, 0, 1)
                    if ahead and layer == 1:
                        pe.wait_ge(S["y_used"], i + 1)
                        project(i + 1, 1)
                    if gat:
                        if layer == 0:
                            node_features(g, 1)
                        else:
                            router_logits(g)
                            pe.wait_ge(S["logit_copied"], g + 1)

            pe.wait_ge(S["wqkv_loaded"], 16)
            project(0, 0)
            project(0, 1)
            pe.wait_ge(S["tables_loaded"], 16 * 4)
            pe.wait_ge(S["identb_ready"], 1)
            pe.wait_ge(S["att_w_loaded"], 48)
            both(None, 0, ahead=True)
            with pe.Fori(0, B - 2) as g:
                both(g, g + 1, ahead=True)
            both(B - 2, B - 1)
            both(B - 1, None)

            pe.wait_ge(S["logit_copied"], B)
            for t in range(NTT):
                mm = pe.transpose(PS[:, 7, t * NGP:(t + 1) * NGP], logitsT[:, t * P:(t + 1) * P],
                                  identf[0:NGP, 0:NGP])
            mm.then_inc(S["logits_turned"], 1)

            def turn_gates():
                pe.wait_ge(S["comb_ready"], 1)
                for t in range(NTT):
                    mm = pe.transpose(PS[0:3 * NG, 7, t * SLOT:(t + 1) * SLOT].bitcast(bf16),
                                      combp[:, t, 0:3 * NG], identb[:])
                mm.then_inc(S["combT_ps"], 1)

            def gate_up(n, slot, c, fresh=False):
                for which, bank, used, ready in ((0, 4, "silu_done", "g_ready"), (1, 5, "u_used", "u_ready")):
                    if not fresh:
                        pe.wait_ge(S[used], n)
                    s = 0
                    for k in range(KD):
                        w0 = (2 * which + k) * P
                        for w, a in ((whi, x2T_hi), (whi, x2T_lo), (wlo, x2T_hi)):
                            mm = pe.matmul(PS[:, bank, :], w[:, slot, w0:w0 + P],
                                           a[:, k, c * CHUNK:(c + 1) * CHUNK], start=(s == 0), stop=(s == 3 * KD - 1))
                            s += 1
                    mm.then_inc(S[ready], 1)
                if fresh:
                    turn_gates()
                    pe.wait_ge(S["combT_ready"], 1)
                else:
                    pe.wait_ge(S["c_used"], n)
                pe.matmul(PS[:, 6, :], gsel[:, slot, :], combT[:, c * CHUNK:(c + 1) * CHUNK],
                          start=True, stop=True).then_inc(S["c_ready"], 1)

            def down(n, tile, slot, c, first=False, last=False):
                pe.wait_ge(S["hid_ready"], n + 1)
                if c == 0:
                    pe.wait_ge(S["wd_split"], tile + 1)
                for t in range(CHUNK // P):
                    bank, cols = 2 * c + t // 2, slice((t % 2) * D, (t % 2 + 1) * D)
                    for s, (a, w) in enumerate(((hid_hi, whi), (hid_lo, whi), (hid_hi, wlo))):
                        mm = pe.matmul(PS[:, bank, cols], a[:, c, t * P:(t + 1) * P], w[:, slot, 4 * P:WJ],
                                       start=(first and s == 0 and t % 2 == 0), stop=(last and s == 2),
                                       skip_group_check=True)
                mm.then_inc(S["down_done"], 1)

            pe.wait_ge(S["w_split"], 1)
            gate_up(0, 0, 0, fresh=True)
            gate_up(1, 0, 1)
            down(0, 0, 0, 0, first=True)
            pe.wait_ge(S["w_split"], 2)
            gate_up(2, 1, 0)
            down(1, 0, 0, 1, first=True)
            with pe.Fori(0, NF // 2 - 1) as m:
                for o in range(2):
                    j = 2 * m + 1 + o
                    slot, after = (1 + o) % 2, o % 2
                    gate_up(NCH * j + 1, slot, 1)
                    down(NCH * j, j, slot, 0)
                    pe.wait_ge(S["w_split"], j + 2)
                    gate_up(NCH * j + 2, after, 0)
                    down(NCH * j + 1, j, slot, 1)
            n = NCH * (NF - 1)
            gate_up(n + 1, 1, 1)
            down(n, NF - 1, 1, 0, last=True)
            down(n + 1, NF - 1, 1, 1, last=True)

        @block.vector
        def _(dve):
            setup = Steps(dve, S["setup_step"])

            def fold_weights():
                dve.wait_ge(S["gat_fold_ps"], 1)
                setup.mark(dve.tensor_copy(w0c[:, D:WC], PS[0:CF, 6, 0:2 * GH]))
                setup.mark(dve.tensor_copy(w1c[:, :, D:WC], PS[:, 7, 0:KD * 2 * GH].rearrange("p (k c) -> p k c", k=KD)))
                setup.wait()
                setup.mark(dve.tensor_copy(w0h[:], w0c[:]))
                setup.mark(dve.tensor_copy(w1h[:], w1c[:]))
                setup.mark(dve.tensor_copy(bh[:], b01[:]))
                dve.wait_ge(S["router_w_loaded"], 16)
                setup.mark(dve.tensor_copy(gw_hi[:], gw_sb[:]))
                setup.wait()
                dve.tensor_tensor(bl[:], b01[:], bh[:].bitcast(f32), ALU.subtract)
                dve.tensor_tensor(w0l[:], w0c[:], w0h[:].bitcast(f32), ALU.subtract)
                dve.tensor_tensor(gw_lo[:], gw_sb[:], gw_hi[:].bitcast(f32), ALU.subtract)
                dve.tensor_tensor(w1l[:], w1c[:], w1h[:].bitcast(f32), ALU.subtract).then_inc(S["gat_w_ready"], 1)

            dve.wait_ge(S["setup_zero"], 6)
            dve.wait_ge(S["att_w_loaded"], 48)
            dve.wait_ge(S["tables_loaded"], 16 * 4)

            def add_biases(i):
                for t in range(NT):
                    dve.wait_ge(S["qkv_ready"], NT * i + t + 1)
                    dve.tensor_tensor(qk[:, t, :], PS[:, 2 * t, :], bqkv_sb[:, 0:2 * D],
                                      ALU.add).then_inc(S["qk_biased"], 1)
                    dve.tensor_tensor(vaug[:, t, :, 0:DH],
                                      PS[:, 2 * t + 1, 0:D].rearrange("p (h d) -> p h d", d=DH),
                                      bqkv_sb[:, 2 * D:3 * D].rearrange("p (h d) -> p h d", d=DH),
                                      ALU.add).then_inc(S["v_ready"], 1)

            def rotate(i, t, chain):
                dve.wait_ge(S["qk_biased"], NT * i + t + 1)
                cosines = rope_sb[:, t, 0, :].unsqueeze(1).broadcast_to([P, 2 * NH, DH])
                chain.link(dve.tensor_tensor(t1[:, t, :].rearrange("p (h d) -> p h d", d=DH),
                                             qk[:, t, :].rearrange("p (h d) -> p h d", d=DH),
                                             cosines, ALU.mult))
                dve.wait_ge(S["t2_ready"], NT * i + t + 1)
                c = t1[:, t, :].rearrange("p (h f e) -> p h f e", e=2, f=DH // 2)
                s = t2[:, t, :].rearrange("p (h f e) -> p h f e", e=2, f=DH // 2)
                dve.tensor_tensor(rot[:, t, :, 0:DH // 2], c[:, :, :, 0], s[:, :, :, 1], ALU.add)
                dve.tensor_tensor(rot[:, t, :, DH // 2:DH], c[:, :, :, 1], s[:, :, :, 0],
                                  ALU.add).then_inc(S["rot_ready"], 1)
                dve.wait_ge(S["rot_ready"], NT * i + t + 1)
                qv = q3[:, t, :].rearrange("p (h s) -> p h s", s=SLOT)
                src = rot[:, t, 0:NH, :]
                dve.tensor_copy(qv[:, :, 2 * DH:3 * DH], src)
                chain.link(dve.tensor_copy(qv[:, :, 0:DH], src))
                dve.tensor_tensor(qv[:, :, DH:2 * DH], src, qv[:, :, 0:DH].bitcast(f32),
                                  ALU.subtract).then_inc(S["q3_ready"], 1)

            def row_maxima(i, u):
                dve.wait_ge(S["s_ready"], 8 * i + u + 1)
                b = 2 * (u % 2)
                dve.tensor_reduce(negm[:, 0, 2 * u:2 * u + 2], PS[:, b:b + 2, 0:P], AX.X, ALU.max, negate=True)
                dve.tensor_reduce(negm[:, 1, 2 * u:2 * u + 2], PS[:, b:b + 2, P:CAUSAL], AX.X, ALU.max,
                                  negate=True).then_inc(S["smax_done"], 1)

            def split_maxima(i, chain):
                dve.wait_ge(S["smax_done"], 8 * (i + 1))
                chain.link(dve.tensor_copy(negm2[:, :, 0:NH], negm[:]))
                dve.tensor_tensor(negm2[:, :, NH:2 * NH], negm[:], negm2[:, :, 0:NH].bitcast(f32),
                                  ALU.subtract).then_inc(S["negm_ready"], 1)

            def turned_maxima(i):
                dve.wait_ge(S["negmT_ps"], i + 1)
                dve.tensor_copy(negmT[:, 0:T], PS[0:2 * NH, 0, 0:T])
                dve.tensor_copy(negmT[:, T:CAUSAL], PS[0:2 * NH, 0, P:T]).then_inc(S["negmT_ready"], 1)

            def attention_over_sums(i, chain):
                dve.wait_ge(S["sums_ps"], i + 1)
                o_ps = PS[:, 0:2, :].rearrange("p t (h d) -> p t h d", d=VS)
                chain.link(dve.reciprocal(orec[:], o_ps[:, :, :, DH]))
                dve.tensor_tensor(o_sb[:].rearrange("p t (h d) -> p t h d", d=DH), o_ps[:, :, :, 0:DH],
                                  orec[:].unsqueeze(3).broadcast_to([P, NT, NH, DH]), ALU.mult).then_inc(S["on_ready"], 1)

            def first_residual(i):
                dve.wait_ge(S["y_ready"], i + 1)
                dve.wait_ge(S["xb_ready"], i + 1)
                dve.tensor_tensor(resid1[:], PS[:, 3, :].rearrange("p (t d) -> p t d", t=NT), xb[:],
                                  ALU.add).then_inc(S["y_used"], 1)

            def moments(resid, chain):
                for t in range(NT):
                    chain.mark(dve.bn_stats(stats[:, t, :], resid[:, t, :]))
                chain.wait()
                dve.tensor_tensor(idle_v[:], mhalf[:, 0:1], mhalf[:, 0:1], ALU.mult)
                for t in range(NT):
                    chain.mark(dve.bn_aggr(meanvar[:, t, :], stats[:, t, :]))
                chain.wait()
                dve.tensor_scalar(vareps[:], meanvar[:, :, 1], EPS, None, ALU.add).then_inc(S["var_ready"], 1)

            def normed(g, n, resid, target):
                dve.wait_ge(S["rstd_ready"], 2 * g + n + 1)
                for t in range(NT):
                    ins = dve.tensor_scalar(target[:, t, :], resid[:, t, :], meanvar[:, t, 0:1], rstd[:, t:t + 1],
                                            ALU.subtract, ALU.mult)
                return ins

            def split_scores(g, layer, chain):
                dve.wait_ge(S["feat_ps"], 2 * g + layer + 1)
                own, near = PS[:, 4:6, D:D + GH], PS[:, 4:6, D + GH:WC]
                dve.tensor_scalar(nself[:], own, -1.0, None, ALU.mult)
                dve.tensor_scalar(nself02[:], own, -0.2, None, ALU.mult)
                chain.link(dve.tensor_scalar(st2[:, :, 0:GH], near, -1.0, None, ALU.mult))
                dve.scalar_tensor_tensor(st2[:, :, GH:2 * GH], near, -1.0, st2[:, :, 0:GH].bitcast(f32),
                                         ALU.mult, ALU.subtract).then_inc(S["st2_ready"], 1)

            def turned_node_scores(g, layer):
                dve.wait_ge(S["stT_ps"], 2 * g + layer + 1)
                dve.tensor_copy(stT[:], PS[0:2 * GH, 7, 0:T]).then_inc(S["stT_ready"], 1)

            def mask_and_min(g, layer, u):
                t, n = u % 2, NU * layer + u
                a = al[:, n % ALS, :, :]
                dve.wait_ge(S["y_copied"], NU * g + n // 2 + 1)
                for r in range(2):
                    h = u // 2 * 2 + r
                    ins = dve.scalar_tensor_tensor(a[:, r, :], PS[:, 4 + u // 2 % 2, r * T:(r + 1) * T],
                                                   nself[:, t, h:h + 1], a[:, r, :], ALU.add, ALU.min)
                ins.then_inc(S["lr_done"], 1)
                dve.wait_ge(S["lr_done"], 2 * NU * g + n + 1)
                dve.tensor_tensor(idle_v[:], mhalf[:, 0:1], mhalf[:, 0:1], ALU.mult)
                for r in range(2):
                    c = t * GH + u // 2 * 2 + r
                    ins = dve.tensor_tensor_reduce(out=a[:, r, :], in0=a[:, r, :], in1=mk[:, t, :], scale=1.0,
                                                   scalar=3.4e38, op0=ALU.add, op1=ALU.min,
                                                   accum_out=gmin[:, c:c + 1])
                ins.then_inc(S["v_masked"], 1)

            def turned_alpha(g, layer, u):
                n = NU * layer + u
                dve.wait_ge(S["aT_ps"], 2 * NU * g + n + 1)
                if n >= ATS:
                    dve.wait_ge(S["gpv_done"], 2 * NU * g + n - ATS + 1)
                dve.tensor_copy(aT[:, n % ATS, :, :],
                                PS[:, 6, :].rearrange("p (a c) -> p a c", c=P)).then_inc(S["aT_done"], 1)

            def divide_and_elu(g, layer, chain):
                dve.wait_ge(S["alpha_ready"], NU * (2 * g + layer + 1))
                chain.link(dve.reciprocal(grec[:], gsum[:]))
                dve.wait_ge(S["gsums_ps"], 2 * g + layer + 1)
                for t in range(NT):
                    heads = lambda a: a.rearrange("p (h o) -> p h o", o=GO)
                    chain.link(dve.tensor_tensor(heads(gy[:, t, :]), heads(PS[:, 6, t * D:(t + 1) * D]),
                                                 grec[:, t, :].unsqueeze(2).broadcast_to([P, GH, GO]), ALU.mult))
                    dve.tensor_scalar(gneg[:, t, :], gy[:, t, :], 0.0, None, ALU.min).then_inc(S["gneg_ready"], 1)

            def layer_out(g, layer, chain):
                for t in range(NT):
                    dve.wait_ge(S["gexp_ready"], NT * (2 * g + layer) + t + 1)
                    ins = dve.scalar_tensor_tensor(gh[:, t, :], gneg[:, t, :], -1.0, gy[:, t, :], ALU.add, ALU.max)
                if layer == 0:
                    ins.then_inc(S["gh_ready"], 1)
                else:
                    chain.link(ins)
                    chain.link(dve.tensor_tensor(resid2[:], gh[:], x1[:], ALU.add))
                    moments(resid2, chain)

            def turned_layer_out(g, layer, chain):
                dve.wait_ge(S["ghT_ps"], 2 * g + layer + 1)
                src = PS[:, 6, :].rearrange("p (k n) -> p k n", k=KD)
                if layer == 0:
                    hi, lo = ghT_hi[:], ghT_lo[:]
                else:
                    hi, lo = x2T_hi[:, :, bass.ts(g, T)], x2T_lo[:, :, bass.ts(g, T)]
                chain.link(dve.tensor_copy(hi, src))
                dve.tensor_tensor(lo, src, hi.bitcast(f32), ALU.subtract).then_inc(S["ghT_ready"], 1)

            def both(g, i):
                gat, att = g is not None, i is not None
                ac = Steps(dve, S["att_step"], ATT_STEPS * i) if att else None
                gc = Steps(dve, S["gat_step"], GAT_STEPS * g) if gat else None
                if gat:
                    dve.wait_ge(S["y_used"], g + 1)
                    moments(resid1, gc)
                if att:
                    add_biases(i)
                if gat:
                    gc.link(normed(g, 0, resid1, x1))
                    gc.link(dve.tensor_scalar(mk[:], x1[:], 1.0, -MASK_SCALE, ALU.subtract, ALU.mult))
                for layer in range(2):
                    if gat and layer == 1:
                        split_scores(g, 1, gc)
                        turned_node_scores(g, 1)
                    if att and layer == 1:
                        turned_maxima(i)
                        if not gat:
                            fold_weights()
                    for s in range(NU):
                        if gat:
                            mask_and_min(g, layer, s)
                            if att and layer == 1 and s:
                                turned_alpha(g, layer, s - 1)
                        if att and layer == 0:
                            if s in (0, 1):
                                rotate(i, s, ac)
                            elif s >= 5:
                                row_maxima(i, s - 5)
                    if att and layer == 0:
                        row_maxima(i, 3)
                        row_maxima(i, 4)
                    if gat and att and layer == 1:
                        turned_alpha(g, layer, NU - 1)
                    if att and layer == 1:
                        attention_over_sums(i, ac)
                    if gat:
                        divide_and_elu(g, layer, gc)
                    if att and layer == 0:
                        row_maxima(i, 5)
                    if att and layer == 1:
                        split_scores(i, 0, Steps(dve, S["head_step"], i))
                    if gat:
                        layer_out(g, layer, gc)
                    if att and layer == 1:
                        first_residual(i)
                        turned_node_scores(i, 0)
                    if gat and layer == 1:
                        normed(g, 1, resid2, x2b).then_inc(S["gh_ready"], 1)
                    if att and layer == 0:
                        row_maxima(i, 6)
                    if gat:
                        turned_layer_out(g, layer, gc)
                    if att and layer == 0:
                        row_maxima(i, 7)
                        split_maxima(i, ac)
                assert not att or ac.n == ATT_STEPS, ac.n
                assert not gat or gc.n == GAT_STEPS, gc.n

            both(None, 0)
            dve.wait_ge(S["consts_loaded"], 16 * 3)
            with dve.Fori(0, B - 1) as g:
                both(g, g + 1)
            both(B - 1, None)

            r = Steps(dve, S["setup_step"], 0)
            r.n = setup.n
            dve.wait_ge(S["logits_turned"], 1)
            routed = PS[:, 7, 0:NTT * NGP].rearrange("p (t g) -> p t g", g=NGP)[:, :, 0:NE]
            r.link(dve.tensor_reduce(r_s[:], routed, AX.X, ALU.max))
            wide = lambda a: a.unsqueeze(2).broadcast_to([P, NTT, NE])
            dve.tensor_tensor(r_a[:], routed, wide(r_s[:]), ALU.subtract).then_inc(S["gate_centered"], 1)
            dve.wait_ge(S["gate_exp"], 2)
            r.link(dve.tensor_reduce(r_s[:], r_b[:], AX.X, ALU.add))
            r.link(dve.reciprocal(r_s[:], r_s[:]))
            r.link(dve.tensor_tensor(r_a[:], r_b[:], wide(r_s[:]), ALU.mult))
            for t in range(NTT):
                ins = dve.max(top8[:, t, :], r_a[:, t, :])
            r.link(ins)
            fourth = top8[:, :, TOPK - 1]
            r.mark(dve.tensor_tensor(r_b[:], r_a[:], wide(fourth), ALU.is_gt))
            r.mark(dve.tensor_tensor(r_c[:], r_a[:], wide(fourth), ALU.is_equal))
            r.wait()
            r.link(dve.tensor_reduce(r_s[:], r_b[:], AX.X, ALU.add))
            r.link(dve.tensor_scalar(r_s[:], r_s[:], -1.0, float(TOPK), ALU.mult, ALU.add))
            rank = comb[:].rearrange("p t g -> p (t g)")[:, 0:NTT * NE]
            r.link(dve.tensor_tensor_scan(rank, reset_sb[:], r_c[:].rearrange("p t g -> p (t g)"), 0.0,
                                          ALU.mult, ALU.add))
            rank3 = rank.rearrange("p (t g) -> p t g", g=NE)
            r.link(dve.tensor_tensor(rank3, rank3, wide(r_s[:]), ALU.is_le))
            r.link(dve.tensor_tensor(r_c[:], r_c[:], rank3, ALU.mult))
            r.link(dve.tensor_tensor(r_b[:], r_b[:], r_c[:], ALU.add))
            r.link(dve.tensor_tensor(r_b[:], r_b[:], r_a[:], ALU.mult))
            r.link(dve.tensor_reduce(r_s[:], r_b[:], AX.X, ALU.add))
            r.link(dve.reciprocal(r_s[:], r_s[:]))
            r.mark(dve.tensor_tensor(comb[:, :, 0:NE], r_b[:], wide(r_s[:]), ALU.mult))
            r.link(dve.tensor_scalar(r_t[:], r_t[:], 1.0, None, ALU.add))
            r.link(dve.reciprocal(comb[:, :, NE], r_t[:]))
            for part in range(3):
                dst = combp[:, :, part * NG:(part + 1) * NG]
                ins = dve.tensor_copy(dst, comb[:])
                if part < 2:
                    r.link(ins)
                    r.link(dve.tensor_tensor(comb[:], comb[:], dst, ALU.subtract))
            ins.then_inc(S["comb_ready"], 1)
            dve.wait_ge(S["combT_ps"], 1)
            dve.tensor_copy(combT[:], PS[0:3 * NG, 7, :].bitcast(bf16)).then_inc(S["combT_ready"], 1)

            def hidden(n, c, fresh=False):
                dve.wait_ge(S["silu_done"], n + 1)
                dve.wait_ge(S["u_ready"], n + 1)
                dve.tensor_tensor(hu[:, c, :], PS[:, 5, :], sg[:, c, :], ALU.mult).then_inc(S["u_used"], 1)
                dve.wait_ge(S["u_used"], n + 1)
                dve.wait_ge(S["c_ready"], n + 1)
                dve.tensor_tensor(hid[:, c, :], PS[:, 6, :], hu[:, c, :], ALU.mult).then_inc(S["c_used"], 1)
                if not fresh:
                    dve.wait_ge(S["down_done"], n - 1)
                dve.wait_ge(S["hid_rounded"], n + 1)
                dve.tensor_tensor(hid_lo[:, c, :], hid[:, c, :], hid_hi[:, c, :].bitcast(f32),
                                  ALU.subtract).then_inc(S["hid_ready"], 1)

            for c in range(NCH):
                hidden(c, c, fresh=True)
            with dve.Fori(1, NF) as j:
                for c in range(NCH):
                    hidden(NCH * j + c, c)

            dve.wait_ge(S["x2_stored"], B)
            f = r
            for c in range(NCH):
                dve.wait_ge(S["down_done"], NCH * NF - NCH + c + 1)
                for b in range(2 * c, 2 * c + 2):
                    f.mark(dve.tensor_tensor(res3[:, 2 * b:2 * b + 2, :],
                                             PS[:, b, :].rearrange("p (t d) -> p t d", d=D),
                                             x2[:, 2 * b:2 * b + 2, :], ALU.add))
                f.wait()
                tiles = range(4 * c, 4 * c + 4)
                for t in tiles:
                    f.mark(dve.bn_stats(stats3[:, t, :], res3[:, t, :]))
                f.wait()
                for t in tiles:
                    f.mark(dve.bn_aggr(mv3[:, t, :], stats3[:, t, :]))
                f.wait()
                dve.tensor_scalar(ve3[:, 4 * c:4 * c + 4], mv3[:, 4 * c:4 * c + 4, 1], EPS, None,
                                  ALU.add).then_inc(S["var3_ready"], 1)
            for t in range(NTT):
                if t % 4 == 0:
                    dve.wait_ge(S["rstd3_ready"], t // 4 + 1)
                dve.tensor_scalar(y3[:, t, :], res3[:, t, :], mv3[:, t, 0:1], rstd3[:, t:t + 1],
                                  ALU.subtract, ALU.mult).then_inc(S["out_ready"], 1)


def layouts(np, a):
    c = np.ascontiguousarray

    def rows(w):
        return c(w.reshape(-1, P, w.shape[-1]).transpose(1, 0, 2))

    x, con = a["x"], a["ctx_512"]
    out = {
        "xT": c(x.transpose(0, 2, 1).reshape(B, KD, P, T).transpose(0, 2, 1, 3)),
        "x": c(x.reshape(B, NT, P, D).transpose(0, 2, 1, 3)),
        "ctxT": c(con.transpose(0, 2, 1)),
        "wqkvT": rows(a["L0_attn_w_qkv"].T),
        "bqkv": a["L0_attn_b_qkv"],
        "woT": rows(a["L0_attn_w_out"].T),
        "bo": a["L0_attn_b_out"],
    }
    for n in range(2):
        w = a[f"L0_xattn_W{n}"]
        fold = np.zeros((GH, GO, 2 * GH), np.float32)
        for h in range(GH):
            fold[h, :, h] = a[f"L0_xattn_a_self{n}"][h]
            fold[h, :, GH + h] = a[f"L0_xattn_a_neigh{n}"][h]
        flat = w.transpose(1, 0, 2).reshape(w.shape[1], D)
        out[f"W{n}f"] = c(flat) if n == 0 else rows(flat)
        out[f"W{n}r"] = rows(flat.T)
        out[f"A{n}"] = rows(fold.reshape(D, 2 * GH))
        out[f"b{n}"] = c(a[f"L0_xattn_b{n}"].reshape(1, D))
    router = np.zeros((D, NGP), np.float32)
    router[:, 0:NE] = a["L0_ffn_gate_w"].T
    router[:, NE] = a["L0_ffn_shared_expert_gate_w"][0]
    out["gwT"] = rows(router)
    hidden = NF * P
    wide = []
    for kind in ("gate", "up"):
        w = np.zeros((hidden, D), np.float32)
        w[0:NE * FE] = a[f"L0_ffn_expert_{kind}_w"].reshape(NE * FE, D)
        w[NE * FE:NE * FE + FS] = a[f"L0_ffn_shared_{kind}_w"]
        wide.append(w.reshape(NF, P, KD, P).transpose(0, 3, 2, 1).reshape(NF, P, KD * P))
    w = np.zeros((hidden, D), np.float32)
    w[0:NE * FE] = a["L0_ffn_expert_down_w"].transpose(0, 2, 1).reshape(NE * FE, D)
    w[NE * FE:NE * FE + FS] = a["L0_ffn_shared_down_w"].T
    wide.append(w.reshape(NF, P, D))
    out["ffnW"] = c(np.concatenate(wide, axis=2))
    return out


def constants(np, bf16):
    half = DH // 2
    freqs = np.float32(10000.0) ** (-np.arange(half, dtype=np.float32) / np.float32(half))
    theta = np.arange(T, dtype=np.float32)[:, None] * freqs[None, :]
    cos, sin = np.cos(theta), np.sin(theta)
    table = np.zeros((T, 2, half, 2), np.float32)
    table[:, 0, :, 0], table[:, 0, :, 1] = cos, cos
    table[:, 1, :, 0], table[:, 1, :, 1] = sin, -sin
    above = np.where(np.arange(P)[None, :] > np.arange(P)[:, None], NEG, 0.0)
    head = np.zeros((2, NH, NH, P), np.float32)
    node = np.zeros((2, GH, GH, P), np.float32)
    for h in range(NH):
        head[:, h, h] = 1.0
    for h in range(GH):
        node[:, h, h] = 1.0
    expert = np.minimum(np.arange(NF * P) // FE, NE)
    gates = np.zeros((3, NG, NF * P), np.float32)
    gates[:, expert, np.arange(NF * P)] = 1.0
    reset = np.ones((P, NTT, NE), np.float32)
    reset[:, :, 0] = 0.0
    return {
        "rope_cs": np.ascontiguousarray(table.reshape(NT, P, 2, DH).transpose(1, 0, 2, 3)),
        "causal_q": above.astype(bf16),
        "causal_k": np.ascontiguousarray(above.T).astype(bf16),
        "ident": np.eye(P, dtype=np.float32),
        "head_sel": head.reshape(2 * NH, NH, P),
        "node_onehot": node.reshape(2 * GH, GH, P),
        "gate_sel": np.ascontiguousarray(gates.reshape(3 * NG, NF, P).transpose(1, 0, 2)).astype(bf16),
        "scan_reset": reset.reshape(P, NTT * NE),
    }


_ORDER = ["xT", "x", "ctxT", "wqkvT", "bqkv", "woT", "bo", "W0f", "W0r", "A0", "b0", "W1f", "W1r", "A1", "b1",
          "gwT", "ffnW", "rope_cs", "causal_q", "causal_k", "ident", "head_sel", "node_onehot", "gate_sel",
          "scan_reset"]


def kernel(**inputs):
    import numpy as np
    import ml_dtypes
    import concourse.bacc as bacc
    from concourse.bass_utils import run_bass_kernel_spmd

    given = {name: np.asarray(value) for name, value in inputs.items()}
    arrays = {**layouts(np, given), **constants(np, ml_dtypes.bfloat16)}
    nc = bacc.Bacc("TRN2", target_bir_lowering=False, num_devices=1)
    args, sent = [], {}
    for name in _ORDER:
        a = np.ascontiguousarray(arrays[name])
        sent[f"in_{name}"] = a
        args.append(nc.dram_tensor(f"in_{name}", a.shape, mybir.dt.from_np(a.dtype), kind="ExternalInput").ap())
    out = nc.dram_tensor("out_0", (NTT, P, D), mybir.dt.float32, kind="ExternalOutput").ap()
    decoder_layer(nc, *args, out)
    result = run_bass_kernel_spmd(nc, [sent], core_ids=[0])
    return result.results[0]["out_0"].reshape(B, T, D)
```
